# Optimizing a Trainium2 kernel written in Bass

```python
import numpy as np
import jax
import jax.numpy as jnp

def _softmax(x, axis=-1):
    return jax.nn.softmax(x, axis=axis)

def _gelu(x):
    return jax.nn.gelu(x, approximate=True)

def _silu(x):
    return jax.nn.silu(x)

def _sigmoid(x):
    return jax.nn.sigmoid(x)

def _layernorm(x, axis=-1, eps=1e-05):
    m = jnp.mean(x, axis=axis, keepdims=True)
    v = jnp.var(x, axis=axis, keepdims=True)
    return (x - m) / jnp.sqrt(v + eps)

def _scatter_add(tgt, idx, src, axis=0):
    return tgt.at[idx].add(src)

def _segment_sum(src, seg, n):
    return jax.ops.segment_sum(src, seg, n)
kernel_name = 'mk_decoder_preln_d1_seqx_r8_495d3c'

def setup_inputs(seed: int=0):
    np.random.seed(seed)
    _w = jnp.asarray

    def _rec_inputs():
        import jax
        import jax.numpy as jnp
        _rk = jax.random.key(seed)
        x = 0.5 + 0.2887 * jax.random.normal(jax.random.fold_in(_rk, 1), (4, 256, 256), jnp.float32)
        _lenS = 256 - jax.random.randint(jax.random.fold_in(_rk, 7), (4,), 0, max(1, 256 // 4) + 1, jnp.int32)
        _lenS2 = 256 - jax.random.randint(jax.random.fold_in(_rk, 8), (4,), 0, max(1, 256 // 4) + 1, jnp.int32)
        _ctx_512P = jax.random.normal(jax.random.fold_in(_rk, 11), (4, 16, 64), jnp.float32)
        _ctx_512c = jax.random.dirichlet(jax.random.fold_in(_rk, 511), 0.3 * jnp.ones((16,), jnp.float32), (4, 256))
        _ctx_512t = jnp.einsum('bsk,bkd->bsd', _ctx_512c, _ctx_512P)
        _ctx_512t = _ctx_512t * jax.lax.rsqrt(jnp.mean(jnp.square(_ctx_512t)) + 1e-12) * 0.953939
        ctx_512 = -0.000392918 + 0.999932 * (_ctx_512t + 0.3 * jax.random.normal(jax.random.fold_in(_rk, 611), (4, 256, 64), jnp.float32))
        return (x, ctx_512)
    x, ctx_512 = _rec_inputs()

    def _L0_attn_setup():
        import jax, jax.numpy as jnp
        import numpy as np
        B, S, E, H = (2, 256, 256, 16)
        D = E // H
        ROPE_BASE = 10000.0

        def rotate_half(x):
            x1 = x[..., ::2]
            x2 = x[..., 1::2]
            return jnp.stack((-x2, x1), axis=-1).reshape(x.shape[:-1] + (x.shape[-1],))

        def rope_cos_sin(seq_len, head_dim, start_pos=0):
            inv_freq = 1.0 / ROPE_BASE ** (jnp.arange(0, head_dim, 2, dtype=jnp.float32) / head_dim)
            positions = jnp.arange(start_pos, start_pos + seq_len, dtype=jnp.float32)
            freqs = jnp.outer(positions, inv_freq)
            emb = jnp.concatenate([freqs, freqs], axis=-1)
            return (emb[None, None].astype(jnp.float32), emb)
        key = jax.random.key(seed)
        k1, k2, k3 = jax.random.split(key, 3)
        x = jax.random.normal(k1, (B, S, E), dtype=jnp.float32)
        Wqkv = jax.random.normal(k2, (3 * E, E), dtype=jnp.float32) * E ** (-0.5)
        Wout = jax.random.normal(k3, (E, E), dtype=jnp.float32) * E ** (-0.5)
        return {'x': x, 'Wqkv': Wqkv, 'Wout': Wout}
    _L0_attn_all = _L0_attn_setup()
    _L0_attn_in = {k: v for k, v in _L0_attn_all.items() if k in ('Wqkv', 'Wout')}
    del _L0_attn_all

    def _L0_xattn_setup():
        import jax, jax.numpy as jnp
        import numpy as np
        B, N, D = (16, 256, 64)
        H = 4
        TOP_K_RATIO = 0.3
        key = jax.random.key(seed)
        k1, k2, k3, k4 = jax.random.split(key, 4)
        h = jax.random.normal(k1, (B, N, D), dtype=jnp.float32)
        adj_raw = jax.random.uniform(k2, (B, N, N), dtype=jnp.float32)
        lim = 1.0 / np.sqrt(D)
        Wq = jax.random.uniform(k3, (D, D), minval=-lim, maxval=lim, dtype=jnp.float32)
        Wk = jax.random.uniform(k4, (D, D), minval=-lim, maxval=lim, dtype=jnp.float32)
        gamma_raw = jnp.float32(-0.85)
        return {'h': h, 'adj_raw': adj_raw, 'Wq': Wq, 'Wk': Wk, 'gamma_raw': gamma_raw}
    _L0_xattn_all = _L0_xattn_setup()
    _L0_xattn_in = {k: v for k, v in _L0_xattn_all.items() if k in ('Wq', 'Wk', 'gamma_raw')}
    del _L0_xattn_all

    def _L0_ffn_setup():
        import jax, jax.numpy as jnp
        import numpy as np
        E, K, H, F = (64, 6, 256, 96)
        G, KG = (8, 4)
        SHARED_F = 96
        SCALE = 2.5
        T = 2 * 128
        CAP = 2 * (T * K // E)

        def _grouped_topk(logits, bias):
            scores = jax.nn.sigmoid(logits.astype(jnp.float32))
            scores_b = scores + bias[None, :]
            gs = scores_b.reshape(-1, G, E // G)
            group_scores = jnp.sum(jax.lax.top_k(gs, 2)[0], axis=-1)
            gidx = jax.lax.top_k(group_scores, KG)[1]
            rows = jnp.arange(group_scores.shape[0])[:, None]
            group_mask = jnp.zeros_like(group_scores).at[rows, gidx].set(1.0)
            score_mask = jnp.repeat(group_mask, E // G, axis=-1) > 0
            tmp = jnp.where(score_mask, scores_b, -jnp.inf)
            topk_ids = jax.lax.top_k(tmp, K)[1]
            topk_w = jnp.take_along_axis(scores, topk_ids, axis=-1)
            topk_w = topk_w / jnp.sum(topk_w, axis=-1, keepdims=True)
            return (topk_w * SCALE, topk_ids)

        def _routed_moe(x, topk_w, topk_ids, w_gate, w_up, w_down):
            Tn = x.shape[0]
            flat_e = topk_ids.reshape(-1)
            order = jnp.argsort(flat_e)
            se = flat_e[order]
            pos = jnp.arange(Tn * K) - jnp.searchsorted(se, se, side='left')
            tok = order // K
            valid = pos < CAP
            slot = jnp.where(valid, pos, CAP)
            buf = jnp.zeros((E, CAP + 1, H), x.dtype).at[se, slot].set(x[tok])[:, :CAP]
            h = jax.nn.silu(jnp.einsum('ech,ehf->ecf', buf, w_gate)) * jnp.einsum('ech,ehf->ecf', buf, w_up)
            out = jnp.einsum('ecf,efh->ech', h, w_down)
            gathered = out[se, jnp.minimum(pos, CAP - 1)] * valid.astype(x.dtype)[:, None]
            w = topk_w.reshape(-1)[order].astype(x.dtype)[:, None]
            return jax.ops.segment_sum(gathered * w, tok, num_segments=Tn)
        key = jax.random.key(seed)
        ks = jax.random.split(key, 9)
        s = 0.02
        return dict(hidden_states=jax.random.normal(ks[0], (2, 128, H), jnp.float32), gate_w=jax.random.normal(ks[1], (H, E), jnp.float32) * s, bias=jax.random.normal(ks[2], (E,), jnp.float32) * s, w_gate=jax.random.normal(ks[3], (E, H, F), jnp.float32) * s, w_up=jax.random.normal(ks[4], (E, H, F), jnp.float32) * s, w_down=jax.random.normal(ks[5], (E, F, H), jnp.float32) * s, ws_gate=jax.random.normal(ks[6], (H, SHARED_F), jnp.float32) * s, ws_up=jax.random.normal(ks[7], (H, SHARED_F), jnp.float32) * s, ws_down=jax.random.normal(ks[8], (SHARED_F, H), jnp.float32) * s)
    _L0_ffn_all = _L0_ffn_setup()
    _L0_ffn_in = {k: v for k, v in _L0_ffn_all.items() if k in ('gate_w', 'bias', 'w_gate', 'w_up', 'w_down', 'ws_gate', 'ws_up', 'ws_down')}
    del _L0_ffn_all
    return {'x': x, 'ctx_512': ctx_512, 'L0_attn_Wqkv': _L0_attn_in['Wqkv'], 'L0_attn_Wout': _L0_attn_in['Wout'], 'L0_xattn_Wq': _L0_xattn_in['Wq'], 'L0_xattn_Wk': _L0_xattn_in['Wk'], 'L0_xattn_gamma_raw': _L0_xattn_in['gamma_raw'], 'L0_ffn_gate_w': _L0_ffn_in['gate_w'], 'L0_ffn_bias': _L0_ffn_in['bias'], 'L0_ffn_w_gate': _L0_ffn_in['w_gate'], 'L0_ffn_w_up': _L0_ffn_in['w_up'], 'L0_ffn_w_down': _L0_ffn_in['w_down'], 'L0_ffn_ws_gate': _L0_ffn_in['ws_gate'], 'L0_ffn_ws_up': _L0_ffn_in['ws_up'], 'L0_ffn_ws_down': _L0_ffn_in['ws_down']}

def reference(x, ctx_512, L0_attn_Wqkv, L0_attn_Wout, L0_xattn_Wq, L0_xattn_Wk, L0_xattn_gamma_raw, L0_ffn_gate_w, L0_ffn_bias, L0_ffn_w_gate, L0_ffn_w_up, L0_ffn_w_down, L0_ffn_ws_gate, L0_ffn_ws_up, L0_ffn_ws_down):
    import jax
    import jax.numpy as jnp

    def _L0_attn_ref(x, Wqkv, Wout):
        import jax, jax.numpy as jnp
        import numpy as np
        B, S, E, H = (2, 256, 256, 16)
        D = E // H
        ROPE_BASE = 10000.0

        def rotate_half(x):
            x1 = x[..., ::2]
            x2 = x[..., 1::2]
            return jnp.stack((-x2, x1), axis=-1).reshape(x.shape[:-1] + (x.shape[-1],))

        def rope_cos_sin(seq_len, head_dim, start_pos=0):
            inv_freq = 1.0 / ROPE_BASE ** (jnp.arange(0, head_dim, 2, dtype=jnp.float32) / head_dim)
            positions = jnp.arange(start_pos, start_pos + seq_len, dtype=jnp.float32)
            freqs = jnp.outer(positions, inv_freq)
            emb = jnp.concatenate([freqs, freqs], axis=-1)
            return (emb[None, None].astype(jnp.float32), emb)
        batch, seq_len, emb = x.shape
        scale = D ** (-0.5)
        qkv = x @ Wqkv.T
        qkv = qkv.reshape(batch, seq_len, 3, H, D)
        qkv = jnp.transpose(qkv, (2, 0, 3, 1, 4))
        q, k, v = (qkv[0], qkv[1], qkv[2])
        inv_freq = 1.0 / ROPE_BASE ** (jnp.arange(0, D, 2, dtype=jnp.float32) / D)
        positions = jnp.arange(seq_len, dtype=jnp.float32)
        freqs = jnp.outer(positions, inv_freq)
        emb_ang = jnp.concatenate([freqs, freqs], axis=-1)
        cos = jnp.cos(emb_ang)[None, None]
        sin = jnp.sin(emb_ang)[None, None]
        q = q * cos + rotate_half(q) * sin
        k = k * cos + rotate_half(k) * sin
        scores = jnp.einsum('bhqd,bhkd->bhqk', q, k) * scale
        causal = jnp.arange(seq_len)[None, :] > jnp.arange(seq_len)[:, None]
        scores = jnp.where(causal[None, None], -jnp.inf, scores)
        attn = jax.nn.softmax(scores, axis=-1)
        out = jnp.einsum('bhqk,bhkd->bhqd', attn, v)
        out = jnp.transpose(out, (0, 2, 1, 3)).reshape(batch, seq_len, emb)
        return out @ Wout.T

    def _L0_xattn_ref(h, adj_raw, Wq, Wk, gamma_raw):
        import jax, jax.numpy as jnp
        import numpy as np
        B, N, D = (16, 256, 64)
        H = 4
        TOP_K_RATIO = 0.3
        b, n, dm = h.shape
        d = dm // H
        Q = (h @ Wq.T).reshape(b, n, H, d).transpose(0, 2, 1, 3)
        K = (h @ Wk.T).reshape(b, n, H, d).transpose(0, 2, 1, 3)
        sim = jnp.einsum('bhnd,bhmd->bnm', Q, K) / (jnp.sqrt(jnp.float32(d)) * H)
        k = max(1, int(n * TOP_K_RATIO))
        topk_vals = jax.lax.top_k(sim, k)[0]
        threshold = topk_vals[:, :, -1:]
        sparse_mask = (sim >= threshold).astype(sim.dtype)
        A_learned = jax.nn.sigmoid(sim) * sparse_mask
        A_learned = (A_learned + jnp.swapaxes(A_learned, -1, -2)) * 0.5
        gamma = jax.nn.sigmoid(gamma_raw)
        return (1.0 - gamma) * adj_raw + gamma * A_learned

    def _L0_ffn_ref(hidden_states, gate_w, bias, w_gate, w_up, w_down, ws_gate, ws_up, ws_down):
        import jax, jax.numpy as jnp
        import numpy as np
        E, K, H, F = (64, 6, 256, 96)
        G, KG = (8, 4)
        SHARED_F = 96
        SCALE = 2.5
        T = 2 * 128
        CAP = 2 * (T * K // E)

        def _grouped_topk(logits, bias):
            scores = jax.nn.sigmoid(logits.astype(jnp.float32))
            scores_b = scores + bias[None, :]
            gs = scores_b.reshape(-1, G, E // G)
            group_scores = jnp.sum(jax.lax.top_k(gs, 2)[0], axis=-1)
            gidx = jax.lax.top_k(group_scores, KG)[1]
            rows = jnp.arange(group_scores.shape[0])[:, None]
            group_mask = jnp.zeros_like(group_scores).at[rows, gidx].set(1.0)
            score_mask = jnp.repeat(group_mask, E // G, axis=-1) > 0
            tmp = jnp.where(score_mask, scores_b, -jnp.inf)
            topk_ids = jax.lax.top_k(tmp, K)[1]
            topk_w = jnp.take_along_axis(scores, topk_ids, axis=-1)
            topk_w = topk_w / jnp.sum(topk_w, axis=-1, keepdims=True)
            return (topk_w * SCALE, topk_ids)

        def _routed_moe(x, topk_w, topk_ids, w_gate, w_up, w_down):
            Tn = x.shape[0]
            flat_e = topk_ids.reshape(-1)
            order = jnp.argsort(flat_e)
            se = flat_e[order]
            pos = jnp.arange(Tn * K) - jnp.searchsorted(se, se, side='left')
            tok = order // K
            valid = pos < CAP
            slot = jnp.where(valid, pos, CAP)
            buf = jnp.zeros((E, CAP + 1, H), x.dtype).at[se, slot].set(x[tok])[:, :CAP]
            h = jax.nn.silu(jnp.einsum('ech,ehf->ecf', buf, w_gate)) * jnp.einsum('ech,ehf->ecf', buf, w_up)
            out = jnp.einsum('ecf,efh->ech', h, w_down)
            gathered = out[se, jnp.minimum(pos, CAP - 1)] * valid.astype(x.dtype)[:, None]
            w = topk_w.reshape(-1)[order].astype(x.dtype)[:, None]
            return jax.ops.segment_sum(gathered * w, tok, num_segments=Tn)
        orig_shape = hidden_states.shape
        x = hidden_states.reshape(-1, H)
        router_logits = x @ gate_w
        topk_w, topk_ids = _grouped_topk(router_logits, bias)
        y = _routed_moe(x, topk_w, topk_ids, w_gate, w_up, w_down)
        shared = jax.nn.silu(x @ ws_gate) * (x @ ws_up) @ ws_down
        return (y + shared).reshape(orig_shape)
    x = x + _L0_attn_ref(_layernorm(x, axis=-1), L0_attn_Wqkv, L0_attn_Wout)
    x = x + _L0_xattn_ref(ctx_512, _layernorm(x, axis=-1), L0_xattn_Wq, L0_xattn_Wk, L0_xattn_gamma_raw)
    x = x + _L0_ffn_ref(_layernorm(x, axis=-1), L0_ffn_gate_w, L0_ffn_bias, L0_ffn_w_gate, L0_ffn_w_up, L0_ffn_w_down, L0_ffn_ws_gate, L0_ffn_ws_up, L0_ffn_ws_down)
    return x

_drawn_inputs = setup_inputs


def setup_inputs(seed=0):
    import zlib

    import numpy as np

    out = dict(_drawn_inputs(seed))
    spreads = {}
    factors = {'L0_ffn_gate_w': 8.0,
     'L0_ffn_bias': 8.0,
     'L0_ffn_w_gate': 8.0,
     'L0_ffn_w_up': 8.0,
     'L0_ffn_w_down': 8.0,
     'L0_ffn_ws_gate': 7.208,
     'L0_ffn_ws_up': 6.944,
     'L0_ffn_ws_down': 7.021}
    for name, (base, spread) in spreads.items():
        noise = np.random.default_rng([zlib.crc32(name.encode()), seed]).standard_normal(out[name].shape)
        drawn = base * np.exp(spread * noise) if base else spread * noise
        out[name] = jnp.asarray(drawn.astype(out[name].dtype))
    for name, factor in factors.items():
        out[name] = (out[name] * factor).astype(out[name].dtype)
    return out
```

```python
from contextlib import ExitStack

import numpy as np
import concourse.bass as bass
from concourse import mybir

F32 = mybir.dt.float32
BF16 = mybir.dt.bfloat16
I32 = mybir.dt.int32
ALU = mybir.AluOpType
ACT = mybir.ActivationFunctionType
AX = mybir.AxisListType.X

P = 128
B, S, E = 4, 256, 256
T = B * S
NT = T // P
TPB = S // P
H, D = 16, 16
DC = 64
HC = 4
TOPA = max(1, int(S * 0.3))
NE, KE, FF = 64, 6, 96
NG, KG = 8, 4
CAP = 2 * (2 * 128 * KE // NE)
CP = 64
SCALE = 2.5
NP = NE // 2
EPG = 8
PPG = EPG // 2
NSM = NE // EPG
RP = 8
EPS = 1e-5
NEG = -1e30
TERMS_Q = (0, 0, 1, 1, 0, 2)
TERMS_K = (0, 1, 0, 1, 2, 0)
KT = len(TERMS_Q) * D

STAGES = [("A", 0), ("A", 1), ("B", 0), ("C", 0), ("A", 2), ("B", 1), ("D", 0), ("C", 1),
          ("A", 3), ("B", 2), ("D", 1), ("C", 2), ("B", 3), ("D", 2), ("C", 3), ("D", 3)]

USES = {
    "A": {"gen": ["xnT", "v"], "proj": ["qk"]},
    "B": {"unit": [("S", 0, 0), ("S", 0, 1), ("S", 1, 0), ("S", 1, 1), ("S", 1, 2), ("S", 1, 3)]},
    "C": {"gen": ["mT"], "unit": [("T", 1, 0), ("T", 0, 0), ("T", 0, 1), ("T", 1, 1), ("T", 0, 2), ("T", 0, 3)],
          "out": [0, 1]},
    "D": {"gen": ["onT", "att", "aT", "x3T", "lg"], "proj": ["otok"]},
}
AREAS = {"gen": [], "proj": ["QT", "KT"], "unit": [("sim", 0), ("sim", 1)], "out": []}
NORMS = []
for _st, _b in STAGES:
    for _area, _names in USES[_st].items():
        AREAS[_area] += [(_n, _b) for _n in _names]
    NORMS += {"A": [("ln1", _b)], "D": [("ln2", _b), ("ln3", _b)]}.get(_st, [])
AREAS["proj"] += []
AREAS["gen"] += ["pos"]
AREAS["unit"] += [("sg", 0), ("sg", 1), ("sd", 0), ("sd", 1)]


def nth(area, name):
    return AREAS[area].index(name)


def decoder_kernel(nc, x, cosT, sinT, ctxT, wxT, wqkvT, woT, gamma, gate_w, bias, w_gu, w_dn, ws_gu, ws_dn, out):
    qk_dram = nc.dram_tensor("qk_parts", [B, 3, 2 * E, S], BF16, kind="Internal").ap()
    x3_dram = nc.dram_tensor("moe_input", [T, E], F32, kind="Internal").ap()
    z_dram = nc.dram_tensor("expert_rows", [T * 8, E], F32, kind="Internal").ap()

    with ExitStack() as ctx:
        def sb(name, shape, dt=F32):
            return ctx.enter_context(nc.sbuf_tensor(name, shape, dt))

        def pb(name, shape):
            return ctx.enter_context(nc.psum_tensor(name, shape, F32))

        def sem(name):
            return ctx.enter_context(nc.semaphore(name))

        res = sb("res", [P, NT, E])
        x3 = sb("x3", [P, NT, E])
        x3T = sb("x3T", [P, 2, T])
        adj = sb("adj", [P, NT, S])
        ring = sb("ring", [P, RP, 2, 2, 2, FF])
        ring_dn = sb("ring_dn", [P, RP, 2, E])
        identf = sb("identf", [P, P])
        identb = sb("identb", [P, P], BF16)
        tri = sb("tri", [P, P], BF16)
        ones = sb("ones", [P, P], BF16)
        gatew = sb("gatew", [P, 2, NE])
        wsgu = sb("wsgu", [P, 2, 2 * FF])
        wsdn = sb("wsdn", [FF, E])
        biasb = sb("biasb", [P, NE])
        logit = sb("logit", [P, NT, NE])
        iotac = sb("iotac", [P, CAP])
        keep = sb("keep", [P, NT, NE])
        mv = sb("mv", [P, TPB, 2])
        st6 = sb("st6", [P, TPB, 6])
        rstd = sb("rstd", [P, TPB])
        srs = sb("srs", [P, TPB])
        gam = sb("gam", [P, 4])
        zero = sb("zero", [P, E])
        cexp = sb("cexp", [P, 2])

        ARENA = 30900
        arena = sb("arena", [P, ARENA])
        at = {"attention": 0, "moe": 0}

        def cut(phase, *shape, dt=F32):
            n = int(np.prod(shape))
            words = n if dt != BF16 else (n + 1) // 2
            a = arena[:, at[phase]:at[phase] + words]
            at[phase] += words
            pass
            if dt != F32:
                a = a.bitcast(dt)
            names = "abcde"[:len(shape)]
            if len(shape) > 1:
                a = a.rearrange(f"p ({' '.join(names)}) -> p {' '.join(names)}",
                                **{k: v for k, v in zip(names[1:], shape[1:])})
            return a

        AT = "attention"
        wqkv = cut(AT, 2, 3 * E)
        wo = cut(AT, 2, E)
        cosb = cut(AT, S)
        sinb = cut(AT, S)
        masks = cut(AT, P, dt=BF16)
        sel = cut(AT, H, P, dt=BF16)
        xn = cut(AT, 2, TPB, E)
        xnT = cut(AT, 2, 2, S)
        qkc = cut(AT, 4, S)
        qks = cut(AT, 4, S)
        parts = cut(AT, 3, 4, S, dt=BF16)
        qst = cut(AT, 2, H, S, dt=BF16)
        kst = cut(AT, 2, H, S, dt=BF16)
        vaug = cut(AT, 2, TPB, H, 32)
        nmax = cut(AT, TPB, H)
        nmr = cut(AT, TPB, H)
        nmp = cut(AT, TPB, P, dt=BF16)
        nmT = cut(AT, S, dt=BF16)
        prob = cut(AT, 6, 1024)
        oT = cut(AT, 4, S)
        otok = cut(AT, TPB, E)
        onT = cut(AT, 2, S)
        rec = cut(AT, TPB, H)
        mix = cut(AT, TPB, E)
        simS = cut(AT, NT, S)
        work = cut(AT, S)
        best = cut(AT, 8)
        ctxs = prob[:, 0, :]
        wx = prob[:, 1, 0:2 * P].rearrange("p (a b) -> p a b", a=2)
        cq = prob[:, 2, :]
        ck = prob[:, 3, :]

        MO = "moe"
        vals = cut(MO, NT, NE, 8, dt=BF16)
        hotbuf = cut(MO, 2, NT, EPG, CP, dt=BF16)
        score = cut(MO, NT, NE)
        sbias = cut(MO, NT, NE)
        hi1, lo1 = cut(MO, NT * NG, 4), cut(MO, NT * NG, 4)
        hi2, lo2, ta2, tb2 = (cut(MO, NT * NG, 2) for _ in range(4))
        hi3, lo3, ta3, tb3 = (cut(MO, NT * NG, 1) for _ in range(4))
        gsum = cut(MO, NT, 12)
        gtop = cut(MO, NT, 8)
        gpick = cut(MO, NT, 8)
        gout = cut(MO, NT, 12)
        gpen = cut(MO, NT, NG)
        cand = cut(MO, NT, NE + 2)
        etop = cut(MO, NT, 8)
        epick = cut(MO, NT, 8)
        eout = cut(MO, NT, NE + 2)
        selm = cut(MO, NT, NE)
        selb = cut(MO, 2 * NT - 1, NE, dt=BF16)
        wsel = cut(MO, NT, NE)
        wsum = cut(MO, NT)
        rank = cut(MO, NT, NE)
        slot = cut(MO, NT, NE)
        info = cut(MO, 2, PPG, 8)
        tokf = cut(MO, 2, PPG)
        rowf = cut(MO, 2, PPG)
        tmpf = cut(MO, 2, PPG)
        toki = cut(MO, NP, dt=I32)
        rowi = cut(MO, NP, dt=I32)
        wslot = cut(MO, NP)
        hsh = cut(MO, T)
        ssh = cut(MO, T)
        xg = cut(MO, 4, E)
        xgT = cut(MO, 2, 2, P)
        act = cut(MO, 2, FF)
        hid = cut(MO, 2, FF)
        hidT = cut(MO, 2, P)
        yrow = cut(MO, 4, E)
        zin = cut(MO, 2, KE, E)
        fin = cut(MO, 2, E)

        unit = pb("unit", [P, 2, 1024])
        proj = pb("proj", [P, 1024])
        gen = pb("gen", [P, 512])
        outp = pb("outp", [P, 512])
        genb = gen[:, :].bitcast(BF16)

        x_in = [sem(f"x_in{b}") for b in range(B)]
        ctx_in, rope_in, wqkv_in, wo_in, moe_in = (sem(n) for n in ("ctx_in", "rope_in", "wqkv_in", "wo_in", "moe_in"))
        parts_out = [sem(f"parts_out{b}") for b in range(B)]
        stack_in = [sem(f"stack_in{b}") for b in range(B)]
        x3_out = sem("x3_out")
        z_zeroed = sem("z_zeroed")
        ring_in = [sem(f"ring_in{i}") for i in range(RP)]
        gathered = [sem(f"gathered{i}") for i in range(4)]
        scattered = [sem(f"scattered{i}") for i in range(4)]
        z_in = [sem(f"z_in{i}") for i in range(2)]
        out_done = [sem(f"out_done{i}") for i in range(2)]
        dve_step, act_step, pool_step = sem("dve_step"), sem("act_step"), sem("pool_step")
        full = {a: sem(f"{a}_full") for a in AREAS}
        free = {"gen": sem("gen_free"), "proj": sem("proj_free"), "out": sem("out_free"),
                "unit": [sem("unit_free0"), sem("unit_free1")]}
        const_ready, const_act = sem("const_ready"), sem("const_act")
        zero_ready = sem("zero_ready")
        gamma_sig, gamma_ready = sem("gamma_sig"), sem("gamma_ready")
        var_ready, rstd_ready = sem("var_ready"), sem("rstd_ready")
        xn_ready, sin_done, roped, part0, rest_ready, part1, part2 = (
            sem(n) for n in ("xn_ready", "sin_done", "roped", "part0", "rest_ready", "part1", "part2"))
        shift_ready, prob_ready, adj_sig, adj_half, adj_row = (
            sem(n) for n in ("shift_ready", "prob_ready", "adj_sig", "adj_half", "adj_row"))
        x3_ready = sem("x3_ready")
        score_ready, sel_ready, vals_ready = sem("score_ready"), sem("sel_ready"), sem("vals_ready")
        sh_act, sh_hid = sem("sh_act"), sem("sh_hid")
        hot_ready, info_full, info_free, index_ready = (
            sem(n) for n in ("hot_ready", "info_full", "info_free", "index_ready"))
        xt_full, xt_free, gu_full, act_ready, hid_ready, ht_full, ht_free, y_full, y_free = (
            sem(n) for n in ("xt_full", "xt_free", "gu_full", "act_ready", "hid_ready", "ht_full", "ht_free",
                             "y_full", "y_free"))
        fin_ready = sem("fin_ready")

        def filled(eng, area, name):
            eng.wait_ge(full[area], nth(area, name) + 1)

        def emptied(eng, area, name):
            n = nth(area, name)
            if area == "unit":
                eng.wait_ge(free["unit"][n % 2], n // 2 + 1)
            else:
                eng.wait_ge(free[area], n + 1)

        def unit_free(name):
            return free["unit"][nth("unit", name) % 2]

        def unit_at(name):
            return unit[:, nth("unit", name) % 2, :]

        def probs_at(key):
            return prob[:, USES["C"]["unit"].index(key), :]

        block = ctx.enter_context(nc.Block())

        @block.sync
        def _(sp):
            xv = x.rearrange("(t p) e -> p t e", p=P)
            sp.dma_start(ctxs[0:DC, :], ctxT).then_inc(ctx_in, 16)
            sp.dma_start(wx[0:DC, :, 0:DC], wxT.rearrange("a k n -> k a n")).then_inc(ctx_in, 16)
            sp.dma_start(res[:, 0:TPB, :], xv[:, 0:TPB, :]).then_inc(x_in[0], 16)
            sp.dma_start(wqkv, wqkvT.rearrange("(c p) n -> p c n", p=P)).then_inc(wqkv_in, 16)
            sp.dma_start(cosb, cosT).then_inc(rope_in, 16)
            sp.dma_start(sinb, sinT).then_inc(rope_in, 16)
            sp.dma_start(gam[:, 0:1], gamma.to_broadcast((P, 1))).then_inc(ctx_in, 16)
            for b in range(1, B):
                sp.dma_start(res[:, TPB * b:TPB * b + TPB, :], xv[:, TPB * b:TPB * b + TPB, :]).then_inc(x_in[b], 16)
            sp.dma_start(wo, woT.rearrange("(c p) n -> p c n", p=P)).then_inc(wo_in, 16)
            sp.dma_start(gatew[:, :, :], gate_w.rearrange("(c p) n -> p c n", p=P)).then_inc(moe_in, 16)
            sp.dma_start(wsgu[:, :, :], ws_gu.rearrange("(c p) n -> p c n", p=P)).then_inc(moe_in, 16)
            sp.dma_start(wsdn[:, :], ws_dn).then_inc(moe_in, 16)
            sp.dma_start(biasb[:, :], bias.to_broadcast((P, NE))).then_inc(moe_in, 16)

            def ring_fill(p):
                sp.dma_start(ring[:, p % RP].rearrange("p e c g f -> p (e c g f)"), w_gu[p]).then_inc(ring_in[p % RP], 16)
                sp.dma_start(ring_dn[0:FF, p % RP].rearrange("p e n -> p (e n)"), w_dn[p]).then_inc(ring_in[p % RP], 16)

            later = {("A", 1): range(0, 2), ("A", 2): range(2, 4), ("A", 3): range(4, 6), ("D", 1): range(6, RP)}
            for stage, b in STAGES:
                if stage == "A":
                    for j, ready in enumerate((part0, part1, part2)):
                        sp.wait_ge(ready, b + 1)
                        sp.dma_start(qk_dram[b, j].rearrange("(c p) s -> p c s", p=P), parts[:, j]).then_inc(parts_out[b], 16)
                    sp.wait_ge(parts_out[b], 48)
                    if b >= 2:
                        filled(sp, "unit", (("T", 0, 3), b - 2))
                    for n in range(len(TERMS_Q)):
                        for dst, terms, off in ((qst, TERMS_Q, 0), (kst, TERMS_K, E)):
                            src = qk_dram[b, terms[n], off:off + E, :].rearrange("(h d) s -> d h s", d=D)
                            sp.dma_start(dst[n * D:(n + 1) * D, b % 2], src).then_inc(stack_in[b], 16)
                    if b == 0:
                        sp.wait_ge(zero_ready, 1)
                        zv = z_dram.rearrange("(t p k) n -> t p k n", p=P, k=8)
                        for t in range(NT):
                            sp.dma_start(zv[t, :, 0:KE, :], zero[:, :].unsqueeze(1).broadcast_to((P, KE, E))).then_inc(z_zeroed, 16)
                if stage == "D":
                    sp.wait_ge(x3_ready, b + 1)
                    sp.dma_start(x3_dram.rearrange("(t p) e -> p t e", p=P)[:, TPB * b:TPB * b + TPB, :],
                                 x3[:, TPB * b:TPB * b + TPB, :]).then_inc(x3_out, 16)
                for p in later.get((stage, b), ()):
                    ring_fill(p)
            for p in range(RP, NP):
                sp.wait_ge(y_full, p - RP + 1)
                ring_fill(p)
            for s in range(4):
                sp.wait_ge(scattered[s], 16 * (NP // 4))
            zv = z_dram.rearrange("(t p k) n -> t p k n", p=P, k=8)
            ov = out.rearrange("(t p) e -> t p e", p=P)
            for t in range(NT + 1):
                if t < NT:
                    if t >= 2:
                        sp.wait_ge(fin_ready, t - 1)
                    sp.dma_start(zin[:, t % 2], zv[t, :, 0:KE, :]).then_inc(z_in[t % 2], 16)
                if t >= 1:
                    sp.wait_ge(fin_ready, t)
                    sp.dma_start(ov[t - 1], fin[:, (t - 1) % 2]).then_inc(out_done[(t - 1) % 2], 16)
            for s in range(2):
                sp.wait_ge(out_done[s], 16 * (NT // 2))

        @block.tensor
        def _(pe):
            mm = nc.tensor.matmul

            def claim(area, name):
                n = nth(area, name)
                if area == "unit":
                    if n >= 2:
                        pe.wait_ge(free["unit"][n % 2], n // 2)
                elif n >= 1:
                    pe.wait_ge(free[area], n)

            def projections_ctx():
                pe.wait_ge(const_ready, 1)
                pe.wait_ge(ctx_in, 48)
                for m, name in enumerate(("QT", "KT")):
                    claim("proj", name)
                    for n in range(2):
                        last = mm(proj[:, n * 512:(n + 1) * 512], wx[:, m, :], ctxs[:, n * 512:(n + 1) * 512], start=True, stop=True)
                    last.then_inc(full["proj"], 1)
                emptied(pe, "proj", "KT")
                for u in range(2):
                    for j in range(4):
                        t = 4 * u + j
                        b = t // TPB
                        last = mm(unit[:, u, j * S:(j + 1) * S], cq[:, t * P:(t + 1) * P], ck[:, b * S:(b + 1) * S], start=True, stop=True)
                    last.then_inc(full["unit"], 1)

            def stage_a(b):
                claim("gen", ("xnT", b))
                pe.wait_ge(xn_ready, b + 1)
                for c in range(2):
                    for t in range(TPB):
                        last = nc.tensor.transpose(gen[:, (2 * c + t) * P:(2 * c + t + 1) * P], xn[:, b % 2, t, c * P:(c + 1) * P], identf[:, :])
                last.then_inc(full["gen"], 1)
                emptied(pe, "gen", ("xnT", b))
                pe.wait_ge(wqkv_in, 16)
                claim("proj", ("qk", b))
                for m in range(4):
                    for c in range(2):
                        last = mm(proj[:, m * S:(m + 1) * S], wqkv[:, c, m * P:(m + 1) * P], xnT[:, b % 2, c, :], start=(c == 0), stop=(c == 1))
                last.then_inc(full["proj"], 1)
                for t in range(TPB):
                    for c in range(2):
                        last = mm(gen[:, t * E:(t + 1) * E], xnT[:, b % 2, c, t * P:(t + 1) * P], wqkv[:, c, 2 * E:3 * E], start=(c == 0), stop=(c == 1))
                last.then_inc(full["gen"], 1)

            def stage_b(b):
                pe.wait_ge(stack_in[b], 16 * 2 * len(TERMS_Q))
                for key in USES["B"]["unit"]:
                    _, t, u = key
                    claim("unit", (key, b))
                    n = P * (t + 1)
                    for j in range(1024 // n):
                        h = 1024 // n * u + j
                        area = unit_at((key, b))[:, j * n:(j + 1) * n]
                        mm(area, qst[0:KT, b % 2, h, t * P:(t + 1) * P], kst[0:KT, b % 2, h, 0:n], start=True, stop=False)
                        last = mm(area[:, n - P:n], identb[:, :], masks, start=False, stop=True)
                    last.then_inc(full["unit"], 1)

            def pv(b, hg):
                key0, key1 = ("T", 0, hg), ("T", 1, hg // 2)
                order = USES["C"]["unit"]
                pe.wait_ge(prob_ready, 6 * b + max(order.index(key0), order.index(key1)) + 1)
                if hg % 2 == 0:
                    claim("out", (hg // 2, b))
                c0 = (hg % 2) * S
                for j in range(4):
                    mm(outp[32 * j:32 * j + 32, c0:c0 + S], vaug[:, b % 2, 0, 4 * hg + j, :],
                       probs_at(key0)[:, j * S:(j + 1) * S], start=True, stop=False, tile_position=(0, 32 * j))
                for j in range(4):
                    k = (4 * hg + j) % 8
                    last = mm(outp[32 * j:32 * j + 32, c0 + P:c0 + S], vaug[:, b % 2, 1, 4 * hg + j, :],
                              probs_at(key1)[:, k * P:(k + 1) * P], start=False, stop=True, tile_position=(0, 32 * j))
                if hg % 2 == 1:
                    last.then_inc(full["out"], 1)

            def stage_c(b):
                claim("gen", ("mT", b))
                pe.wait_ge(shift_ready, b + 1)
                for t in range(TPB):
                    last = nc.tensor.transpose(genb[:, t * P:(t + 1) * P], nmp[:, t, :], identb[:, :])
                last.then_inc(full["gen"], 1)
                emptied(pe, "gen", ("mT", b))
                for n, key in enumerate(USES["C"]["unit"]):
                    _, kt, u = key
                    claim("unit", (key, b))
                    w = S - kt * P
                    for j in range(1024 // w):
                        h = 1024 // w * u + j
                        area = unit_at((key, b))[:, j * w:(j + 1) * w]
                        mm(area, kst[0:KT, b % 2, h, kt * P:(kt + 1) * P], qst[0:KT, b % 2, h, kt * P:S], start=True, stop=False)
                        last = mm(area, sel[:, h, :], nmT[:, kt * P:S], start=False, stop=True)
                    last.then_inc(full["unit"], 1)
                    if n == 3:
                        pv(b, 0)
                    if n == 4:
                        pv(b, 1)
                pv(b, 2)
                pv(b, 3)

            def stage_d(b):
                claim("proj", ("otok", b))
                emptied(pe, "out", (1, b))
                for t in range(TPB):
                    for hg in range(4):
                        last = nc.tensor.transpose(proj[:, (4 * t + hg) * P:(4 * t + hg + 1) * P], oT[:, hg, t * P:(t + 1) * P], identf[:, :])
                last.then_inc(full["proj"], 1)
                claim("gen", ("onT", b))
                emptied(pe, "proj", ("otok", b))
                for c in range(2):
                    for t in range(TPB):
                        last = nc.tensor.transpose(gen[:, (2 * c + t) * P:(2 * c + t + 1) * P], otok[:, t, c * P:(c + 1) * P], identf[:, :])
                last.then_inc(full["gen"], 1)
                emptied(pe, "gen", ("onT", b))
                pe.wait_ge(wo_in, 16)
                for t in range(TPB):
                    for c in range(2):
                        last = mm(gen[:, t * E:(t + 1) * E], onT[:, c, t * P:(t + 1) * P], wo[:, c, :], start=(c == 0), stop=(c == 1))
                last.then_inc(full["gen"], 1)
                claim("gen", ("aT", b))
                pe.wait_ge(adj_row, b + 1)
                for i in range(TPB):
                    for j in range(TPB):
                        last = nc.tensor.transpose(gen[:, i * S + j * P:i * S + (j + 1) * P], adj[:, TPB * b + j, i * P:(i + 1) * P], identf[:, :])
                last.then_inc(full["gen"], 1)
                claim("gen", ("x3T", b))
                pe.wait_ge(x3_ready, b + 1)
                for c in range(2):
                    for t in range(TPB):
                        last = nc.tensor.transpose(gen[:, (2 * c + t) * P:(2 * c + t + 1) * P], x3[:, TPB * b + t, c * P:(c + 1) * P], identf[:, :])
                last.then_inc(full["gen"], 1)
                emptied(pe, "gen", ("x3T", b))
                pe.wait_ge(moe_in, 64)
                for t in range(TPB):
                    for c in range(2):
                        g = TPB * b + t
                        last = mm(gen[:, t * NE:(t + 1) * NE], x3T[:, c, g * P:(g + 1) * P], gatew[:, c, :], start=(c == 0), stop=(c == 1))
                last.then_inc(full["gen"], 1)

            def shared_in():
                for n in range(2):
                    claim("unit", ("sg", n))
                    for g in range(2):
                        for c in range(2):
                            last = mm(unit_at(("sg", n))[0:FF, g * 512:(g + 1) * 512], wsgu[:, c, g * FF:(g + 1) * FF], x3T[:, c, n * 512:(n + 1) * 512], start=(c == 0), stop=(c == 1))
                    last.then_inc(full["unit"], 1)

            def shared_out():
                for n in range(2):
                    claim("unit", ("sd", n))
                    pe.wait_ge(sh_hid, n + 1)
                    for j in range(4):
                        t = 4 * n + j
                        last = mm(unit_at(("sd", n))[:, j * E:(j + 1) * E], hsh[0:FF, t * P:(t + 1) * P], wsdn[:, :], start=True, stop=True)
                    last.then_inc(full["unit"], 1)

            def positions():
                claim("gen", "pos")
                pe.wait_ge(sel_ready, 1)
                sf = selb.rearrange("p t e -> p (t e)")
                mm(gen[:, :], tri[:, :], sf[:, (NT - 1) * NE:], start=True, stop=False)
                for j in range(1, NT):
                    last = mm(gen[:, :], ones[:, :], sf[:, (NT - 1 - j) * NE:(2 * NT - 1 - j) * NE], start=False, stop=(j == NT - 1))
                last.then_inc(full["gen"], 1)

            def slot_map(g):
                pe.wait_ge(hot_ready, g + 1)
                if g == 0:
                    pe.wait_ge(vals_ready, 1)
                    emptied(pe, "gen", "pos")
                else:
                    pe.wait_ge(info_free, g)
                for q in range(PPG):
                    e = EPG * g + 2 * q
                    for t in range(NT):
                        last = mm(gen[:, q * 16:(q + 1) * 16], hotbuf[:, g % 2, t, 2 * q:2 * q + 2, :].rearrange("p a b -> p (a b)"),
                                  vals[:, t, e:e + 2, :].rearrange("p a b -> p (a b)"), start=(t == 0), stop=(t == NT - 1))
                last.then_inc(info_full, 1)

            def tokens_in(p):
                pe.wait_ge(gathered[p % 4], 16 * (p // 4 + 1))
                if p >= 2:
                    pe.wait_ge(xt_free, p - 1)
                for c in range(2):
                    last = nc.tensor.transpose(unit[:, 0, (p % 2) * 512 + c * P:(p % 2) * 512 + (c + 1) * P], xg[:, p % 4, c * P:(c + 1) * P], identf[:, :])
                last.then_inc(xt_full, 1)

            def gate_up(p):
                pe.wait_ge(xt_free, p + 1)
                pe.wait_ge(ring_in[p % RP], 32 * (p // RP + 1))
                if p >= 2:
                    pe.wait_ge(hid_ready, p - 1)
                for c in range(2):
                    for e in range(2):
                        last = mm(unit[CP * e:CP * e + CP, 1, (p % 2) * 512:(p % 2) * 512 + 2 * FF], xgT[:, p % 2, c, CP * e:CP * (e + 1)],
                                  ring[:, p % RP, e, c].rearrange("p g f -> p (g f)"), start=(c == 0), stop=(c == 1), tile_position=(0, CP * e))
                last.then_inc(gu_full, 1)

            def hidden(p):
                pe.wait_ge(hid_ready, p + 1)
                if p >= 1:
                    pe.wait_ge(ht_free, p)
                nc.tensor.transpose(outp[0:FF, 0:P], hid[:, p % 2, :], identf[:, :]).then_inc(ht_full, 1)

            def down(p):
                pe.wait_ge(ht_free, p + 1)
                if p >= 2:
                    pe.wait_ge(y_free, p - 1)
                for e in range(2):
                    last = mm(proj[CP * e:CP * e + CP, (p % 2) * 512:(p % 2) * 512 + E], hidT[:, p % 2, CP * e:CP * (e + 1)],
                              ring_dn[:, p % RP, e, :], start=True, stop=True, tile_position=(0, CP * e))
                last.then_inc(y_full, 1)

            projections_ctx()
            for stage, b in STAGES:
                {"A": stage_a, "B": stage_b, "C": stage_c, "D": stage_d}[stage](b)
            shared_in()
            positions()
            shared_out()
            slot_map(0)
            slot_map(1)
            emptied(pe, "unit", ("sd", 0))
            emptied(pe, "unit", ("sd", 1))
            for p in range(NP + 3):
                if p < NP:
                    tokens_in(p)
                if 0 <= p - 1 < NP:
                    gate_up(p - 1)
                if 0 <= p - 3 < NP:
                    down(p - 3)
                if 0 <= p - 2 < NP:
                    hidden(p - 2)
                if p % PPG == 0 and p // PPG + 2 < NSM:
                    slot_map(p // PPG + 2)

        @block.scalar
        def _(sc):
            steps = [0]
            act_fn = nc.scalar.activation

            def link(ins):
                steps[0] += 1
                ins.then_inc(act_step, 1)
                sc.wait_ge(act_step, steps[0])

            def context():
                sc.wait_ge(ctx_in, 48)
                act_fn(gam[:, 1:2], gam[:, 0:1], ACT.Sigmoid).then_inc(gamma_sig, 1)
                for name, dst in (("QT", cq), ("KT", ck)):
                    filled(sc, "proj", name)
                    nc.scalar.copy(dst, proj[:, :]).then_inc(free["proj"], 1)
                for u in range(2):
                    filled(sc, "unit", ("sim", u))
                    act_fn(adj[:, 4 * u:4 * u + 4, :].rearrange("p t s -> p (t s)"), unit[:, u, :], ACT.Sigmoid,
                           scale=1.0 / (HC * (DC // HC) ** 0.5)).then_inc(adj_sig, 1)
                    nc.scalar.copy(simS[:, 4 * u:4 * u + 4, :].rearrange("p t s -> p (t s)"), unit[:, u, :]).then_inc(free["unit"][u], 1)

            def stage_a(b):
                filled(sc, "gen", ("xnT", b))
                nc.scalar.copy(xnT[:, b % 2].rearrange("p c s -> p (c s)"), gen[:, :]).then_inc(free["gen"], 1)
                filled(sc, "gen", ("v", b))
                if b == 0:
                    sc.wait_ge(const_ready, 1)
                if b >= 2:
                    filled(sc, "out", (1, b - 2))
                nc.scalar.copy(vaug[:, b % 2, :, :, 0:D], gen[:, :].rearrange("p (t h d) -> p t h d", t=TPB, h=H)).then_inc(free["gen"], 1)
                sc.wait_ge(roped, b + 1)
                if b >= 1:
                    sc.wait_ge(parts_out[b - 1], 48)
                nc.scalar.copy(parts[:, 0], qkc).then_inc(part0, 1)
                sc.wait_ge(rest_ready, b + 1)
                nc.scalar.copy(parts[:, 1], qkc).then_inc(part1, 1)

            def stage_c(b):
                for n, key in enumerate(USES["C"]["unit"]):
                    filled(sc, "unit", (key, b))
                    if b == 0 and n == 0:
                        filled(sc, "unit", ("sim", 1))
                    if b >= 1 and n == 0:
                        filled(sc, "out", (1, b - 1))
                    act_fn(prob[:, n, :], unit_at((key, b)), ACT.Exp, scale=D ** -0.5).then_inc(unit_free((key, b)), 1)

            def stage_d(b):
                filled(sc, "gen", ("onT", b))
                nc.scalar.copy(onT.rearrange("p c s -> p (c s)"), gen[:, :]).then_inc(free["gen"], 1)
                filled(sc, "gen", ("x3T", b))
                nc.scalar.copy(x3T[:, :, b * S:(b + 1) * S], gen[:, :].rearrange("p (c s) -> p c s", c=2)).then_inc(free["gen"], 1)
                filled(sc, "gen", ("lg", b))
                nc.scalar.copy(logit[:, TPB * b:TPB * b + TPB, :], gen[:, 0:TPB * NE].rearrange("p (t e) -> p t e", t=TPB)).then_inc(free["gen"], 1)

            context()
            for stage, b in STAGES:
                if stage != "B":
                    {"A": stage_a, "C": stage_c, "D": stage_d}[stage](b)
            emptied(sc, "gen", ("lg", B - 1))
            act_fn(score, logit[:, :, :], ACT.Sigmoid).then_inc(score_ready, 1)
            for n in range(2):
                filled(sc, "unit", ("sg", n))
                act_fn(ssh[0:FF, n * 512:(n + 1) * 512], unit_at(("sg", n))[0:FF, 0:512], ACT.Silu).then_inc(sh_act, 1)
            for p in range(NP + 3):
                if 0 <= p - 1 < NP:
                    q = p - 1
                    sc.wait_ge(gu_full, q + 1)
                    if q >= 2:
                        sc.wait_ge(hid_ready, q - 1)
                    act_fn(act[:, q % 2, :], unit[:, 1, (q % 2) * 512:(q % 2) * 512 + FF], ACT.Silu).then_inc(act_ready, 1)
                if 0 <= p - 3 < NP:
                    q = p - 3
                    sc.wait_ge(y_full, q + 1)
                    if q >= 4:
                        sc.wait_ge(scattered[q % 4], 16 * (q // 4))
                    act_fn(yrow[:, q % 4, :], proj[:, (q % 2) * 512:(q % 2) * 512 + E], ACT.Copy, scale=wslot[:, q:q + 1]).then_inc(y_free, 1)

        @block.gpsimd
        def _(gp):
            steps = [0]

            def link(ins):
                steps[0] += 1
                ins.then_inc(pool_step, 1)
                gp.wait_ge(pool_step, steps[0])

            pool = nc.gpsimd
            pool.memset(zero[:, :], 0.0).then_inc(zero_ready, 1)
            link(pool.memset(identf[:, :], 0.0))
            link(pool.affine_select(out=identf[:, :], in_=identf[:, :], compare_op=ALU.not_equal, fill=1.0,
                                    base=0, pattern=[[-1, P]], channel_multiplier=1))
            link(pool.tensor_copy(identb[:, :], identf[:, :]))
            link(pool.memset(ctxs[DC:P, :], 0.0))
            link(pool.memset(wx[DC:P, :, :], 0.0))
            link(pool.memset(wx[0:DC, :, DC:P], 0.0))
            link(pool.memset(masks, 0.0))
            link(pool.affine_select(out=masks, in_=masks, compare_op=ALU.is_ge, fill=NEG, base=0,
                                    pattern=[[-1, P]], channel_multiplier=1))
            link(pool.memset(vaug, 0.0))
            link(pool.memset(vaug[:, :, :, :, D:D + 1].rearrange("p a t h o -> p (a t h) o"), 1.0))
            pool.memset(cexp[:, 0:1], -0.5).then_inc(const_ready, 1)

            def inverse_root(name):
                gp.wait_ge(var_ready, NORMS.index(name) + 1)
                link(pool.tensor_scalar(srs[:, :], mv[:, :, 1], EPS, None, ALU.add))
                end = pool.tensor_tensor(rstd[:, :], srs[:, :], cexp[:, 0:1].broadcast_to((P, TPB)), ALU.pow)
                if name[0] == "ln2":
                    link(end)
                    gp.wait_ge(gamma_ready, 1)
                    end = pool.tensor_scalar(rstd[:, :], rstd[:, :], gam[:, 2:3], None, ALU.mult)
                end.then_inc(rstd_ready, 1)

            def stage_a(b):
                if b == 0:
                    link(pool.memset(nmp, 0.0))
                    link(pool.memset(sel, 0.0))
                    for j in range(3):
                        link(pool.affine_select(out=sel, in_=sel, compare_op=ALU.not_equal, fill=1.0, base=-16 * j,
                                                pattern=[[-1, H], [0, P]], channel_multiplier=1))
                    gp.wait_ge(gamma_sig, 1)
                    link(pool.tensor_scalar(gam[:, 2:3], gam[:, 1:2], -1.0, 1.0, ALU.mult, ALU.add))
                    pool.tensor_scalar(gam[:, 3:4], gam[:, 1:2], 0.5, None, ALU.mult).then_inc(gamma_ready, 1)
                inverse_root(("ln1", b))
                emptied(gp, "proj", ("qk", b))
                gp.wait_ge(rope_in, 32)
                pool.tensor_tensor(qks, qks, sinb.unsqueeze(1).broadcast_to((P, 4, S)), ALU.mult).then_inc(sin_done, 1)
                if b == 0:
                    gp.wait_ge(gamma_ready, 1)
                    for u in range(2):
                        gp.wait_ge(adj_sig, u + 1)
                        half = adj[:, 4 * u:4 * u + 4, :].rearrange("p t s -> p (t s)")
                        pool.tensor_scalar(half, half, gam[:, 3:4], None, ALU.mult).then_inc(adj_half, 1)
                gp.wait_ge(part1, b + 1)
                pool.tensor_tensor(parts[:, 2], qkc, parts[:, 1], ALU.subtract).then_inc(part2, 1)

            def stage_c(b):
                for n, key in enumerate(USES["C"]["unit"]):
                    emptied(gp, "unit", (key, b))
                    w = S - key[1] * P
                    v = prob[:, n, :].rearrange("p (h q) -> p h q", q=w)[:, :, 0:P]
                    pool.affine_select(out=v, in_=v, compare_op=ALU.is_ge, fill=0.0, base=0,
                                       pattern=[[0, 1024 // w], [1, P]], channel_multiplier=-1).then_inc(prob_ready, 1)

            def stage_d(b):
                inverse_root(("ln2", b))
                inverse_root(("ln3", b))

            for stage, b in STAGES:
                if stage != "B":
                    {"A": stage_a, "C": stage_c, "D": stage_d}[stage](b)
                if (stage, b) == ("A", 2):
                    link(pool.memset(tri[:, :], 1.0))
                    link(pool.affine_select(out=tri[:, :], in_=tri[:, :], compare_op=ALU.is_ge, fill=0.0, base=-1,
                                            pattern=[[1, P]], channel_multiplier=-1))
                    link(pool.memset(ones[:, :], 1.0))
                    link(pool.iota(iotac[:, :], pattern=[[1, CAP]], base=0, channel_multiplier=0, allow_small_or_imprecise_dtypes=True))
                    link(pool.memset(keep[:, :, :], 1.0))
                    link(pool.memset(keep[:, :, 0:1], 0.0))
                    pool.memset(ring_dn[FF:P].rearrange("p a e n -> p (a e n)"), 0.0).then_inc(const_act, 1)
                    gp.wait_ge(const_act, 1)
            gp.wait_ge(x3_ready, B)
            emptied(gp, "gen", ("lg", B - 1))
            link(pool.memset(gsum, NEG))
            link(pool.memset(selb[:, 0:NT - 1, :], 0.0))
            link(pool.memset(hidT, 0.0))
            link(pool.memset(hotbuf.rearrange("p a t e c -> p (a t e c)"), 0.0))
            link(pool.memset(vals.rearrange("p t e v -> p (t e v)"), 1.0))
            link(pool.iota(vals[:, :, :, 0], pattern=[[0, NT], [0, NE]], base=0,
                           channel_multiplier=1, allow_small_or_imprecise_dtypes=True))
            pool.iota(vals[:, :, :, 1], pattern=[[P, NT], [0, NE]], base=0,
                      channel_multiplier=0, allow_small_or_imprecise_dtypes=True).then_inc(const_act, 1)

            for s in range(1):
                gp.wait_ge(x3_out, 16 * B)
                gp.wait_ge(z_zeroed, 16 * NT)

            def gather(p):
                gp.wait_ge(index_ready, p // PPG + 1)
                if p >= 4:
                    gp.wait_ge(xt_full, p - 3)
                pool.indirect_dma_start(out=xg[:, p % 4, :], out_offset=None, in_=x3_dram,
                                        in_offset=bass.IndirectOffsetOnAxis(ap=toki[:, p:p + 1], axis=0)).then_inc(gathered[p % 4], 16)

            for p in range(NP + 4):
                if p < NP:
                    gather(p)
                if p >= 4:
                    q = p - 4
                    gp.wait_ge(y_free, q + 1)
                    pool.indirect_dma_start(out=z_dram, out_offset=bass.IndirectOffsetOnAxis(ap=rowi[:, q:q + 1], axis=0),
                                            in_=yrow[:, q % 4, :], in_offset=None, bounds_check=T * 8 - 1,
                                            oob_is_err=False).then_inc(scattered[q % 4], 16)

        @block.vector
        def _(ve):
            steps = [0]
            v = nc.vector

            def link(ins):
                steps[0] += 1
                ins.then_inc(dve_step, 1)
                ve.wait_ge(dve_step, steps[0])

            def adjacency():
                rounds = (TOPA - 1) // 8
                for t in range(NT):
                    for r in range(rounds + 1):
                        src = simS[:, t, :] if r == 0 else work
                        if r == 0:
                            emptied(ve, "unit", ("sim", t // 4))
                        link(v.max(best, src))
                        if r < rounds:
                            link(v.match_replace(work, best, src, NEG))
                        yield t
                    col = (TOPA - 1) % 8
                    ve.wait_ge(adj_half, t // 4 + 1)
                    ins = v.scalar_tensor_tensor(adj[:, t, :], simS[:, t, :], best[:, col:col + 1], adj[:, t, :], ALU.is_ge, ALU.mult)
                    if t % TPB == TPB - 1:
                        ins.then_inc(adj_row, 1)
                        ve.wait_ge(adj_row, t // TPB + 1)
                    else:
                        link(ins)
                    yield t
                while True:
                    yield NT

            filler = adjacency()
            at_tile = [0]

            def fill(n):
                for _ in range(n):
                    at_tile[0] = next(filler)

            def stats(name, src):
                for t in range(TPB):
                    link(v.bn_stats(st6[:, t, :], src[:, t, :]))
                v.bn_aggr(mv[:, 0, :], st6[:, 0, :])
                v.bn_aggr(mv[:, 1, :], st6[:, 1, :]).then_inc(var_ready, 1)
                ve.wait_ge(rstd_ready, NORMS.index(name) + 1)

            def stage_a(b):
                ve.wait_ge(x_in[b], 16)
                stats(("ln1", b), res[:, TPB * b:TPB * b + TPB, :])
                if b >= 2:
                    filled(ve, "gen", ("xnT", b - 2))
                for t in range(TPB):
                    ins = v.tensor_scalar(xn[:, b % 2, t, :], res[:, TPB * b + t, :], mv[:, t, 0:1], rstd[:, t:t + 1], ALU.subtract, ALU.mult)
                ins.then_inc(xn_ready, 1)
                fill(2)
                filled(ve, "proj", ("qk", b))
                ve.wait_ge(rope_in, 32)
                if b >= 1:
                    ve.wait_ge(part2, b)
                pv = proj[:, :].rearrange("p (m s) -> p m s", m=4)
                v.tensor_tensor(qkc, pv, cosb.unsqueeze(1).broadcast_to((P, 4, S)), ALU.mult)
                v.stream_shuffle(qks.rearrange("p m s -> p (m s)"), proj[:, :], [i ^ 1 for i in range(32)]).then_inc(free["proj"], 1)
                fill(3)
                ve.wait_ge(sin_done, b + 1)
                v.tensor_tensor(qkc, qkc, qks, ALU.add).then_inc(roped, 1)
                fill(2)
                ve.wait_ge(part0, b + 1)
                v.tensor_tensor(qkc, qkc, parts[:, 0], ALU.subtract).then_inc(rest_ready, 1)
                if b == 0:
                    fill(4)

            def stage_b(b):
                for key in USES["B"]["unit"]:
                    _, t, u = key
                    n = P * (t + 1)
                    c = 1024 // n
                    filled(ve, "unit", (key, b))
                    v.tensor_reduce(nmax[:, t, c * u:c * u + c], unit_at((key, b)).rearrange("p (h k) -> p h k", k=n), axis=AX,
                                    op=ALU.max, negate=True).then_inc(unit_free((key, b)), 1)
                    fill(3)
                emptied(ve, "unit", (USES["B"]["unit"][-1], b))
                if b >= 1:
                    filled(ve, "gen", ("mT", b - 1))
                link(v.tensor_copy(nmp[:, :, 0:H], nmax))
                link(v.tensor_tensor(nmr, nmax, nmp[:, :, 0:H], ALU.subtract))
                link(v.tensor_copy(nmp[:, :, H:2 * H], nmr))
                v.tensor_tensor(nmp[:, :, 2 * H:3 * H], nmr, nmp[:, :, H:2 * H], ALU.subtract).then_inc(shift_ready, 1)

            def stage_c(b):
                filled(ve, "gen", ("mT", b))
                if b >= 1:
                    filled(ve, "unit", (("T", 0, 3), b - 1))
                v.tensor_copy(nmT, genb[:, 0:S]).then_inc(free["gen"], 1)
                for half in range(2):
                    fill(3)
                    filled(ve, "out", (half, b))
                    if b >= 1:
                        filled(ve, "proj", ("otok", b - 1))
                    v.tensor_copy(oT[:, 2 * half:2 * half + 2, :].rearrange("p g s -> p (g s)"), outp[:, :]).then_inc(free["out"], 1)

            def stage_d(b):
                while at_tile[0] < TPB * (b + 1):
                    fill(1)
                rows = res[:, TPB * b:TPB * b + TPB, :]
                filled(ve, "proj", ("otok", b))
                ov = proj[:, :].rearrange("p (t h d) -> p t h d", t=TPB, d=32)
                link(v.reciprocal(rec, ov[:, :, :, D]))
                if b >= 1:
                    filled(ve, "gen", ("onT", b - 1))
                v.tensor_tensor(otok.rearrange("p t (h d) -> p t h d", d=D), ov[:, :, :, 0:D],
                                rec.unsqueeze(3).broadcast_to((P, TPB, H, D)), ALU.mult).then_inc(free["proj"], 1)
                filled(ve, "gen", ("att", b))
                n = nth("gen", ("att", b))
                v.tensor_tensor(rows, rows, gen[:, :].rearrange("p (t e) -> p t e", t=TPB), ALU.add).then_inc(free["gen"], 1)
                ve.wait_ge(free["gen"], n + 1)
                stats(("ln2", b), rows)
                for t in range(TPB):
                    ins = v.tensor_scalar(mix[:, t, :], rows[:, t, :], mv[:, t, 0:1], rstd[:, t:t + 1], ALU.subtract, ALU.mult)
                link(ins)
                filled(ve, "gen", ("aT", b))
                a = adj[:, TPB * b:TPB * b + TPB, :]
                v.tensor_tensor(a, a, gen[:, :].rearrange("p (t e) -> p t e", t=TPB), ALU.add).then_inc(free["gen"], 1)
                ve.wait_ge(free["gen"], n + 2)
                link(v.tensor_tensor(mix, mix, a, ALU.add))
                link(v.tensor_tensor(rows, rows, mix, ALU.add))
                stats(("ln3", b), rows)
                for t in range(TPB):
                    ins = v.tensor_scalar(x3[:, TPB * b + t, :], rows[:, t, :], mv[:, t, 0:1], rstd[:, t:t + 1], ALU.subtract, ALU.mult)
                ins.then_inc(x3_ready, 1)

            def top2(hi, lo, hs, ls, ta, tb, n):
                link(v.tensor_tensor(hi, hs[:, :, 0:n], hs[:, :, n:2 * n], ALU.max))
                link(v.tensor_tensor(ta, hs[:, :, 0:n], hs[:, :, n:2 * n], ALU.min))
                link(v.tensor_tensor(tb, ls[:, :, 0:n], ls[:, :, n:2 * n], ALU.max))
                link(v.tensor_tensor(lo, ta, tb, ALU.max))

            def route():
                ve.wait_ge(const_act, 2)
                ve.wait_ge(score_ready, 1)
                link(v.tensor_tensor(sbias, score, biasb[:, :].unsqueeze(1).broadcast_to((P, NT, NE)), ALU.add))
                g8 = sbias.rearrange("p t (g j) -> p (t g) j", j=NE // NG)
                link(v.tensor_tensor(hi1, g8[:, :, 0:4], g8[:, :, 4:8], ALU.max))
                link(v.tensor_tensor(lo1, g8[:, :, 0:4], g8[:, :, 4:8], ALU.min))
                top2(hi2, lo2, hi1, lo1, ta2, tb2, 2)
                top2(hi3, lo3, hi2, lo2, ta3, tb3, 1)
                tg = lambda a: a.rearrange("p (t g) o -> p t (g o)", t=NT)
                link(v.tensor_tensor(gsum[:, :, 0:NG], tg(hi3), tg(lo3), ALU.add))
                for t in range(NT):
                    ins = v.max(gtop[:, t, :], gsum[:, t, 0:NG])
                link(ins)
                v.memset(gpick, NEG)
                link(v.memset(epick, 3 * NEG))
                link(v.tensor_copy(gpick[:, :, 0:KG], gtop[:, :, 0:KG]))
                for t in range(NT):
                    ins = v.match_replace(gout[:, t, :], gpick[:, t, :], gsum[:, t, :], -NEG)
                link(ins)
                link(v.tensor_scalar(gpen, gout[:, :, 0:NG], -NEG / 10, 1.0, ALU.is_ge, ALU.subtract))
                link(v.tensor_scalar(gpen, gpen, -NEG, None, ALU.mult))
                link(v.memset(cand, 3 * NEG))
                link(v.tensor_tensor(cand[:, :, 0:NE].rearrange("p t (g j) -> p t g j", g=NG),
                                     sbias.rearrange("p t (g j) -> p t g j", g=NG),
                                     gpen.unsqueeze(3).broadcast_to((P, NT, NG, NE // NG)), ALU.add))
                for t in range(NT):
                    ins = v.max(etop[:, t, :], cand[:, t, 0:NE])
                link(ins)
                link(v.tensor_copy(epick[:, :, 0:KE], etop[:, :, 0:KE]))
                for t in range(NT):
                    ins = v.match_replace(eout[:, t, :], epick[:, t, :], cand[:, t, :], -NEG)
                link(ins)
                v.tensor_scalar(selb[:, NT - 1:, :], eout[:, :, 0:NE], -NEG / 10, None, ALU.is_ge).then_inc(sel_ready, 1)
                link(v.tensor_scalar(selm, eout[:, :, 0:NE], -NEG / 10, None, ALU.is_ge))
                link(v.tensor_tensor(wsel, score, selm, ALU.mult))
                link(v.reduce_sum(wsum, wsel, axis=AX))
                link(v.reciprocal(wsum, wsum))
                link(v.tensor_scalar(wsum, wsum, SCALE, None, ALU.mult))
                link(v.tensor_tensor(wsel, wsel, wsum.unsqueeze(2).broadcast_to((P, NT, NE)), ALU.mult))
                link(v.tensor_copy(vals[:, :, :, 3], wsel))
                link(v.tensor_tensor(wsel, wsel, vals[:, :, :, 3], ALU.subtract))
                link(v.tensor_copy(vals[:, :, :, 4], wsel))
                link(v.tensor_tensor(vals[:, :, :, 5], wsel, vals[:, :, :, 4], ALU.subtract))
                fl = lambda a: a.rearrange("p t e -> p (t e)")
                link(v.tensor_tensor_scan(fl(rank), fl(keep[:, :, :]), fl(selm), 0.0, ALU.mult, ALU.add))
                v.tensor_scalar(vals[:, :, :, 2], rank, -1.0, None, ALU.add).then_inc(vals_ready, 1)
                link(v.tensor_scalar(selm, selm, -float(T), float(T), ALU.mult, ALU.add))
                filled(ve, "gen", "pos")
                n = nth("gen", "pos")
                v.tensor_tensor(fl(slot), gen[:, :], fl(selm), ALU.add).then_inc(free["gen"], 1)
                ve.wait_ge(free["gen"], n + 1)

            def shared():
                for n in range(2):
                    ve.wait_ge(sh_act, n + 1)
                    u = unit_at(("sg", n))
                    cols = slice(n * 512, (n + 1) * 512)
                    v.tensor_tensor(hsh[0:FF, cols], ssh[0:FF, cols], u[0:FF, 512:1024], ALU.mult).then_inc(unit_free(("sg", n)), 1)
                    emptied(ve, "unit", ("sg", n))
                    v.memset(st6[:, 0, 0:1], 0.0).then_inc(sh_hid, 1)

            def shared_add():
                for n in range(2):
                    filled(ve, "unit", ("sd", n))
                    r = res[:, 4 * n:4 * n + 4, :].rearrange("p t e -> p (t e)")
                    v.tensor_tensor(r, r, unit_at(("sd", n)), ALU.add).then_inc(unit_free(("sd", n)), 1)

            def one_hot(g):
                if g >= 2:
                    ve.wait_ge(info_full, g - 1)
                v.tensor_tensor(hotbuf[:, g % 2, :, :, 0:CAP], slot[:, :, EPG * g:EPG * (g + 1)].unsqueeze(3).broadcast_to((P, NT, EPG, CAP)),
                                iotac[:, :].unsqueeze(1).unsqueeze(1).broadcast_to((P, NT, EPG, CAP)), ALU.is_equal).then_inc(hot_ready, 1)

            def indices(g):
                ve.wait_ge(info_full, g + 1)
                o = g % 2
                gv = gen[:, 0:PPG * 16].rearrange("p (q e v) -> p q e v", q=PPG, e=2)
                v.tensor_copy(info[0:CP, o], gv[0:CP, :, 0, :])
                v.tensor_copy(info[CP:P, o], gv[CP:P, :, 1, :]).then_inc(info_free, 1)
                ve.wait_ge(info_free, g + 1)
                cols = slice(PPG * g, PPG * (g + 1))
                link(v.tensor_tensor(tokf[:, o], info[:, o, :, 0], info[:, o, :, 1], ALU.add))
                v.tensor_copy(toki[:, cols], tokf[:, o])
                link(v.tensor_scalar(tmpf[:, o], info[:, o, :, 6], -16.0 * T, 16.0 * T, ALU.mult, ALU.add))
                link(v.scalar_tensor_tensor(rowf[:, o], tokf[:, o], 8.0, info[:, o, :, 2], ALU.mult, ALU.add))
                link(v.tensor_tensor(rowf[:, o], rowf[:, o], tmpf[:, o], ALU.add))
                link(v.tensor_copy(rowi[:, cols], rowf[:, o]))
                link(v.tensor_tensor(tmpf[:, o], info[:, o, :, 3], info[:, o, :, 4], ALU.add))
                v.tensor_tensor(wslot[:, cols], tmpf[:, o], info[:, o, :, 5], ALU.add).then_inc(index_ready, 1)

            for stage, b in STAGES:
                {"A": stage_a, "B": stage_b, "C": stage_c, "D": stage_d}[stage](b)
            shared()
            route()
            shared_add()
            one_hot(0)
            one_hot(1)
            indices(0)
            indices(1)
            for p in range(NP + 3):
                if p < NP:
                    ve.wait_ge(xt_full, p + 1)
                    if p >= 2:
                        ve.wait_ge(gu_full, p - 1)
                    v.tensor_copy(xgT[:, p % 2].rearrange("p c s -> p (c s)"), unit[:, 0, (p % 2) * 512:(p % 2) * 512 + E]).then_inc(xt_free, 1)
                if 0 <= p - 1 < NP:
                    q = p - 1
                    ve.wait_ge(act_ready, q + 1)
                    if q >= 2:
                        ve.wait_ge(ht_full, q - 1)
                    v.tensor_tensor(hid[:, q % 2, :], act[:, q % 2, :], unit[:, 1, (q % 2) * 512 + FF:(q % 2) * 512 + 2 * FF], ALU.mult).then_inc(hid_ready, 1)
                if 0 <= p - 2 < NP:
                    q = p - 2
                    ve.wait_ge(ht_full, q + 1)
                    if q >= 2:
                        ve.wait_ge(y_full, q - 1)
                    v.tensor_copy(hidT[0:FF, q % 2, :], outp[0:FF, 0:P]).then_inc(ht_free, 1)
                if p % PPG == 0 and p // PPG + 2 < NSM:
                    one_hot(p // PPG + 2)
                    indices(p // PPG + 2)
            for t in range(NT):
                ve.wait_ge(z_in[t % 2], 16 * (t // 2 + 1))
                if t >= 2:
                    ve.wait_ge(out_done[t % 2], 16 * (t // 2))
                link(v.reduce_sum(fin[:, t % 2], zin[:, t % 2].rearrange("p k e -> p e k"), axis=AX))
                v.tensor_tensor(fin[:, t % 2], fin[:, t % 2], res[:, t, :], ALU.add).then_inc(fin_ready, 1)


def rope_tables():
    inv = 1.0 / np.float32(10000.0) ** (np.arange(0, D, 2, dtype=np.float32) / np.float32(D))
    ang = np.outer(np.arange(S, dtype=np.float32), inv.astype(np.float32)).astype(np.float32)
    ang = np.concatenate([ang, ang], axis=-1).T
    sign = np.where(np.arange(D) % 2 == 0, -1.0, 1.0).astype(np.float32)[:, None]
    cos, sin = np.cos(ang).astype(np.float32), (np.sin(ang) * sign).astype(np.float32)
    return np.tile(cos, (P // D, 1)), np.tile(sin, (P // D, 1))


def kernel(x, ctx_512, L0_attn_Wqkv, L0_attn_Wout, L0_xattn_Wq, L0_xattn_Wk, L0_xattn_gamma_raw, L0_ffn_gate_w, L0_ffn_bias,
           L0_ffn_w_gate, L0_ffn_w_up, L0_ffn_w_down, L0_ffn_ws_gate, L0_ffn_ws_up, L0_ffn_ws_down):
    import numpy as _np
    import concourse.bacc as _bacc
    from concourse import mybir as _mybir
    from concourse.bass_utils import run_bass_kernel_spmd as _run

    a = _np.asarray
    cos, sin = rope_tables()
    gu = _np.stack([a(L0_ffn_w_gate), a(L0_ffn_w_up)], axis=2).reshape(NP, 2, 2, P, 2, FF)
    ins = {
        "x": a(x).reshape(T, E),
        "cosT": cos, "sinT": sin,
        "ctxT": a(ctx_512).reshape(T, DC).T,
        "wxT": _np.stack([a(L0_xattn_Wq).T, a(L0_xattn_Wk).T]),
        "wqkvT": a(L0_attn_Wqkv).T,
        "woT": a(L0_attn_Wout).T,
        "gamma": a(L0_xattn_gamma_raw).reshape(1, 1),
        "gate_w": a(L0_ffn_gate_w),
        "bias": a(L0_ffn_bias).reshape(1, NE),
        "w_gu": gu.transpose(0, 3, 1, 2, 4, 5).reshape(NP, P, 8 * FF),
        "w_dn": a(L0_ffn_w_down).reshape(NP, 2, FF, E).transpose(0, 2, 1, 3).reshape(NP, FF, 2 * E),
        "ws_gu": _np.concatenate([a(L0_ffn_ws_gate), a(L0_ffn_ws_up)], axis=1),
        "ws_dn": a(L0_ffn_ws_down),
    }
    nc = _bacc.Bacc("TRN2", target_bir_lowering=False, num_devices=1)
    arrays, args = {}, []
    for name, arr in ins.items():
        arr = _np.ascontiguousarray(arr)
        arrays[f"in_{name}"] = arr
        args.append(nc.dram_tensor(f"in_{name}", arr.shape, _mybir.dt.from_np(arr.dtype), kind="ExternalInput").ap())
    args.append(nc.dram_tensor("out_0", (T, E), _mybir.dt.float32, kind="ExternalOutput").ap())
    decoder_kernel(nc, *args)
    r = _run(nc, [arrays], core_ids=[0])
    return r.results[0]["out_0"].reshape(B, S, E)
```

```python
from contextlib import ExitStack

import numpy as np
import concourse.bass as bass
from concourse import mybir

F32 = mybir.dt.float32
BF16 = mybir.dt.bfloat16
I32 = mybir.dt.int32
ALU = mybir.AluOpType
ACT = mybir.ActivationFunctionType
AX = mybir.AxisListType.X

P = 128
B, S, E = 4, 256, 256
T = B * S
NT = T // P
TPB = S // P
H, D = 16, 16
DC = 64
HC = 4
TOPA = max(1, int(S * 0.3))
NE, KE, FF = 64, 6, 96
NG, KG = 8, 4
CAP = 2 * (2 * 128 * KE // NE)
CP = 64
SCALE = 2.5
NP = NE // 2
EPG = 8
PPG = EPG // 2
NSM = NE // EPG
RP = 8
NX = 8
NZ = 4
FILL_START, FILL_PROJ, FILL_SIN, FILL_MAX, FILL_D = 8, 8, 5, 3, 3
EPS = 1e-5
NEG = -1e30
TERMS_Q = (0, 0, 0, 1, 1, 2)
TERMS_K = (0, 1, 2, 0, 1, 0)
KT = len(TERMS_Q) * D

STAGES = [("X0", 0), ("A1", 0), ("X1", 0), ("A2", 0), ("X2", 0), ("A1", 1), ("A2", 1), ("M", 0), ("A1", 2), ("A2", 2),
          ("M", 1), ("D1", 0), ("A1", 3), ("D2", 0), ("A2", 3), ("D3", 0),
          ("M", 2), ("D1", 1), ("D2", 1), ("D3", 1), ("M", 3), ("D1", 2), ("D2", 2), ("D3", 2),
          ("M", 4), ("D1", 3), ("D2", 3), ("D3", 3)]

S_UNITS = [("S", 0, 0), ("S", 0, 1), ("S", 1, 0), ("S", 1, 1), ("S", 1, 2), ("S", 1, 3)]
T_UNITS = [("T", 1, 0), ("T", 0, 0), ("T", 0, 1), ("T", 1, 1), ("T", 0, 2), ("T", 0, 3)]

AREAS = {"gen": [], "proj": [], "unit": [], "out": []}
NORMS = []
for _st, _b in STAGES:
    AREAS["gen"] += [(_n, _b) for _n in {"A1": ["xnT", "v"], "D1": ["aT", "onT", "att"], "D3": ["x3T", "lg"]}.get(_st, [])]
    AREAS["proj"] += [(_n, _b) for _n in {"X0": ["QT"], "X1": ["KT"], "A1": ["qk"], "D1": ["otok"]}.get(_st, [])]
    NORMS += {"A1": [("ln1", _b)], "D1": [("ln2", _b)], "D2": [("ln3", _b)]}.get(_st, [])
    if _st == "X2":
        AREAS["unit"] += [("sim", 0), ("sim", 1)]
    if _st == "M":
        if _b >= 1:
            AREAS["gen"] += [("mT", _b - 1)]
            AREAS["out"] += [(0, _b - 1), (1, _b - 1)]
        for _n in range(6):
            AREAS["unit"] += [(T_UNITS[_n], _b - 1)] * (_b >= 1) + [(S_UNITS[_n], _b)] * (_b < B)
AREAS["gen"] += ["pos"]
AREAS["unit"] += [("sg", 0), ("sg", 1), ("sd", 0), ("sd", 1)]


def nth(area, name):
    return AREAS[area].index(name)


def decoder_kernel(nc, x, cosT, sinT, ctxT, wxT, wqkvT, woT, gamma, gate_w, bias, w_gu, w_dn, ws_gu, ws_dn, out):
    qk_dram = nc.dram_tensor("qk_parts", [B, 3, 2 * E, S], BF16, kind="Internal").ap()
    x3_dram = nc.dram_tensor("moe_input", [T, E], F32, kind="Internal").ap()
    z_dram = nc.dram_tensor("expert_rows", [T * 8, E], F32, kind="Internal").ap()

    with ExitStack() as ctx:
        def sb(name, shape, dt=F32):
            return ctx.enter_context(nc.sbuf_tensor(name, shape, dt))

        def pb(name, shape):
            return ctx.enter_context(nc.psum_tensor(name, shape, F32))

        def sem(name):
            return ctx.enter_context(nc.semaphore(name))

        res = sb("res", [P, NT, E])
        x3 = sb("x3", [P, NT, E])
        x3T = sb("x3T", [P, 2, T])
        adj = sb("adj", [P, NT, S])
        ring = sb("ring", [P, RP, 2, 2, 2, FF])
        ring_dn = sb("ring_dn", [P, RP, 2, E])
        identf = sb("identf", [P, P])
        identb = sb("identb", [P, P], BF16)
        tri = sb("tri", [P, P], BF16)
        ones = sb("ones", [P, P], BF16)
        gatew = sb("gatew", [P, 2, NE])
        wsgu = sb("wsgu", [P, 2, 2 * FF])
        wsdn = sb("wsdn", [FF, E])
        biasb = sb("biasb", [P, NE])
        logit = sb("logit", [P, NT, NE])
        iotac = sb("iotac", [P, CAP, NT], BF16)
        keep = sb("keep", [P, NT, NE])
        mv = sb("mv", [P, 3, TPB, 2])
        st6 = sb("st6", [P, TPB, 6])
        rstd = sb("rstd", [P, 3, TPB])
        srs = sb("srs", [P, TPB])
        gam = sb("gam", [P, 4])
        zero = sb("zero", [P, E])
        cexp = sb("cexp", [P, 2])

        ARENA = 32000
        arena = sb("arena", [P, ARENA])
        at = {"attention": 0, "moe": 0}

        def cut(phase, *shape, dt=F32):
            n = int(np.prod(shape))
            words = n if dt != BF16 else (n + 1) // 2
            a = arena[:, at[phase]:at[phase] + words]
            at[phase] += words
            pass
            if dt != F32:
                a = a.bitcast(dt)
            names = "abcde"[:len(shape)]
            if len(shape) > 1:
                a = a.rearrange(f"p ({' '.join(names)}) -> p {' '.join(names)}",
                                **{k: v for k, v in zip(names[1:], shape[1:])})
            return a

        AT = "attention"
        wqkv = cut(AT, 2, 3 * E)
        wo = cut(AT, 2, E)
        cosb = cut(AT, S)
        sinb = cut(AT, S)
        masks = cut(AT, P, dt=BF16)
        sel = cut(AT, H, P, dt=BF16)
        xn = cut(AT, 2, TPB, E)
        xnT = cut(AT, 2, 2, S)
        qkc = cut(AT, 4, S)
        qks = cut(AT, 4, S)
        parts = cut(AT, 3, 4, S, dt=BF16)
        qst = cut(AT, 2, H, S, dt=BF16)
        kst = cut(AT, 2, H, S, dt=BF16)
        vaug = cut(AT, 3, TPB, H, 32)
        nmax = cut(AT, TPB, H)
        nmr = cut(AT, TPB, H)
        nmp = cut(AT, TPB, P, dt=BF16)
        nmT = cut(AT, S, dt=BF16)
        prob = cut(AT, 6, 1024)
        oT = cut(AT, 4, S)
        otok = cut(AT, TPB, E)
        onT = cut(AT, 2, S)
        rec = cut(AT, TPB, H)
        mix = otok
        simS = cut(AT, NT, S)
        work = cut(AT, 2, S)
        best = cut(AT, 2, 8)
        ctxs = prob[:, 0, :]
        wx = prob[:, 1, 0:2 * P].rearrange("p (a b) -> p a b", a=2)
        cq = prob[:, 2, :]
        ck = prob[:, 3, :]

        MO = "moe"
        vals = cut(MO, NT, NE, 8, dt=BF16)
        hotbuf = cut(MO, 2, EPG, CP, NT, dt=BF16)
        score = cut(MO, NT, NE)
        sbias = cut(MO, NT, NE)
        hi1, lo1 = cut(MO, NT * NG, 4), cut(MO, NT * NG, 4)
        hi2, lo2, ta2, tb2 = (cut(MO, NT * NG, 2) for _ in range(4))
        hi3, lo3, ta3, tb3 = (cut(MO, NT * NG, 1) for _ in range(4))
        gsum = cut(MO, NT, 12)
        gtop = cut(MO, NT, 8)
        gpick = cut(MO, NT, 8)
        gout = cut(MO, NT, 12)
        gpen = cut(MO, NT, NG)
        cand = cut(MO, NT, NE + 2)
        etop = cut(MO, NT, 8)
        epick = cut(MO, NT, 8)
        eout = cut(MO, NT, NE + 2)
        selm = cut(MO, NT, NE)
        selb = cut(MO, 2 * NT - 1, NE, dt=BF16)
        wsel = cut(MO, NT, NE)
        wsum = cut(MO, NT)
        rank = cut(MO, NT, NE)
        slot = cut(MO, NE, NT, dt=BF16)
        info = cut(MO, 2, PPG, 8)
        tokf = cut(MO, 2, PPG)
        rowf = cut(MO, 2, PPG)
        tmpf = cut(MO, 2, PPG)
        toki = cut(MO, NP, dt=I32)
        rowi = cut(MO, NP, dt=I32)
        wslot = cut(MO, NP)
        hsh = cut(MO, T)
        ssh = cut(MO, T)
        xg = cut(MO, NX, E)
        xgT = cut(MO, 2, 2, P)
        act = cut(MO, 2, FF)
        hid = cut(MO, 2, FF)
        hidT = cut(MO, 2, P)
        yrow = cut(MO, NX, E)
        zin = cut(MO, NZ, KE, E)
        fin = cut(MO, NZ, E)

        unit = pb("unit", [P, 2, 1024])
        proj = pb("proj", [P, 1024])
        gen = pb("gen", [P, 512])
        outp = pb("outp", [P, 512])
        genb = gen[:, :].bitcast(BF16)

        x_in = [sem(f"x_in{b}") for b in range(B)]
        ctx_in, gamma_in, rope_in, wqkv_in, wo_in, moe_in = (sem(n) for n in ("ctx_in", "gamma_in", "rope_in", "wqkv_in", "wo_in", "moe_in"))
        parts_out = [sem(f"parts_out{b}") for b in range(B)]
        stack_in = [sem(f"stack_in{b}") for b in range(B)]
        x3_out = sem("x3_out")
        z_zeroed = sem("z_zeroed")
        ring_in = [sem(f"ring_in{i}") for i in range(RP)]
        gathered = [sem(f"gathered{i}") for i in range(NX)]
        scattered = [sem(f"scattered{i}") for i in range(NX)]
        z_in = [sem(f"z_in{i}") for i in range(NZ)]
        out_done = [sem(f"out_done{i}") for i in range(NZ)]
        dve_step, act_step, pool_step = sem("dve_step"), sem("act_step"), sem("pool_step")
        full = {a: sem(f"{a}_full") for a in AREAS}
        free = {"gen": sem("gen_free"), "proj": sem("proj_free"), "out": sem("out_free"),
                "unit": [sem("unit_free0"), sem("unit_free1")]}
        ident_ready, pads_ready, const_ready, order_ready, pick_ready, vals_init = (
            sem(n) for n in ("ident_ready", "pads_ready", "const_ready", "order_ready", "pick_ready", "vals_init"))
        zero_ready = sem("zero_ready")
        gamma_sig = sem("gamma_sig")
        var_ready, rstd_ready = sem("var_ready"), sem("rstd_ready")
        xn_ready, shuffled, sin_done, roped, part0, rest_ready, part1, part2 = (
            sem(n) for n in ("xn_ready", "shuffled", "sin_done", "roped", "part0", "rest_ready", "part1", "part2"))
        shift_ready, prob_ready, sim_ready, adj_half, adj_row = (
            sem(n) for n in ("shift_ready", "prob_ready", "sim_ready", "adj_half", "adj_row"))
        x3_ready = sem("x3_ready")
        score_ready, sel_ready, vals_ready = sem("score_ready"), sem("sel_ready"), sem("vals_ready")
        sh_act, sh_hid = sem("sh_act"), sem("sh_hid")
        hot_ready, info_full, info_free, index_ready = (
            sem(n) for n in ("hot_ready", "info_full", "info_free", "index_ready"))
        xt_full, xt_free, gu_full, act_ready, hid_ready, ht_full, ht_free, y_full, y_free = (
            sem(n) for n in ("xt_full", "xt_free", "gu_full", "act_ready", "hid_ready", "ht_full", "ht_free",
                             "y_full", "y_free"))
        fin_ready = sem("fin_ready")

        def filled(eng, area, name):
            eng.wait_ge(full[area], nth(area, name) + 1)

        def emptied(eng, area, name):
            n = nth(area, name)
            if area == "unit":
                eng.wait_ge(free["unit"][n % 2], n // 2 + 1)
            else:
                eng.wait_ge(free[area], n + 1)

        def unit_free(name):
            return free["unit"][nth("unit", name) % 2]

        def unit_at(name):
            return unit[:, nth("unit", name) % 2, :]

        def probs_at(key):
            return prob[:, T_UNITS.index(key), :]

        block = ctx.enter_context(nc.Block())

        @block.sync
        def _(sp):
            xv = x.rearrange("(t p) e -> p t e", p=P)
            sp.dma_start(ctxs[0:DC, :], ctxT).then_inc(ctx_in, 16)
            sp.dma_start(wx[0:DC, :, 0:DC], wxT.rearrange("a k n -> k a n")).then_inc(ctx_in, 16)
            sp.dma_start(res[:, 0:TPB, :], xv[:, 0:TPB, :]).then_inc(x_in[0], 16)
            sp.dma_start(wqkv, wqkvT.rearrange("(c p) n -> p c n", p=P)).then_inc(wqkv_in, 16)
            sp.dma_start(cosb, cosT).then_inc(rope_in, 16)
            sp.dma_start(sinb, sinT).then_inc(rope_in, 16)
            sp.dma_start(gam[:, 0:1], gamma.to_broadcast((P, 1))).then_inc(gamma_in, 16)
            for b in range(1, B):
                sp.dma_start(res[:, TPB * b:TPB * b + TPB, :], xv[:, TPB * b:TPB * b + TPB, :]).then_inc(x_in[b], 16)
            sp.dma_start(wo, woT.rearrange("(c p) n -> p c n", p=P)).then_inc(wo_in, 16)
            sp.dma_start(gatew[:, :, :], gate_w.rearrange("(c p) n -> p c n", p=P)).then_inc(moe_in, 16)
            sp.dma_start(wsgu[:, :, :], ws_gu.rearrange("(c p) n -> p c n", p=P)).then_inc(moe_in, 16)
            sp.dma_start(wsdn[:, :], ws_dn).then_inc(moe_in, 16)
            sp.dma_start(biasb[:, :], bias.to_broadcast((P, NE))).then_inc(moe_in, 16)

            def ring_fill(p):
                sp.dma_start(ring[:, p % RP].rearrange("p e c g f -> p (e c g f)"), w_gu[p]).then_inc(ring_in[p % RP], 16)
                sp.dma_start(ring_dn[0:FF, p % RP].rearrange("p e n -> p (e n)"), w_dn[p]).then_inc(ring_in[p % RP], 16)

            later = {("A2", 1): range(0, 2), ("A2", 2): range(2, 4), ("A2", 3): range(4, 6), ("D3", 1): range(6, RP)}
            for stage, b in STAGES:
                if stage == "A2":
                    for j, ready in enumerate((part0, part1, part2)):
                        sp.wait_ge(ready, b + 1)
                        sp.dma_start(qk_dram[b, j].rearrange("(c p) s -> p c s", p=P), parts[:, j]).then_inc(parts_out[b], 16)
                    sp.wait_ge(parts_out[b], 48)
                    if b >= 2:
                        filled(sp, "unit", (T_UNITS[-1], b - 2))
                    for dst, terms, off in ((qst, TERMS_Q, 0), (kst, TERMS_K, E)):
                        for n, m in ((0, 3), (3, 2), (5, 1)):
                            for i in range(n, n + m):
                                src = qk_dram[b, terms[i], off:off + E, :].rearrange("(h d) s -> d h s", d=D)
                                sp.dma_start(dst[i * D:(i + 1) * D, b % 2], src).then_inc(stack_in[b], 16)
                    if b == 1:
                        sp.wait_ge(zero_ready, 1)
                        zv = z_dram.rearrange("(t p k) n -> t p k n", p=P, k=8)
                        for t in range(NT):
                            sp.dma_start(zv[t, :, 0:KE, :], zero[:, :].unsqueeze(1).broadcast_to((P, KE, E))).then_inc(z_zeroed, 16)
                if stage == "D3":
                    sp.wait_ge(x3_ready, b + 1)
                    sp.dma_start(x3_dram.rearrange("(t p) e -> p t e", p=P)[:, TPB * b:TPB * b + TPB, :],
                                 x3[:, TPB * b:TPB * b + TPB, :]).then_inc(x3_out, 16)
                for p in later.get((stage, b), ()):
                    ring_fill(p)
            for p in range(RP, NP):
                sp.wait_ge(y_full, p - RP + 1)
                ring_fill(p)
            for s in range(NX):
                sp.wait_ge(scattered[s], 16 * (NP // NX))
            zv = z_dram.rearrange("(t p k) n -> t p k n", p=P, k=8)
            ov = out.rearrange("(t p) e -> t p e", p=P)

            def rows_in(t):
                sp.dma_start(zin[:, t % NZ], zv[t, :, 0:KE, :]).then_inc(z_in[t % NZ], 16)

            for t in range(NZ):
                rows_in(t)
            for t in range(NT):
                sp.wait_ge(fin_ready, t + 1)
                sp.dma_start(ov[t], fin[:, t % NZ]).then_inc(out_done[t % NZ], 16)
                if t + NZ < NT:
                    rows_in(t + NZ)
            for s in range(NZ):
                sp.wait_ge(out_done[s], 16 * (NT // NZ))

        @block.tensor
        def _(pe):
            mm = nc.tensor.matmul

            def claim(area, name):
                n = nth(area, name)
                if area == "unit":
                    if n >= 2:
                        pe.wait_ge(free["unit"][n % 2], n // 2)
                elif n >= 1:
                    pe.wait_ge(free[area], n)

            def context_projection(m):
                claim("proj", ("QT", 0) if m == 0 else ("KT", 0))
                if m == 0:
                    pe.wait_ge(pads_ready, 1)
                    pe.wait_ge(ctx_in, 32)
                for n in range(2):
                    last = mm(proj[:, n * 512:(n + 1) * 512], wx[:, m, :], ctxs[:, n * 512:(n + 1) * 512], start=True, stop=True)
                last.then_inc(full["proj"], 1)

            def similarity():
                emptied(pe, "proj", ("KT", 0))
                for u in range(2):
                    for j in range(4):
                        t = 4 * u + j
                        b = t // TPB
                        last = mm(unit[:, u, j * S:(j + 1) * S], cq[:, t * P:(t + 1) * P], ck[:, b * S:(b + 1) * S], start=True, stop=True)
                    last.then_inc(full["unit"], 1)

            def stage_a(b):
                claim("gen", ("xnT", b))
                pe.wait_ge(ident_ready, 1)
                pe.wait_ge(xn_ready, b + 1)
                for c in range(2):
                    for t in range(TPB):
                        last = nc.tensor.transpose(gen[:, (2 * c + t) * P:(2 * c + t + 1) * P], xn[:, b % 2, t, c * P:(c + 1) * P], identf[:, :])
                last.then_inc(full["gen"], 1)
                emptied(pe, "gen", ("xnT", b))
                pe.wait_ge(wqkv_in, 16)
                claim("proj", ("qk", b))
                for m in range(4):
                    for c in range(2):
                        last = mm(proj[:, m * S:(m + 1) * S], wqkv[:, c, m * P:(m + 1) * P], xnT[:, b % 2, c, :], start=(c == 0), stop=(c == 1))
                last.then_inc(full["proj"], 1)
                for t in range(TPB):
                    for c in range(2):
                        last = mm(gen[:, t * E:(t + 1) * E], xnT[:, b % 2, c, t * P:(t + 1) * P], wqkv[:, c, 2 * E:3 * E], start=(c == 0), stop=(c == 1))
                last.then_inc(full["gen"], 1)

            def s_unit(b, key):
                _, t, u = key
                claim("unit", (key, b))
                n = P * (t + 1)
                for j in range(1024 // n):
                    h = 1024 // n * u + j
                    area = unit_at((key, b))[:, j * n:(j + 1) * n]
                    mm(area, qst[0:KT, b % 2, h, t * P:(t + 1) * P], kst[0:KT, b % 2, h, 0:n], start=True, stop=False)
                    last = mm(area[:, n - P:n], identb[:, :], masks, start=False, stop=True)
                last.then_inc(full["unit"], 1)

            def t_unit(b, key):
                _, kt, u = key
                claim("unit", (key, b))
                w = S - kt * P
                for j in range(1024 // w):
                    h = 1024 // w * u + j
                    area = unit_at((key, b))[:, j * w:(j + 1) * w]
                    mm(area, kst[0:KT, b % 2, h, kt * P:(kt + 1) * P], qst[0:KT, b % 2, h, kt * P:S], start=True, stop=False)
                    last = mm(area, sel[:, h, :], nmT[:, kt * P:S], start=False, stop=True)
                last.then_inc(full["unit"], 1)

            def pv(b, hg):
                key0, key1 = ("T", 0, hg), ("T", 1, hg // 2)
                order = T_UNITS
                pe.wait_ge(prob_ready, 6 * b + max(order.index(key0), order.index(key1)) + 1)
                if hg % 2 == 0:
                    claim("out", (hg // 2, b))
                c0 = (hg % 2) * S
                for j in range(4):
                    mm(outp[32 * j:32 * j + 32, c0:c0 + S], vaug[:, b % 3, 0, 4 * hg + j, :],
                       probs_at(key0)[:, j * S:(j + 1) * S], start=True, stop=False, tile_position=(0, 32 * j))
                for j in range(4):
                    k = (4 * hg + j) % 8
                    last = mm(outp[32 * j:32 * j + 32, c0 + P:c0 + S], vaug[:, b % 3, 1, 4 * hg + j, :],
                              probs_at(key1)[:, k * P:(k + 1) * P], start=False, stop=True, tile_position=(0, 32 * j))
                if hg % 2 == 1:
                    last.then_inc(full["out"], 1)

            def stage_m(b):
                if b >= 1:
                    claim("gen", ("mT", b - 1))
                    pe.wait_ge(shift_ready, b)
                    for t in range(TPB):
                        last = nc.tensor.transpose(genb[:, t * P:(t + 1) * P], nmp[:, t, :], identb[:, :])
                    last.then_inc(full["gen"], 1)
                    emptied(pe, "gen", ("mT", b - 1))
                else:
                    pe.wait_ge(const_ready, 1)
                if b < B:
                    pe.wait_ge(stack_in[b], 16 * 2 * len(TERMS_Q))
                for n in range(6):
                    if b >= 1:
                        t_unit(b - 1, T_UNITS[n])
                    if b < B:
                        s_unit(b, S_UNITS[n])
                    if b >= 1 and n >= 3:
                        pv(b - 1, n - 3)
                if b >= 1:
                    pv(b - 1, 3)

            def stage_d1(b):
                claim("gen", ("aT", b))
                pe.wait_ge(adj_row, b + 1)
                for i in range(TPB):
                    for j in range(TPB):
                        last = nc.tensor.transpose(gen[:, i * S + j * P:i * S + (j + 1) * P], adj[:, TPB * b + j, i * P:(i + 1) * P], identf[:, :])
                last.then_inc(full["gen"], 1)
                claim("proj", ("otok", b))
                emptied(pe, "out", (1, b))
                for t in range(TPB):
                    for hg in range(4):
                        last = nc.tensor.transpose(proj[:, (4 * t + hg) * P:(4 * t + hg + 1) * P], oT[:, hg, t * P:(t + 1) * P], identf[:, :])
                last.then_inc(full["proj"], 1)
                claim("gen", ("onT", b))
                emptied(pe, "proj", ("otok", b))
                for c in range(2):
                    for t in range(TPB):
                        last = nc.tensor.transpose(gen[:, (2 * c + t) * P:(2 * c + t + 1) * P], otok[:, t, c * P:(c + 1) * P], identf[:, :])
                last.then_inc(full["gen"], 1)
                emptied(pe, "gen", ("onT", b))
                pe.wait_ge(wo_in, 16)
                for t in range(TPB):
                    for c in range(2):
                        last = mm(gen[:, t * E:(t + 1) * E], onT[:, c, t * P:(t + 1) * P], wo[:, c, :], start=(c == 0), stop=(c == 1))
                last.then_inc(full["gen"], 1)

            def stage_d3(b):
                claim("gen", ("x3T", b))
                pe.wait_ge(x3_ready, b + 1)
                for c in range(2):
                    for t in range(TPB):
                        last = nc.tensor.transpose(gen[:, (2 * c + t) * P:(2 * c + t + 1) * P], x3[:, TPB * b + t, c * P:(c + 1) * P], identf[:, :])
                last.then_inc(full["gen"], 1)
                emptied(pe, "gen", ("x3T", b))
                pe.wait_ge(moe_in, 64)
                for t in range(TPB):
                    for c in range(2):
                        g = TPB * b + t
                        last = mm(gen[:, t * NE:(t + 1) * NE], x3T[:, c, g * P:(g + 1) * P], gatew[:, c, :], start=(c == 0), stop=(c == 1))
                last.then_inc(full["gen"], 1)

            def shared_in():
                for n in range(2):
                    claim("unit", ("sg", n))
                    for g in range(2):
                        for c in range(2):
                            last = mm(unit_at(("sg", n))[0:FF, g * 512:(g + 1) * 512], wsgu[:, c, g * FF:(g + 1) * FF], x3T[:, c, n * 512:(n + 1) * 512], start=(c == 0), stop=(c == 1))
                    last.then_inc(full["unit"], 1)

            def shared_out():
                for n in range(2):
                    claim("unit", ("sd", n))
                    pe.wait_ge(sh_hid, n + 1)
                    for j in range(4):
                        t = 4 * n + j
                        last = mm(unit_at(("sd", n))[:, j * E:(j + 1) * E], hsh[0:FF, t * P:(t + 1) * P], wsdn[:, :], start=True, stop=True)
                    last.then_inc(full["unit"], 1)

            def positions():
                claim("gen", "pos")
                pe.wait_ge(sel_ready, 1)
                pe.wait_ge(order_ready, 1)
                sf = selb.rearrange("p t e -> p (t e)")
                mm(gen[:, :], tri[:, :], sf[:, (NT - 1) * NE:], start=True, stop=False)
                for j in range(1, NT):
                    last = mm(gen[:, :], ones[:, :], sf[:, (NT - 1 - j) * NE:(2 * NT - 1 - j) * NE], start=False, stop=(j == NT - 1))
                last.then_inc(full["gen"], 1)

            def slot_map(g):
                pe.wait_ge(hot_ready, g + 1)
                if g == 0:
                    pe.wait_ge(vals_ready, 1)
                    emptied(pe, "gen", "pos")
                else:
                    pe.wait_ge(info_free, g)
                for q in range(PPG):
                    e = EPG * g + 2 * q
                    for t in range(NT):
                        last = mm(gen[:, q * 16:(q + 1) * 16], hotbuf[:, g % 2, 2 * q:2 * q + 2, :, t].rearrange("p a b -> p (a b)"),
                                  vals[:, t, e:e + 2, :].rearrange("p a b -> p (a b)"), start=(t == 0), stop=(t == NT - 1))
                last.then_inc(info_full, 1)

            def tokens_in(p):
                pe.wait_ge(gathered[p % NX], 16 * (p // NX + 1))
                if p >= 2:
                    pe.wait_ge(xt_free, p - 1)
                for c in range(2):
                    last = nc.tensor.transpose(unit[:, 0, (p % 2) * 512 + c * P:(p % 2) * 512 + (c + 1) * P], xg[:, p % NX, c * P:(c + 1) * P], identf[:, :])
                last.then_inc(xt_full, 1)

            def gate_up(p):
                pe.wait_ge(xt_free, p + 1)
                pe.wait_ge(ring_in[p % RP], 32 * (p // RP + 1))
                if p >= 2:
                    pe.wait_ge(hid_ready, p - 1)
                for c in range(2):
                    for e in range(2):
                        last = mm(unit[CP * e:CP * e + CP, 1, (p % 2) * 512:(p % 2) * 512 + 2 * FF], xgT[:, p % 2, c, CP * e:CP * (e + 1)],
                                  ring[:, p % RP, e, c].rearrange("p g f -> p (g f)"), start=(c == 0), stop=(c == 1), tile_position=(0, CP * e))
                last.then_inc(gu_full, 1)

            def hidden(p):
                pe.wait_ge(hid_ready, p + 1)
                if p >= 1:
                    pe.wait_ge(ht_free, p)
                nc.tensor.transpose(outp[0:FF, 0:P], hid[:, p % 2, :], identf[:, :]).then_inc(ht_full, 1)

            def down(p):
                pe.wait_ge(ht_free, p + 1)
                if p >= 2:
                    pe.wait_ge(y_free, p - 1)
                for e in range(2):
                    last = mm(proj[CP * e:CP * e + CP, (p % 2) * 512:(p % 2) * 512 + E], hidT[:, p % 2, CP * e:CP * (e + 1)],
                              ring_dn[:, p % RP, e, :], start=True, stop=True, tile_position=(0, CP * e))
                last.then_inc(y_full, 1)

            run = {"X0": lambda b: context_projection(0), "X1": lambda b: context_projection(1), "X2": lambda b: similarity(),
                   "A1": stage_a, "M": stage_m, "D1": stage_d1, "D3": stage_d3}
            for stage, b in STAGES:
                if stage in run:
                    run[stage](b)
            shared_in()
            positions()
            shared_out()
            slot_map(0)
            slot_map(1)
            emptied(pe, "unit", ("sd", 0))
            emptied(pe, "unit", ("sd", 1))
            for p in range(NP + 3):
                if p < NP:
                    tokens_in(p)
                if 0 <= p - 1 < NP:
                    gate_up(p - 1)
                if 0 <= p - 3 < NP:
                    down(p - 3)
                if 0 <= p - 2 < NP:
                    hidden(p - 2)
                if p % PPG == 0 and p // PPG + 2 < NSM:
                    slot_map(p // PPG + 2)

        @block.scalar
        def _(sc):
            steps = [0]
            act_fn = nc.scalar.activation

            def link(ins):
                steps[0] += 1
                ins.then_inc(act_step, 1)
                sc.wait_ge(act_step, steps[0])

            def copy_ctx(name, dst):
                filled(sc, "proj", (name, 0))
                nc.scalar.copy(dst, proj[:, :]).then_inc(free["proj"], 1)

            def similarity():
                sc.wait_ge(gamma_in, 16)
                act_fn(gam[:, 1:2], gam[:, 0:1], ACT.Sigmoid).then_inc(gamma_sig, 1)
                for u in range(2):
                    filled(sc, "unit", ("sim", u))
                    nc.scalar.copy(simS[:, 4 * u:4 * u + 4, :].rearrange("p t s -> p (t s)"), unit[:, u, :]).then_inc(sim_ready, 1)
                    act_fn(adj[:, 4 * u:4 * u + 4, :].rearrange("p t s -> p (t s)"), unit[:, u, :], ACT.Sigmoid,
                           scale=1.0 / (HC * (DC // HC) ** 0.5)).then_inc(free["unit"][u], 1)

            def stage_a1(b):
                filled(sc, "gen", ("xnT", b))
                nc.scalar.copy(xnT[:, b % 2].rearrange("p c s -> p (c s)"), gen[:, :]).then_inc(free["gen"], 1)
                filled(sc, "gen", ("v", b))
                if b == 0:
                    sc.wait_ge(pads_ready, 1)
                if b >= 3:
                    filled(sc, "out", (1, b - 3))
                nc.scalar.copy(vaug[:, b % 3, :, :, 0:D], gen[:, :].rearrange("p (t h d) -> p t h d", t=TPB, h=H)).then_inc(free["gen"], 1)

            def stage_a2(b):
                sc.wait_ge(roped, b + 1)
                if b >= 1:
                    sc.wait_ge(parts_out[b - 1], 48)
                nc.scalar.copy(parts[:, 0], qkc).then_inc(part0, 1)
                sc.wait_ge(rest_ready, b + 1)
                nc.scalar.copy(parts[:, 1], qkc).then_inc(part1, 1)

            def head_outputs(b, half):
                filled(sc, "out", (half, b))
                if b >= 1:
                    filled(sc, "proj", ("otok", b - 1))
                nc.scalar.copy(oT[:, 2 * half:2 * half + 2, :].rearrange("p g s -> p (g s)"), outp[:, :]).then_inc(free["out"], 1)

            def stage_m(b):
                if b == 0:
                    return
                b = b - 1
                for n, key in enumerate(T_UNITS):
                    filled(sc, "unit", (key, b))
                    if b == 0 and n == 0:
                        filled(sc, "unit", ("sim", 1))
                    if b >= 1 and n == 0:
                        filled(sc, "out", (1, b - 1))
                    act_fn(prob[:, n, :], unit_at((key, b)), ACT.Exp, scale=D ** -0.5).then_inc(unit_free((key, b)), 1)
                head_outputs(b, 0)
                head_outputs(b, 1)

            def stage_d1(b):
                filled(sc, "gen", ("onT", b))
                nc.scalar.copy(onT.rearrange("p c s -> p (c s)"), gen[:, :]).then_inc(free["gen"], 1)

            def stage_d3(b):
                filled(sc, "gen", ("x3T", b))
                nc.scalar.copy(x3T[:, :, b * S:(b + 1) * S], gen[:, :].rearrange("p (c s) -> p c s", c=2)).then_inc(free["gen"], 1)
                filled(sc, "gen", ("lg", b))
                nc.scalar.copy(logit[:, TPB * b:TPB * b + TPB, :], gen[:, 0:TPB * NE].rearrange("p (t e) -> p t e", t=TPB)).then_inc(free["gen"], 1)

            run = {"X0": lambda b: copy_ctx("QT", cq), "X1": lambda b: copy_ctx("KT", ck), "X2": lambda b: similarity(),
                   "A1": stage_a1, "A2": stage_a2, "M": stage_m, "D1": stage_d1, "D3": stage_d3}
            for stage, b in STAGES:
                if stage in run:
                    run[stage](b)
            emptied(sc, "gen", ("lg", B - 1))
            act_fn(score, logit[:, :, :], ACT.Sigmoid).then_inc(score_ready, 1)
            for n in range(2):
                filled(sc, "unit", ("sg", n))
                act_fn(ssh[0:FF, n * 512:(n + 1) * 512], unit_at(("sg", n))[0:FF, 0:512], ACT.Silu).then_inc(sh_act, 1)
            for p in range(NP + 3):
                if 0 <= p - 1 < NP:
                    q = p - 1
                    sc.wait_ge(gu_full, q + 1)
                    if q >= 2:
                        sc.wait_ge(hid_ready, q - 1)
                    act_fn(act[:, q % 2, :], unit[:, 1, (q % 2) * 512:(q % 2) * 512 + FF], ACT.Silu).then_inc(act_ready, 1)
                if 0 <= p - 3 < NP:
                    q = p - 3
                    sc.wait_ge(y_full, q + 1)
                    if q >= NX:
                        sc.wait_ge(scattered[q % NX], 16 * (q // NX))
                    act_fn(yrow[:, q % NX, :], proj[:, (q % 2) * 512:(q % 2) * 512 + E], ACT.Copy, scale=wslot[:, q:q + 1]).then_inc(y_free, 1)

        @block.gpsimd
        def _(gp):
            steps = [0]

            def link(ins):
                steps[0] += 1
                ins.then_inc(pool_step, 1)
                gp.wait_ge(pool_step, steps[0])

            pool = nc.gpsimd
            link(pool.memset(cexp[:, 0:1], -0.5))
            link(pool.memset(identf[:, :], 0.0))
            pool.affine_select(out=identf[:, :], in_=identf[:, :], compare_op=ALU.not_equal, fill=1.0,
                               base=0, pattern=[[-1, P]], channel_multiplier=1).then_inc(ident_ready, 1)
            gp.wait_ge(ident_ready, 1)

            def inverse_root(kind, b):
                gp.wait_ge(var_ready, NORMS.index((kind, b)) + 1)
                k = int(kind[2]) - 1
                link(pool.tensor_scalar(srs[:, :], mv[:, k, :, 1], EPS, None, ALU.add))
                end = pool.tensor_tensor(rstd[:, k, :], srs[:, :], cexp[:, 0:1].broadcast_to((P, TPB)), ALU.pow)
                if kind == "ln2":
                    link(end)
                    end = pool.tensor_scalar(rstd[:, k, :], rstd[:, k, :], gam[:, 2:3], None, ALU.mult)
                end.then_inc(rstd_ready, 1)

            def constants():
                link(pool.tensor_copy(identb[:, :], identf[:, :]))
                link(pool.memset(masks, 0.0))
                link(pool.affine_select(out=masks, in_=masks, compare_op=ALU.is_ge, fill=NEG, base=0,
                                        pattern=[[-1, P]], channel_multiplier=1))
                link(pool.memset(nmp, 0.0))
                link(pool.memset(sel, 0.0))
                for j in range(3):
                    end = pool.affine_select(out=sel, in_=sel, compare_op=ALU.not_equal, fill=1.0, base=-16 * j,
                                             pattern=[[-1, H], [0, P]], channel_multiplier=1)
                    if j < 2:
                        link(end)
                end.then_inc(const_ready, 1)
                gp.wait_ge(gamma_sig, 1)
                link(pool.tensor_scalar(gam[:, 2:3], gam[:, 1:2], -1.0, 1.0, ALU.mult, ALU.add))
                link(pool.tensor_scalar(gam[:, 3:4], gam[:, 1:2], 0.5, None, ALU.mult))
                for u in range(2):
                    emptied(gp, "unit", ("sim", u))
                    half = adj[:, 4 * u:4 * u + 4, :].rearrange("p t s -> p (t s)")
                    pool.tensor_scalar(half, half, gam[:, 3:4], None, ALU.mult).then_inc(adj_half, 1)
                pool.memset(zero[:, :], 0.0).then_inc(zero_ready, 1)

            def moe_constants():
                link(pool.memset(tri[:, :], 1.0))
                link(pool.affine_select(out=tri[:, :], in_=tri[:, :], compare_op=ALU.is_ge, fill=0.0, base=-1,
                                        pattern=[[1, P]], channel_multiplier=-1))
                link(pool.memset(ones[:, :], 1.0))
                link(pool.iota(iotac[:, :, :], pattern=[[1, CAP], [0, NT]], base=0, channel_multiplier=0, allow_small_or_imprecise_dtypes=True))
                link(pool.memset(keep[:, :, :], 1.0))
                link(pool.memset(keep[:, :, 0:1], 0.0))
                pool.memset(ring_dn[FF:P].rearrange("p a e n -> p (a e n)"), 0.0).then_inc(order_ready, 1)
                gp.wait_ge(order_ready, 1)

            def stage_a2(b):
                gp.wait_ge(shuffled, b + 1)
                gp.wait_ge(rope_in, 32)
                pool.tensor_tensor(qks, qks, sinb.unsqueeze(1).broadcast_to((P, 4, S)), ALU.mult).then_inc(sin_done, 1)
                if b >= 1:
                    gp.wait_ge(part0, b + 1)
                    pool.tensor_tensor(qkc, qkc, parts[:, 0], ALU.subtract).then_inc(rest_ready, 1)
                gp.wait_ge(part1, b + 1)
                pool.tensor_tensor(parts[:, 2], qkc, parts[:, 1], ALU.subtract).then_inc(part2, 1)
                if b == 0:
                    constants()
                if b == 2:
                    moe_constants()

            def stage_m(b):
                if b == 0:
                    return
                for n, key in enumerate(T_UNITS):
                    emptied(gp, "unit", (key, b - 1))
                    w = S - key[1] * P
                    v = prob[:, n, :].rearrange("p (h q) -> p h q", q=w)[:, :, 0:P]
                    pool.affine_select(out=v, in_=v, compare_op=ALU.is_ge, fill=0.0, base=0,
                                       pattern=[[0, 1024 // w], [1, P]], channel_multiplier=-1).then_inc(prob_ready, 1)

            run = {"A1": lambda b: inverse_root("ln1", b), "A2": stage_a2, "M": stage_m,
                   "D1": lambda b: inverse_root("ln2", b), "D2": lambda b: inverse_root("ln3", b)}
            for stage, b in STAGES:
                if stage in run:
                    run[stage](b)

            gp.wait_ge(x3_ready, B)
            emptied(gp, "gen", ("onT", B - 1))
            filled(gp, "gen", ("att", B - 1))
            link(pool.memset(gsum, NEG))
            pool.memset(selb[:, 0:NT - 1, :], 0.0).then_inc(pick_ready, 1)
            gp.wait_ge(pick_ready, 1)
            link(pool.memset(vals.rearrange("p t e v -> p (t e v)"), 1.0))
            link(pool.iota(vals[:, :, :, 0], pattern=[[0, NT], [0, NE]], base=0,
                           channel_multiplier=1, allow_small_or_imprecise_dtypes=True))
            pool.iota(vals[:, :, :, 1], pattern=[[P, NT], [0, NE]], base=0,
                      channel_multiplier=0, allow_small_or_imprecise_dtypes=True).then_inc(vals_init, 1)
            gp.wait_ge(vals_init, 1)
            link(pool.memset(hidT, 0.0))
            pool.memset(hotbuf[:, :, :, CAP:CP, :].rearrange("p a e c t -> p (a e) (c t)"), 0.0).then_inc(vals_init, 1)

            def gather(p):
                gp.wait_ge(index_ready, p // PPG + 1)
                if p >= NX:
                    gp.wait_ge(xt_full, p - NX + 1)
                pool.indirect_dma_start(out=xg[:, p % NX, :], out_offset=None, in_=x3_dram,
                                        in_offset=bass.IndirectOffsetOnAxis(ap=toki[:, p:p + 1], axis=0)).then_inc(gathered[p % NX], 16)

            def scatter(p):
                gp.wait_ge(y_free, p + 1)
                pool.indirect_dma_start(out=z_dram, out_offset=bass.IndirectOffsetOnAxis(ap=rowi[:, p:p + 1], axis=0),
                                        in_=yrow[:, p % NX, :], in_offset=None, bounds_check=T * 8 - 1,
                                        oob_is_err=False).then_inc(scattered[p % NX], 16)

            gp.wait_ge(x3_out, 16 * B)
            gp.wait_ge(z_zeroed, 16 * NT)
            lag = NX - 1
            for p in range(NP + lag):
                if p < NP:
                    gather(p)
                if p >= lag:
                    scatter(p - lag)

        @block.vector
        def _(ve):
            steps = [0]
            v = nc.vector

            def mark(ins):
                steps[0] += 1
                ins.then_inc(dve_step, 1)
                return steps[0]

            def need(n):
                ve.wait_ge(dve_step, n)

            def link(ins):
                need(mark(ins))

            def adjacency():
                rounds = (TOPA - 1) // 8
                col = (TOPA - 1) % 8
                for t in range(0, NT, 2):
                    ve.wait_ge(sim_ready, t // 4 + 1)
                    last = [0, 0]
                    for r in range(rounds + 1):
                        for i in range(2):
                            if last[i]:
                                need(last[i])
                            last[i] = mark(v.max(best[:, i, :], simS[:, t + i, :] if r == 0 else work[:, i, :]))
                            yield t
                        for i in range(2):
                            if r < rounds:
                                need(last[i])
                                last[i] = mark(v.match_replace(work[:, i, :], best[:, i, :], simS[:, t + i, :] if r == 0 else work[:, i, :], NEG))
                                yield t
                    ve.wait_ge(adj_half, t // 4 + 1)
                    for i in range(2):
                        need(last[i])
                        ins = v.scalar_tensor_tensor(adj[:, t + i, :], simS[:, t + i, :], best[:, i, col:col + 1], adj[:, t + i, :], ALU.is_ge, ALU.mult)
                        if i == 0:
                            end = mark(ins)
                    ins.then_inc(adj_row, 1)
                    need(end)
                    ve.wait_ge(adj_row, t // TPB + 1)
                    yield t + 2
                while True:
                    yield NT

            filler = adjacency()
            at_tile = [0]

            def fill(n):
                for _ in range(n):
                    at_tile[0] = max(at_tile[0], next(filler))

            def stats(kind, b, src):
                k = int(kind[2]) - 1
                if NORMS.index((kind, b)):
                    ve.wait_ge(var_ready, NORMS.index((kind, b)))
                ends = [mark(v.bn_stats(st6[:, t, :], src[:, t, :])) for t in range(TPB)]
                for t in range(TPB):
                    need(ends[t])
                    ins = v.bn_aggr(mv[:, k, t, :], st6[:, t, :])
                ins.then_inc(var_ready, 1)

            def normalise(dst, src, kind, b):
                k = int(kind[2]) - 1
                ve.wait_ge(rstd_ready, NORMS.index((kind, b)) + 1)
                for t in range(TPB):
                    ins = v.tensor_scalar(dst[:, t, :], src[:, t, :], mv[:, k, t, 0:1], rstd[:, k, t:t + 1], ALU.subtract, ALU.mult)
                return ins

            def pads():
                v.memset(ctxs[DC:P, :], 0.0)
                v.memset(wx[DC:P, :, :], 0.0)
                v.memset(wx[0:DC, :, DC:P], 0.0)
                link(v.memset(vaug.rearrange("p a t h d -> p (a t h d)"), 0.0))
                v.memset(vaug[:, :, :, :, D:D + 1].rearrange("p a t h o -> p (a t h) o"), 1.0).then_inc(pads_ready, 1)

            def stage_a1(b):
                ve.wait_ge(x_in[b], 16)
                src = res[:, TPB * b:TPB * b + TPB, :]
                stats("ln1", b, src)
                if b >= 1:
                    fill(3)
                if b >= 2:
                    filled(ve, "gen", ("xnT", b - 2))
                normalise(xn[:, b % 2], src, "ln1", b).then_inc(xn_ready, 1)
                if b >= 1:
                    fill(FILL_PROJ)

            def stage_a2(b):
                filled(ve, "proj", ("qk", b))
                ve.wait_ge(rope_in, 32)
                if b >= 1:
                    ve.wait_ge(part2, b)
                pv = proj[:, :].rearrange("p (m s) -> p m s", m=4)
                v.stream_shuffle(qks.rearrange("p m s -> p (m s)"), proj[:, :], [i ^ 1 for i in range(32)]).then_inc(shuffled, 1)
                v.tensor_tensor(qkc, pv, cosb.unsqueeze(1).broadcast_to((P, 4, S)), ALU.mult).then_inc(free["proj"], 1)
                if b >= 1:
                    fill(FILL_SIN)
                ve.wait_ge(sin_done, b + 1)
                emptied(ve, "proj", ("qk", b))
                v.tensor_tensor(qkc, qkc, qks, ALU.add).then_inc(roped, 1)
                if b == 0:
                    ve.wait_ge(part0, 1)
                    v.tensor_tensor(qkc, qkc, parts[:, 0], ALU.subtract).then_inc(rest_ready, 1)

            def stage_m(b):
                if b >= 1:
                    filled(ve, "gen", ("mT", b - 1))
                    if b >= 2:
                        filled(ve, "unit", (T_UNITS[-1], b - 2))
                    v.tensor_copy(nmT, genb[:, 0:S]).then_inc(free["gen"], 1)
                if b == B:
                    return
                for key in S_UNITS:
                    _, t, u = key
                    n = P * (t + 1)
                    c = 1024 // n
                    fill(FILL_MAX)
                    filled(ve, "unit", (key, b))
                    v.tensor_reduce(nmax[:, t, c * u:c * u + c], unit_at((key, b)).rearrange("p (h k) -> p h k", k=n), axis=AX,
                                    op=ALU.max, negate=True).then_inc(unit_free((key, b)), 1)
                emptied(ve, "unit", (S_UNITS[-1], b))
                emptied(ve, "unit", (S_UNITS[-2], b))
                if b >= 1:
                    filled(ve, "gen", ("mT", b - 1))
                link(v.tensor_copy(nmp[:, :, 0:H], nmax))
                link(v.tensor_tensor(nmr, nmax, nmp[:, :, 0:H], ALU.subtract))
                link(v.tensor_copy(nmp[:, :, H:2 * H], nmr))
                v.tensor_tensor(nmp[:, :, 2 * H:3 * H], nmr, nmp[:, :, H:2 * H], ALU.subtract).then_inc(shift_ready, 1)

            def stage_d1(b):
                while at_tile[0] < TPB * (b + 1):
                    fill(1)
                rows = res[:, TPB * b:TPB * b + TPB, :]
                a = adj[:, TPB * b:TPB * b + TPB, :]
                filled(ve, "gen", ("aT", b))
                v.tensor_tensor(a, a, gen[:, :].rearrange("p (t e) -> p t e", t=TPB), ALU.add).then_inc(free["gen"], 1)
                fill(FILL_D)
                filled(ve, "proj", ("otok", b))
                ov = proj[:, :].rearrange("p (t h d) -> p t h d", t=TPB, d=32)
                link(v.reciprocal(rec, ov[:, :, :, D]))
                if b >= 1:
                    filled(ve, "gen", ("onT", b - 1))
                v.tensor_tensor(otok.rearrange("p t (h d) -> p t h d", d=D), ov[:, :, :, 0:D],
                                rec.unsqueeze(3).broadcast_to((P, TPB, H, D)), ALU.mult).then_inc(free["proj"], 1)
                fill(FILL_D + 4)
                filled(ve, "gen", ("att", b))
                v.tensor_tensor(rows, rows, gen[:, :].rearrange("p (t e) -> p t e", t=TPB), ALU.add).then_inc(free["gen"], 1)
                emptied(ve, "gen", ("att", b))
                stats("ln2", b, rows)

            def stage_d2(b):
                rows = res[:, TPB * b:TPB * b + TPB, :]
                a = adj[:, TPB * b:TPB * b + TPB, :]
                fill(FILL_D)
                link(normalise(mix, rows, "ln2", b))
                link(v.tensor_tensor(mix, mix, a, ALU.add))
                link(v.tensor_tensor(rows, rows, mix, ALU.add))
                stats("ln3", b, rows)

            def stage_d3(b):
                fill(FILL_D)
                normalise(x3[:, TPB * b:TPB * b + TPB, :], res[:, TPB * b:TPB * b + TPB, :], "ln3", b).then_inc(x3_ready, 1)

            def top2(hi, lo, hs, ls, ta, tb, n):
                link(v.tensor_tensor(hi, hs[:, :, 0:n], hs[:, :, n:2 * n], ALU.max))
                link(v.tensor_tensor(ta, hs[:, :, 0:n], hs[:, :, n:2 * n], ALU.min))
                link(v.tensor_tensor(tb, ls[:, :, 0:n], ls[:, :, n:2 * n], ALU.max))
                link(v.tensor_tensor(lo, ta, tb, ALU.max))

            def route():
                ve.wait_ge(pick_ready, 1)
                ve.wait_ge(score_ready, 1)
                link(v.tensor_tensor(sbias, score, biasb[:, :].unsqueeze(1).broadcast_to((P, NT, NE)), ALU.add))
                g8 = sbias.rearrange("p t (g j) -> p (t g) j", j=NE // NG)
                link(v.tensor_tensor(hi1, g8[:, :, 0:4], g8[:, :, 4:8], ALU.max))
                link(v.tensor_tensor(lo1, g8[:, :, 0:4], g8[:, :, 4:8], ALU.min))
                top2(hi2, lo2, hi1, lo1, ta2, tb2, 2)
                top2(hi3, lo3, hi2, lo2, ta3, tb3, 1)
                tg = lambda a: a.rearrange("p (t g) o -> p t (g o)", t=NT)
                link(v.tensor_tensor(gsum[:, :, 0:NG], tg(hi3), tg(lo3), ALU.add))
                for t in range(NT):
                    ins = v.max(gtop[:, t, :], gsum[:, t, 0:NG])
                link(ins)
                v.memset(gpick, NEG)
                link(v.memset(epick, 3 * NEG))
                link(v.tensor_copy(gpick[:, :, 0:KG], gtop[:, :, 0:KG]))
                for t in range(NT):
                    ins = v.match_replace(gout[:, t, :], gpick[:, t, :], gsum[:, t, :], -NEG)
                link(ins)
                link(v.tensor_scalar(gpen, gout[:, :, 0:NG], -NEG / 10, 1.0, ALU.is_ge, ALU.subtract))
                link(v.tensor_scalar(gpen, gpen, -NEG, None, ALU.mult))
                link(v.memset(cand, 3 * NEG))
                link(v.tensor_tensor(cand[:, :, 0:NE].rearrange("p t (g j) -> p t g j", g=NG),
                                     sbias.rearrange("p t (g j) -> p t g j", g=NG),
                                     gpen.unsqueeze(3).broadcast_to((P, NT, NG, NE // NG)), ALU.add))
                for t in range(NT):
                    ins = v.max(etop[:, t, :], cand[:, t, 0:NE])
                link(ins)
                link(v.tensor_copy(epick[:, :, 0:KE], etop[:, :, 0:KE]))
                for t in range(NT):
                    ins = v.match_replace(eout[:, t, :], epick[:, t, :], cand[:, t, :], -NEG)
                link(ins)
                v.tensor_scalar(selb[:, NT - 1:, :], eout[:, :, 0:NE], -NEG / 10, None, ALU.is_ge).then_inc(sel_ready, 1)
                link(v.tensor_scalar(selm, eout[:, :, 0:NE], -NEG / 10, None, ALU.is_ge))
                link(v.tensor_tensor(wsel, score, selm, ALU.mult))
                link(v.reduce_sum(wsum, wsel, axis=AX))
                link(v.reciprocal(wsum, wsum))
                link(v.tensor_scalar(wsum, wsum, SCALE, None, ALU.mult))
                link(v.tensor_tensor(wsel, wsel, wsum.unsqueeze(2).broadcast_to((P, NT, NE)), ALU.mult))
                ve.wait_ge(vals_init, 1)
                link(v.tensor_copy(vals[:, :, :, 3], wsel))
                link(v.tensor_tensor(wsel, wsel, vals[:, :, :, 3], ALU.subtract))
                link(v.tensor_copy(vals[:, :, :, 4], wsel))
                link(v.tensor_tensor(vals[:, :, :, 5], wsel, vals[:, :, :, 4], ALU.subtract))
                fl = lambda a: a.rearrange("p t e -> p (t e)")
                link(v.tensor_tensor_scan(fl(rank), fl(keep[:, :, :]), fl(selm), 0.0, ALU.mult, ALU.add))
                v.tensor_scalar(vals[:, :, :, 2], rank, -1.0, None, ALU.add).then_inc(vals_ready, 1)
                ve.wait_ge(vals_ready, 1)
                link(v.tensor_scalar(selm, selm, -float(T), float(T), ALU.mult, ALU.add))
                filled(ve, "gen", "pos")
                n = nth("gen", "pos")
                v.tensor_tensor(slot, gen[:, :].rearrange("p (t e) -> p e t", t=NT), selm.rearrange("p t e -> p e t"), ALU.add).then_inc(free["gen"], 1)
                ve.wait_ge(free["gen"], n + 1)
                ve.wait_ge(vals_init, 2)

            def shared():
                for n in range(2):
                    ve.wait_ge(sh_act, n + 1)
                    u = unit_at(("sg", n))
                    cols = slice(n * 512, (n + 1) * 512)
                    v.tensor_tensor(hsh[0:FF, cols], ssh[0:FF, cols], u[0:FF, 512:1024], ALU.mult).then_inc(unit_free(("sg", n)), 1)
                    emptied(ve, "unit", ("sg", n))
                    v.memset(st6[:, 0, 0:1], 0.0).then_inc(sh_hid, 1)

            def shared_add():
                for n in range(2):
                    filled(ve, "unit", ("sd", n))
                    r = res[:, 4 * n:4 * n + 4, :].rearrange("p t e -> p (t e)")
                    v.tensor_tensor(r, r, unit_at(("sd", n)), ALU.add).then_inc(unit_free(("sd", n)), 1)

            def one_hot(g):
                if g >= 2:
                    ve.wait_ge(info_full, g - 1)
                v.tensor_tensor(hotbuf[:, g % 2, :, 0:CAP, :], slot[:, EPG * g:EPG * (g + 1), :].unsqueeze(2).broadcast_to((P, EPG, CAP, NT)),
                                iotac[:, :, :].unsqueeze(1).broadcast_to((P, EPG, CAP, NT)), ALU.is_equal).then_inc(hot_ready, 1)

            def indices(g):
                ve.wait_ge(info_full, g + 1)
                o = g % 2
                gv = gen[:, 0:PPG * 16].rearrange("p (q e v) -> p q e v", q=PPG, e=2)
                v.tensor_copy(info[0:CP, o], gv[0:CP, :, 0, :])
                v.tensor_copy(info[CP:P, o], gv[CP:P, :, 1, :]).then_inc(info_free, 1)
                ve.wait_ge(info_free, g + 1)
                cols = slice(PPG * g, PPG * (g + 1))
                link(v.tensor_tensor(tokf[:, o], info[:, o, :, 0], info[:, o, :, 1], ALU.add))
                v.tensor_copy(toki[:, cols], tokf[:, o])
                link(v.tensor_scalar(tmpf[:, o], info[:, o, :, 6], -16.0 * T, 16.0 * T, ALU.mult, ALU.add))
                link(v.scalar_tensor_tensor(rowf[:, o], tokf[:, o], 8.0, info[:, o, :, 2], ALU.mult, ALU.add))
                link(v.tensor_tensor(rowf[:, o], rowf[:, o], tmpf[:, o], ALU.add))
                link(v.tensor_copy(rowi[:, cols], rowf[:, o]))
                link(v.tensor_tensor(tmpf[:, o], info[:, o, :, 3], info[:, o, :, 4], ALU.add))
                v.tensor_tensor(wslot[:, cols], tmpf[:, o], info[:, o, :, 5], ALU.add).then_inc(index_ready, 1)

            pads()
            run = {"A1": stage_a1, "A2": stage_a2, "M": stage_m, "D1": stage_d1, "D2": stage_d2, "D3": stage_d3}
            for stage, b in STAGES:
                if stage in run:
                    run[stage](b)
                if (stage, b) == ("X2", 0):
                    fill(FILL_START)
            shared()
            route()
            shared_add()
            one_hot(0)
            one_hot(1)
            indices(0)
            indices(1)
            for p in range(NP + 3):
                if p < NP:
                    ve.wait_ge(xt_full, p + 1)
                    if p >= 2:
                        ve.wait_ge(gu_full, p - 1)
                    v.tensor_copy(xgT[:, p % 2].rearrange("p c s -> p (c s)"), unit[:, 0, (p % 2) * 512:(p % 2) * 512 + E]).then_inc(xt_free, 1)
                if 0 <= p - 1 < NP:
                    q = p - 1
                    ve.wait_ge(act_ready, q + 1)
                    if q >= 2:
                        ve.wait_ge(ht_full, q - 1)
                    v.tensor_tensor(hid[:, q % 2, :], act[:, q % 2, :], unit[:, 1, (q % 2) * 512 + FF:(q % 2) * 512 + 2 * FF], ALU.mult).then_inc(hid_ready, 1)
                if 0 <= p - 2 < NP:
                    q = p - 2
                    ve.wait_ge(ht_full, q + 1)
                    if q >= 2:
                        ve.wait_ge(y_full, q - 1)
                    v.tensor_copy(hidT[0:FF, q % 2, :], outp[0:FF, 0:P]).then_inc(ht_free, 1)
                if p % PPG == 0 and p // PPG + 2 < NSM:
                    one_hot(p // PPG + 2)
                    indices(p // PPG + 2)
            for t in range(NT):
                ve.wait_ge(z_in[t % NZ], 16 * (t // NZ + 1))
                if t >= NZ:
                    ve.wait_ge(out_done[t % NZ], 16 * (t // NZ))
                link(v.reduce_sum(fin[:, t % NZ], zin[:, t % NZ].rearrange("p k e -> p e k"), axis=AX))
                v.tensor_tensor(fin[:, t % NZ], fin[:, t % NZ], res[:, t, :], ALU.add).then_inc(fin_ready, 1)


def rope_tables():
    inv = 1.0 / np.float32(10000.0) ** (np.arange(0, D, 2, dtype=np.float32) / np.float32(D))
    ang = np.outer(np.arange(S, dtype=np.float32), inv.astype(np.float32)).astype(np.float32)
    ang = np.concatenate([ang, ang], axis=-1).T
    sign = np.where(np.arange(D) % 2 == 0, -1.0, 1.0).astype(np.float32)[:, None]
    cos, sin = np.cos(ang).astype(np.float32), (np.sin(ang) * sign).astype(np.float32)
    return np.tile(cos, (P // D, 1)), np.tile(sin, (P // D, 1))


def kernel(x, ctx_512, L0_attn_Wqkv, L0_attn_Wout, L0_xattn_Wq, L0_xattn_Wk, L0_xattn_gamma_raw, L0_ffn_gate_w, L0_ffn_bias,
           L0_ffn_w_gate, L0_ffn_w_up, L0_ffn_w_down, L0_ffn_ws_gate, L0_ffn_ws_up, L0_ffn_ws_down):
    import numpy as _np
    import concourse.bacc as _bacc
    from concourse import mybir as _mybir
    from concourse.bass_utils import run_bass_kernel_spmd as _run

    a = _np.asarray
    cos, sin = rope_tables()
    gu = _np.stack([a(L0_ffn_w_gate), a(L0_ffn_w_up)], axis=2).reshape(NP, 2, 2, P, 2, FF)
    ins = {
        "x": a(x).reshape(T, E),
        "cosT": cos, "sinT": sin,
        "ctxT": a(ctx_512).reshape(T, DC).T,
        "wxT": _np.stack([a(L0_xattn_Wq).T, a(L0_xattn_Wk).T]),
        "wqkvT": a(L0_attn_Wqkv).T,
        "woT": a(L0_attn_Wout).T,
        "gamma": a(L0_xattn_gamma_raw).reshape(1, 1),
        "gate_w": a(L0_ffn_gate_w),
        "bias": a(L0_ffn_bias).reshape(1, NE),
        "w_gu": gu.transpose(0, 3, 1, 2, 4, 5).reshape(NP, P, 8 * FF),
        "w_dn": a(L0_ffn_w_down).reshape(NP, 2, FF, E).transpose(0, 2, 1, 3).reshape(NP, FF, 2 * E),
        "ws_gu": _np.concatenate([a(L0_ffn_ws_gate), a(L0_ffn_ws_up)], axis=1),
        "ws_dn": a(L0_ffn_ws_down),
    }
    nc = _bacc.Bacc("TRN2", target_bir_lowering=False, num_devices=1)
    arrays, args = {}, []
    for name, arr in ins.items():
        arr = _np.ascontiguousarray(arr)
        arrays[f"in_{name}"] = arr
        args.append(nc.dram_tensor(f"in_{name}", arr.shape, _mybir.dt.from_np(arr.dtype), kind="ExternalInput").ap())
    args.append(nc.dram_tensor("out_0", (T, E), _mybir.dt.float32, kind="ExternalOutput").ap())
    decoder_kernel(nc, *args)
    r = _run(nc, [arrays], core_ids=[0])
    return r.results[0]["out_0"].reshape(B, S, E)
```

```python
from contextlib import ExitStack

import numpy as np
import concourse.bass as bass
from concourse import mybir

F32 = mybir.dt.float32
BF16 = mybir.dt.bfloat16
I32 = mybir.dt.int32
ALU = mybir.AluOpType
ACT = mybir.ActivationFunctionType
AX = mybir.AxisListType.X

P = 128
B, S, E = 4, 256, 256
T = B * S
NT = T // P
TPB = S // P
H, D = 16, 16
DC = 64
HC = 4
TOPA = max(1, int(S * 0.3))
NE, KE, FF = 64, 6, 96
NG, KG = 8, 4
CAP = 2 * (2 * 128 * KE // NE)
CP = 64
SCALE = 2.5
NP = NE // 2
EPG = 8
PPG = EPG // 2
NSM = NE // EPG
ROUTED = NT - TPB
RA = 8
RP = 16
CPG = EPG * CAP // P
NC = NSM * CPG
NX = 12
NY = 8
LAG = 10
NZ = 4
PIECES = [(t, slice(0, E)) for t in range(NT - 1)] + [(NT - 1, slice(0, E // 2)), (NT - 1, slice(E // 2, E))]
HOTTED = {PPG * (g - 3): g for g in range(3, NSM)}
MAPPED = {0: 2, **{p + 2: g for p, g in HOTTED.items()}}
INDEXED = {1: 2, **{p + 3: g for p, g in HOTTED.items()}}
WARM = (5, 10, 0, 8)
EPS = 1e-5
NEG = -1e30
V_TOKEN8, V_FAR, V_RANK, V_TILE8, V_TOKEN, V_WEIGHT = range(6)
TERMS_Q = (0, 0, 0, 1, 1, 2)
TERMS_K = (0, 1, 2, 0, 1, 0)
KT = len(TERMS_Q) * D
HPC = P // D

STEPS = [(step[:-1] if step[0] not in "FG" else step[0], int(step[-1] if step[0] not in "FG" else step[1:])) for step in """
    A1a0 X00 A1b0 A1c0 A2a0 X10 A1d0 A1a1 A2b0 A1b1 A1c1 A2c0 A2d0 A2a1 X20 F4
    MT0 A2b1 F31 U00 U10 F7 A2c1 A2d1 A1a2 A1d1 U20 A1b2 F18 U30 A1c2 A1d2 A2a2 F6 U40 F3 U50 A2b2 A1a3 MS0 A2c2 A2d2
    MT1 A1b3 ME0 F13 U01 F11 U11 A1c3 A2a3 U21 A2b3 F12 A2c3 U31 A2d3 F2 U41 U51 MS1 F1
    MT2 ME1 U02 F6 A1d3 U12 D1b0 D1a0 D1c0 U22 D1d0 F5 D1e0 U32 D20 U42 U52 ME2 D3a0 MS2
    MT3 F8 U03 D1a1 U13 D1b1 D3b0 D1c1 U23 D1d1 U33 D1e1 U43 D1a2 D21 U53 MS3
    MT4 D3a1 ME3 F21 U04 D1b2 U14 D3b1 D1c2 U24 D1d2 F39 U34 D1e2 U44 U54 ME4 F14 D22 D1a3 D1b3 D3a2 D1c3 G21 D3b2 R0 V0
    D1d3 Sa0 D1e3 G9 D23 G4 D3a3 MS4 P0 G13 Sb0 D3b3 Sc0 G1
""".split()]

S_UNITS = [("S", 0, 0), ("S", 0, 1), ("S", 1, 0), ("S", 1, 1), ("S", 1, 2), ("S", 1, 3)]
T_UNITS = [("T", 1, 0), ("T", 0, 0), ("T", 0, 1), ("T", 1, 1), ("T", 0, 2), ("T", 0, 3)]

AREAS = {"gen": [], "proj": [], "unit": [], "out": []}
USES = {"A1b": ("gen", "xnT"), "A1d": ("gen", "v"), "D1a": ("gen", "aT"), "D1d": ("gen", "onT"), "D1e": ("gen", "att"),
        "D3a": ("gen", "x3T"), "D3b": ("gen", "lg"), "X0": ("proj", "QT"), "X1": ("proj", "KT"), "A1c": ("proj", "qk"), "D1b": ("proj", "otok"),
        "P": ("out", "pos")}
NORMS = []
for _st, _b in STEPS:
    if _st in USES:
        AREAS[USES[_st][0]].append((USES[_st][1], _b))
    NORMS += {"A1a": [("ln1", _b)], "D1e": [("ln2", _b)], "D2": [("ln3", _b)]}.get(_st, [])
    if _st == "X2":
        AREAS["unit"] += [("sim", 0), ("sim", 1)]
    if _st == "MT" and _b >= 1:
        AREAS["gen"] += [("mT", _b - 1)]
        AREAS["out"] += [(0, _b - 1), (1, _b - 1)]
    if _st[0] == "U":
        _n = int(_st[1])
        AREAS["unit"] += [(T_UNITS[_n], _b - 1)] * (_b >= 1) + [(S_UNITS[_n], _b)] * (_b < B)
    if _st in ("Sa", "Sc"):
        AREAS["unit"] += [("sg" if _st == "Sa" else "sd", _b)]
AREAS["unit"] += [(_n, _i) for _n, _i in (("sg", 0), ("sd", 0), ("sg", 1)) if (_n, _i) not in AREAS["unit"]]
AREAS["out"] += [("pos", 1)]
AREAS["proj"] += [("sd", 1)]


def nth(area, name):
    return AREAS[area].index(name)


def decoder_kernel(nc, x, cosT, sinT, ctxT, wxT, wqkvT, woT, gamma, gate_w, bias, w_gu, w_dn, ws_gu, ws_dn, out):
    qk_dram = nc.dram_tensor("qk_parts", [B, 2, 3, P, TPB * S], BF16, kind="Internal").ap()
    x3_dram = nc.dram_tensor("moe_input", [T, E], F32, kind="Internal").ap()
    z_dram = nc.dram_tensor("expert_rows", [T * 8, E], F32, kind="Internal").ap()

    with ExitStack() as ctx:
        def sb(name, shape, dt=F32):
            return ctx.enter_context(nc.sbuf_tensor(name, shape, dt))

        def pb(name, shape):
            return ctx.enter_context(nc.psum_tensor(name, shape, F32))

        def sem(name):
            return ctx.enter_context(nc.semaphore(name))

        res = sb("res", [P, NT, E])
        x3 = sb("x3", [P, NT, E])
        x3T = sb("x3T", [P, 2, T])
        adj = sb("adj", [P, NT, S])
        ring = sb("ring", [P, RA, 2, 2, 2, FF])
        ring_dn = sb("ring_dn", [P, RA, 2, E])
        identf = sb("identf", [P, P])
        identb = sb("identb", [P, P], BF16)
        tri = sb("tri", [P, P], BF16)
        ones = sb("ones", [P, P], BF16)
        gatew = sb("gatew", [P, 2, NE])
        wsgu = sb("wsgu", [P, 2, 2 * FF])
        wsdn = sb("wsdn", [FF, E])
        biasb = sb("biasb", [P, NE])
        logit = sb("logit", [P, NT, NE])
        iotac = sb("iotac", [P, CAP, NT], BF16)
        keep = sb("keep", [P, NT, NE])
        mv = sb("mv", [P, 3, TPB, 2])
        st6 = sb("st6", [P, TPB, 6])
        rstd = sb("rstd", [P, 3, TPB])
        srs = sb("srs", [P, TPB])
        gam = sb("gam", [P, 4])
        zero = sb("zero", [P, E])
        cexp = sb("cexp", [P, 2])

        ARENA = 32000
        arena = sb("arena", [P, ARENA])
        at = {"attention": 0, "moe": 0}

        def cut(phase, *shape, dt=F32):
            n = int(np.prod(shape))
            words = n if dt != BF16 else (n + 1) // 2
            a = arena[:, at[phase]:at[phase] + words]
            at[phase] += words
            if dt != F32:
                a = a.bitcast(dt)
            names = "abcde"[:len(shape)]
            if len(shape) > 1:
                a = a.rearrange(f"p ({' '.join(names)}) -> p {' '.join(names)}",
                                **{k: v for k, v in zip(names[1:], shape[1:])})
            return a

        AT = "attention"
        wqkv = cut(AT, 2, 3 * E)
        cosb = cut(AT, S)
        sinb = cut(AT, S)
        xn = cut(AT, 2, TPB, E)
        xnT = cut(AT, 2, 2, S)
        qkc = cut(AT, 4, S)
        qks = cut(AT, 4, S)
        parts = cut(AT, 3, 4, S, dt=BF16)
        qst1, kst1 = cut(AT, H, S, dt=BF16), cut(AT, H, S, dt=BF16)
        simS = cut(AT, NT, S)
        work = cut(AT, 2, S)
        wo = cut(AT, 2, E)
        masks = cut(AT, P, dt=BF16)
        sel = cut(AT, H, P, dt=BF16)
        late = ring[:, RA - 6:].rearrange("p r e c g f -> p (r e c g f)")[:, 0:H * S].bitcast(BF16).rearrange("p (a h s) -> p a h s", a=2, h=H)
        qst = [cut(AT, H, S, dt=BF16), qst1, late[:, 0]]
        kst = [cut(AT, H, S, dt=BF16), kst1, late[:, 1]]
        vaug = cut(AT, 3, TPB, H, 32)
        nmax = cut(AT, TPB, H)
        nmr = cut(AT, TPB, H)
        nmp = cut(AT, TPB, P, dt=BF16)
        nmT = cut(AT, S, dt=BF16)
        prob = cut(AT, 6, 1024)
        oT = cut(AT, 4, S)
        otok = cut(AT, TPB, E)
        onT = cut(AT, 2, S)
        rec = cut(AT, TPB, H)
        mix = otok
        best = cut(AT, 2, 8)
        ctxs = prob[:, 0, :]
        wx = prob[:, 1, 0:2 * P].rearrange("p (a b) -> p a b", a=2)
        cq = prob[:, 2, :]
        ck = prob[:, 3, :]

        MO = "moe"
        score = cut(MO, NT, NE)
        sbias = cut(MO, NT, NE)
        hi1, lo1 = cut(MO, NT * NG, 4), cut(MO, NT * NG, 4)
        hi2, lo2, ta2, tb2 = (cut(MO, NT * NG, 2) for _ in range(4))
        hi3, lo3, ta3, tb3 = (cut(MO, NT * NG, 1) for _ in range(4))
        gsum = cut(MO, NT, 12)
        gtop = cut(MO, NT, 8)
        gpick = cut(MO, NT, 8)
        gout = cut(MO, NT, 12)
        gpen = cut(MO, NT, NG)
        cand = cut(MO, NT, NE + 2)
        etop = cut(MO, NT, 8)
        epick = cut(MO, NT, 8)
        eout = cut(MO, NT, NE + 2)
        selb = cut(MO, 2 * NT - 1, NE, dt=BF16)
        wsel = cut(MO, NT, NE)
        wsum = cut(MO, NT)
        slot = cut(MO, NE, NT, dt=BF16)
        hsh = cut(MO, T)
        ssh = cut(MO, T)
        vals = cut(MO, NT, NE, 8, dt=BF16)
        assert at["moe"] <= 14336 - 512
        hotbuf = cut(MO, 2, EPG, CAP, NT, dt=BF16)
        info = cut(MO, 2, PPG, 8)
        infoc = cut(MO, 2, CPG, 2)
        rowf = cut(MO, 2, PPG)
        toki = cut(MO, NC, dt=I32)
        rowi = cut(MO, NP, dt=I32)
        wslot = cut(MO, NP)
        xg = cut(MO, NX, E)
        xgT = cut(MO, 2, 2, EPG * CAP + CP - CAP)
        act = cut(MO, 2, FF)
        hid = cut(MO, 2, FF)
        hidT = cut(MO, 2, P)
        yrow = cut(MO, NY, E)
        base = at[MO]
        ring2 = cut(MO, RP - RA, 2, 2, 2 * FF)
        ring2_dn = cut(MO, RP - RA, 2, E)
        assert at[MO] <= ARENA
        at[MO] = base
        zin = cut(MO, NZ, KE, E)
        fin = cut(MO, NZ, E)

        unit = pb("unit", [P, 2, 1024])
        proj = pb("proj", [P, 1024])
        gen = pb("gen", [P, 512])
        outp = pb("outp", [P, 512])
        genb = gen[:, :].bitcast(BF16)

        x_in = [sem(f"x_in{b}") for b in range(B)]
        ctx_in, gamma_in, rope_in, wqkv_in, wo_in, moe_in = (sem(n) for n in ("ctx_in", "gamma_in", "rope_in", "wqkv_in", "wo_in", "moe_in"))
        parts_out = [[sem(f"parts_out{b}_{j}") for j in range(3)] for b in range(B)]
        stack_in = [sem(f"stack_in{b}") for b in range(B)]
        x3_out = sem("x3_out")
        z_zeroed = sem("z_zeroed")
        ring_in = [sem(f"ring_in{i}") for i in range(RP)]
        gathered = [sem(f"gathered{i}") for i in range(NX)]
        scattered = [sem(f"scattered{i}") for i in range(NY)]
        z_in = [sem(f"z_in{i}") for i in range(NZ)]
        out_done = [sem(f"out_done{i}") for i in range(NZ)]
        dve_step, act_step, pool_step = sem("dve_step"), sem("act_step"), sem("pool_step")
        full = {a: sem(f"{a}_full") for a in AREAS}
        free = {"gen": sem("gen_free"), "proj": sem("proj_free"), "out": sem("out_free"),
                "unit": [sem("unit_free0"), sem("unit_free1")]}
        ident_ready, pads_ready, const_ready, order_ready, pick_ready, vals_init = (
            sem(n) for n in ("ident_ready", "pads_ready", "const_ready", "order_ready", "pick_ready", "vals_init"))
        zero_ready = sem("zero_ready")
        gamma_sig = sem("gamma_sig")
        var_ready, rstd_ready = sem("var_ready"), sem("rstd_ready")
        xn_ready, shuffled, sin_done, roped, part0, rest_ready, part1, part2 = (
            sem(n) for n in ("xn_ready", "shuffled", "sin_done", "roped", "part0", "rest_ready", "part1", "part2"))
        shift_ready, prob_ready, sim_ready, adj_half, adj_row = (
            sem(n) for n in ("shift_ready", "prob_ready", "sim_ready", "adj_half", "adj_row"))
        x3_ready = sem("x3_ready")
        score_ready, sel_ready, vals_ready = sem("score_ready"), sem("sel_ready"), sem("vals_ready")
        sh_act = sem("sh_act")
        hot_ready, info_full, info_free, index_ready, chunk_full, chunk_free, token_ready = (
            sem(n) for n in ("hot_ready", "info_full", "info_free", "index_ready", "chunk_full", "chunk_free", "token_ready"))
        xt_full, xt_free, gu_full, act_ready, hid_ready, ht_full, ht_free, y_full, y_free = (
            sem(n) for n in ("xt_full", "xt_free", "gu_full", "act_ready", "hid_ready", "ht_full", "ht_free",
                             "y_full", "y_free"))
        fin_ready = sem("fin_ready")

        def filled(eng, area, name):
            eng.wait_ge(full[area], nth(area, name) + 1)

        def emptied(eng, area, name):
            n = nth(area, name)
            if area == "unit":
                eng.wait_ge(free["unit"][n % 2], n // 2 + 1)
            else:
                eng.wait_ge(free[area], n + 1)

        def unit_free(name):
            return free["unit"][nth("unit", name) % 2]

        def unit_at(name):
            return unit[:, nth("unit", name) % 2, :]

        def gate_up_weights(p):
            s = p % RP
            return ring[:, s].rearrange("p e c g f -> p e c (g f)") if s < RA else ring2[:, s - RA]

        def down_weights(p):
            s = p % RP
            return ring_dn[:, s] if s < RA else ring2_dn[:, s - RA]

        def probs_at(key):
            return prob[:, T_UNITS.index(key), :]

        block = ctx.enter_context(nc.Block())

        @block.sync
        def _(sp):
            xv = x.rearrange("(t p) e -> p t e", p=P)
            sp.dma_start(ctxs[0:DC, :], ctxT).then_inc(ctx_in, 16)
            sp.dma_start(wx[0:DC, :, 0:DC], wxT.rearrange("a k n -> k a n")).then_inc(ctx_in, 16)
            sp.dma_start(res[:, 0:TPB, :], xv[:, 0:TPB, :]).then_inc(x_in[0], 16)
            sp.dma_start(wqkv, wqkvT.rearrange("(c p) n -> p c n", p=P)).then_inc(wqkv_in, 16)
            sp.dma_start(cosb, cosT).then_inc(rope_in, 16)
            sp.dma_start(sinb, sinT).then_inc(rope_in, 16)
            sp.dma_start(gam[:, 0:1], gamma.to_broadcast((P, 1))).then_inc(gamma_in, 16)
            for b in range(1, B):
                sp.dma_start(res[:, TPB * b:TPB * b + TPB, :], xv[:, TPB * b:TPB * b + TPB, :]).then_inc(x_in[b], 16)
            sp.dma_start(wo, woT.rearrange("(c p) n -> p c n", p=P)).then_inc(wo_in, 16)
            sp.dma_start(gatew[:, :, :], gate_w.rearrange("(c p) n -> p c n", p=P)).then_inc(moe_in, 16)
            sp.dma_start(wsgu[:, :, :], ws_gu.rearrange("(c p) n -> p c n", p=P)).then_inc(moe_in, 16)
            sp.dma_start(wsdn[:, :], ws_dn).then_inc(moe_in, 16)
            sp.dma_start(biasb[:, :], bias.to_broadcast((P, NE))).then_inc(moe_in, 16)

            def ring_fill(p):
                sp.dma_start(gate_up_weights(p).rearrange("p e c n -> p (e c n)"), w_gu[p]).then_inc(ring_in[p % RP], 16)
                sp.dma_start(down_weights(p)[0:FF].rearrange("p e n -> p (e n)"), w_dn[p]).then_inc(ring_in[p % RP], 16)

            def store(b, j):
                sp.wait_ge((part0, part1, part2)[j], b + 1)
                sp.dma_start(qk_dram[b, :, j].rearrange("a p n -> p a n"), parts[:, j].rearrange("p (a c) s -> p a (c s)", a=2)).then_inc(parts_out[b][j], 16)

            def load(b, newest):
                sp.wait_ge(parts_out[b][newest], 16)
                for a, dst, terms in ((0, qst, TERMS_Q), (1, kst, TERMS_K)):
                    for n, m in ((0, 3), (3, 2), (5, 1)):
                        if max(terms[n:n + m]) != newest:
                            continue
                        to = dst[b % 3][n * D:(n + m) * D].rearrange("p h s -> p (h s)")
                        src = qk_dram[b, a].rearrange("j (d h) n -> (j d) (h n)", d=D)
                        if m > 1 and terms[n] == terms[n + 1]:
                            src = src[terms[n] * D:(terms[n] + 1) * D].unsqueeze(0).broadcast_to((m, D, H * S))
                        else:
                            src = src[terms[n] * D:(terms[n] + m) * D]
                        sp.dma_start(to, src).then_inc(stack_in[b], 16)

            later = {("A2d", 1): range(0, 1), ("A2d", 2): range(1, RA - 6), ("D3a", 1): range(RA - 6, RA), ("D3a", 3): range(RA, RP)}
            for stage, b in STEPS:
                if stage == "A2d":
                    if b >= 3:
                        filled(sp, "unit", (T_UNITS[-1], b - 3))
                    store(b, 0)
                    store(b, 1)
                    load(b, 0)
                    store(b, 2)
                    load(b, 1)
                    load(b, 2)
                    if b == 1:
                        sp.wait_ge(zero_ready, 1)
                        zv = z_dram.rearrange("(t p k) n -> t p k n", p=P, k=8)
                        for t in range(NT):
                            sp.dma_start(zv[t, :, 0:KE, :], zero[:, :].unsqueeze(1).broadcast_to((P, KE, E))).then_inc(z_zeroed, 16)
                if stage == "D3a":
                    sp.wait_ge(x3_ready, b + 1)
                    sp.dma_start(x3_dram.rearrange("(t p) e -> p t e", p=P)[:, TPB * b:TPB * b + TPB, :],
                                 x3[:, TPB * b:TPB * b + TPB, :]).then_inc(x3_out, 16)
                if (stage, b) == ("D3a", 1):
                    filled(sp, "unit", (T_UNITS[-1], 2))
                if (stage, b) == ("D3a", B - 1):
                    filled(sp, "gen", ("att", B - 1))
                for p in later.get((stage, b), ()):
                    ring_fill(p)
            for p in range(RP, NP):
                sp.wait_ge(y_full, p - RP + 1)
                ring_fill(p)
            for s in range(NY):
                sp.wait_ge(scattered[s], 16 * (NP // NY))
            zv = z_dram.rearrange("(t p k) n -> t p k n", p=P, k=8)
            ov = out.rearrange("(t p) e -> t p e", p=P)

            def rows_in(i):
                t, cols = PIECES[i]
                sp.dma_start(zin[:, i % NZ, :, cols], zv[t, :, 0:KE, cols]).then_inc(z_in[i % NZ], 16)

            for i in range(NZ):
                rows_in(i)
            for i, (t, cols) in enumerate(PIECES):
                sp.wait_ge(fin_ready, i + 1)
                sp.dma_start(ov[t, :, cols], fin[:, i % NZ, cols]).then_inc(out_done[i % NZ], 16)
                if i + NZ < len(PIECES):
                    rows_in(i + NZ)
            for s in range(NZ):
                sp.wait_ge(out_done[s], 16 * len(range(s, len(PIECES), NZ)))

        @block.tensor
        def _(pe):
            mm = nc.tensor.matmul

            def claim(area, name):
                n = nth(area, name)
                if area == "unit":
                    if n >= 2:
                        pe.wait_ge(free["unit"][n % 2], n // 2)
                elif n >= 1:
                    pe.wait_ge(free[area], n)

            def context_projection(m):
                claim("proj", ("QT", 0) if m == 0 else ("KT", 0))
                if m == 0:
                    pe.wait_ge(pads_ready, 1)
                    pe.wait_ge(ctx_in, 32)
                for n in range(2):
                    last = mm(proj[:, n * 512:(n + 1) * 512], wx[:, m, :], ctxs[:, n * 512:(n + 1) * 512], start=True, stop=True)
                last.then_inc(full["proj"], 1)

            def similarity():
                emptied(pe, "proj", ("KT", 0))
                for u in range(2):
                    for j in range(4):
                        t = 4 * u + j
                        b = t // TPB
                        last = mm(unit[:, u, j * S:(j + 1) * S], cq[:, t * P:(t + 1) * P], ck[:, b * S:(b + 1) * S], start=True, stop=True)
                    last.then_inc(full["unit"], 1)

            def transpose_norm(b):
                claim("gen", ("xnT", b))
                pe.wait_ge(ident_ready, 1)
                pe.wait_ge(xn_ready, b + 1)
                for c in range(2):
                    for t in range(TPB):
                        last = nc.tensor.transpose(gen[:, (2 * c + t) * P:(2 * c + t + 1) * P], xn[:, b % 2, t, c * P:(c + 1) * P], identf[:, :])
                last.then_inc(full["gen"], 1)

            def project_qk(b):
                emptied(pe, "gen", ("xnT", b))
                pe.wait_ge(wqkv_in, 16)
                claim("proj", ("qk", b))
                for m in range(4):
                    for c in range(2):
                        last = mm(proj[:, m * S:(m + 1) * S], wqkv[:, c, m * P:(m + 1) * P], xnT[:, b % 2, c, :], start=(c == 0), stop=(c == 1))
                last.then_inc(full["proj"], 1)

            def project_v(b):
                claim("gen", ("v", b))
                for t in range(TPB):
                    for c in range(2):
                        last = mm(gen[:, t * E:(t + 1) * E], xnT[:, b % 2, c, t * P:(t + 1) * P], wqkv[:, c, 2 * E:3 * E], start=(c == 0), stop=(c == 1))
                last.then_inc(full["gen"], 1)

            def s_unit(b, key):
                _, t, u = key
                claim("unit", (key, b))
                n = P * (t + 1)
                for j in range(1024 // n):
                    h = 1024 // n * u + j
                    area = unit_at((key, b))[:, j * n:(j + 1) * n]
                    mm(area, qst[b % 3][0:KT, h, t * P:(t + 1) * P], kst[b % 3][0:KT, h, 0:n], start=True, stop=False)
                    last = mm(area[:, n - P:n], identb[:, :], masks, start=False, stop=True)
                last.then_inc(full["unit"], 1)

            def t_unit(b, key):
                _, kt, u = key
                claim("unit", (key, b))
                w = S - kt * P
                for j in range(1024 // w):
                    h = 1024 // w * u + j
                    area = unit_at((key, b))[:, j * w:(j + 1) * w]
                    mm(area, kst[b % 3][0:KT, h, kt * P:(kt + 1) * P], qst[b % 3][0:KT, h, kt * P:S], start=True, stop=False)
                    last = mm(area, sel[:, h, :], nmT[:, kt * P:S], start=False, stop=True)
                last.then_inc(full["unit"], 1)

            def pv(b, hg):
                key0, key1 = ("T", 0, hg), ("T", 1, hg // 2)
                order = T_UNITS
                pe.wait_ge(prob_ready, 6 * b + max(order.index(key0), order.index(key1)) + 1)
                if hg % 2 == 0:
                    claim("out", (hg // 2, b))
                c0 = (hg % 2) * S
                for j in range(4):
                    mm(outp[32 * j:32 * j + 32, c0:c0 + S], vaug[:, b % 3, 0, 4 * hg + j, :],
                       probs_at(key0)[:, j * S:(j + 1) * S], start=True, stop=False, tile_position=(0, 32 * j))
                for j in range(4):
                    k = (4 * hg + j) % 8
                    last = mm(outp[32 * j:32 * j + 32, c0 + P:c0 + S], vaug[:, b % 3, 1, 4 * hg + j, :],
                              probs_at(key1)[:, k * P:(k + 1) * P], start=False, stop=True, tile_position=(0, 32 * j))
                if hg % 2 == 1:
                    last.then_inc(full["out"], 1)

            def shifts_turned(b):
                if b >= 1:
                    claim("gen", ("mT", b - 1))
                    pe.wait_ge(shift_ready, b)
                    for t in range(TPB):
                        last = nc.tensor.transpose(genb[:, t * P:(t + 1) * P], nmp[:, t, :], identb[:, :])
                    last.then_inc(full["gen"], 1)
                else:
                    pe.wait_ge(const_ready, 1)

            def units(n):
                def step(b):
                    if n == 0 and b >= 1:
                        emptied(pe, "gen", ("mT", b - 1))
                    if n == 0 and b < B:
                        pe.wait_ge(stack_in[b], 16 * 6)
                    if b >= 1:
                        t_unit(b - 1, T_UNITS[n])
                    if b < B:
                        s_unit(b, S_UNITS[n])
                    if b >= 1 and n >= 3:
                        pv(b - 1, n - 3)
                return step

            def last_outputs(b):
                if b >= 1:
                    pv(b - 1, 3)

            def adjacency_turned(b):
                claim("gen", ("aT", b))
                pe.wait_ge(adj_row, b + 1)
                for i in range(TPB):
                    for j in range(TPB):
                        last = nc.tensor.transpose(gen[:, i * S + j * P:i * S + (j + 1) * P], adj[:, TPB * b + j, i * P:(i + 1) * P], identf[:, :])
                last.then_inc(full["gen"], 1)

            def heads_by_token(b):
                claim("proj", ("otok", b))
                emptied(pe, "out", (1, b))
                for t in range(TPB):
                    for hg in range(4):
                        last = nc.tensor.transpose(proj[:, (4 * t + hg) * P:(4 * t + hg + 1) * P], oT[:, hg, t * P:(t + 1) * P], identf[:, :])
                last.then_inc(full["proj"], 1)

            def heads_by_dim(b):
                claim("gen", ("onT", b))
                emptied(pe, "proj", ("otok", b))
                for c in range(2):
                    for t in range(TPB):
                        last = nc.tensor.transpose(gen[:, (2 * c + t) * P:(2 * c + t + 1) * P], otok[:, t, c * P:(c + 1) * P], identf[:, :])
                last.then_inc(full["gen"], 1)

            def project_out(b):
                claim("gen", ("att", b))
                emptied(pe, "gen", ("onT", b))
                pe.wait_ge(wo_in, 16)
                for t in range(TPB):
                    for c in range(2):
                        last = mm(gen[:, t * E:(t + 1) * E], onT[:, c, t * P:(t + 1) * P], wo[:, c, :], start=(c == 0), stop=(c == 1))
                last.then_inc(full["gen"], 1)

            def transpose_x3(b):
                claim("gen", ("x3T", b))
                pe.wait_ge(x3_ready, b + 1)
                for c in range(2):
                    for t in range(TPB):
                        last = nc.tensor.transpose(gen[:, (2 * c + t) * P:(2 * c + t + 1) * P], x3[:, TPB * b + t, c * P:(c + 1) * P], identf[:, :])
                last.then_inc(full["gen"], 1)

            def router(b):
                claim("gen", ("lg", b))
                emptied(pe, "gen", ("x3T", b))
                pe.wait_ge(moe_in, 64)
                for t in range(TPB):
                    for c in range(2):
                        g = TPB * b + t
                        last = mm(gen[:, t * NE:(t + 1) * NE], x3T[:, c, g * P:(g + 1) * P], gatew[:, c, :], start=(c == 0), stop=(c == 1))
                last.then_inc(full["gen"], 1)

            def shared_in(n):
                claim("unit", ("sg", n))
                emptied(pe, "gen", ("x3T", 2 * n + 1))
                for g in range(2):
                    for c in range(2):
                        last = mm(unit_at(("sg", n))[0:FF, g * 512:(g + 1) * 512], wsgu[:, c, g * FF:(g + 1) * FF], x3T[:, c, n * 512:(n + 1) * 512], start=(c == 0), stop=(c == 1))
                last.then_inc(full["unit"], 1)

            def shared_out(n):
                area, to = (("unit", unit_at(("sd", 0))), ("proj", proj))[n]
                claim(area, ("sd", n))
                emptied(pe, "unit", ("sg", n))
                for j in range(4):
                    t = 4 * n + j
                    last = mm(to[:, j * E:(j + 1) * E], hsh[0:FF, t * P:(t + 1) * P], wsdn[:, :], start=True, stop=True)
                last.then_inc(full[area], 1)

            def positions(n):
                claim("out", ("pos", n))
                pe.wait_ge(sel_ready, n + 1)
                pe.wait_ge(order_ready, 1)
                pe.wait_ge(pick_ready, 1)
                sf = selb.rearrange("p t e -> p (t e)")
                t0, t1 = ((0, ROUTED), (ROUTED, NT))[n]
                for j in range(t1):
                    last = mm(outp[:, t0 * NE:t1 * NE], ones[:, :] if j else tri[:, :], sf[:, (NT - 1 - j + t0) * NE:(NT - 1 - j + t1) * NE], start=(j == 0), stop=(j == t1 - 1))
                last.then_inc(full["out"], 1)

            def keep_clock(n):
                for _ in range(n):
                    mm(proj[:, 0:448], ones[:, :], selb.rearrange("p t e -> p (t e)")[:, 0:448], start=True, stop=True)

            def slot_map(g):
                pe.wait_ge(hot_ready, 2 * (g + 1))
                if g == 0:
                    pe.wait_ge(vals_ready, 1)
                    pe.wait_ge(vals_init, 1)
                    emptied(pe, "gen", ("lg", B - 1))
                else:
                    pe.wait_ge(info_free, g)
                for j in range(CPG):
                    for t in range(NT):
                        last = mm(gen[:, PPG * 8 + 2 * j:PPG * 8 + 2 * j + 2], hotbuf[:, g % 2].rearrange("p e c t -> p (e c) t")[:, j * P:(j + 1) * P, t],
                           vals[:, t, 0, V_TILE8:V_TOKEN + 1], start=(t == 0), stop=(t == NT - 1))
                last.then_inc(chunk_full, 1)
                if g == 0:
                    pe.wait_ge(chunk_free, 1)
                    pe.wait_ge(vals_ready, 2)
                for q in range(PPG):
                    for t in range(NT):
                        for e in range(2):
                            last = mm(gen[CP * e:CP * e + CAP, q * 8:(q + 1) * 8], hotbuf[:, g % 2, 2 * q + e, :, t],
                                      vals[:, t, EPG * g + 2 * q + e, :], start=(t == 0), stop=(t == NT - 1), tile_position=(0, CP * e))
                last.then_inc(info_full, 1)

            def tokens_in(k):
                pe.wait_ge(gathered[k % NX], 16 * (k // NX + 1))
                if k >= 2:
                    pe.wait_ge(xt_free, k - 1)
                for c in range(2):
                    last = nc.tensor.transpose(unit[:, 0, (k % 2) * 512 + c * P:(k % 2) * 512 + (c + 1) * P], xg[:, k % NX, c * P:(c + 1) * P], identf[:, :])
                last.then_inc(xt_full, 1)

            def gate_up(p):
                g, q = divmod(p, PPG)
                pe.wait_ge(xt_free, CPG * g + min(q, CPG - 1) + 1)
                pe.wait_ge(ring_in[p % RP], 32 * (p // RP + 1))
                if p == 0:
                    pe.wait_ge(vals_init, 2)
                if p >= 2:
                    pe.wait_ge(hid_ready, p - 1)
                for c in range(2):
                    for e in range(2):
                        first = (2 * q + e) * CAP
                        last = mm(unit[CP * e:CP * e + CP, 1, (p % 2) * 512:(p % 2) * 512 + 2 * FF], xgT[:, g % 2, c, first:first + CP],
                                  gate_up_weights(p)[:, e, c], start=(c == 0), stop=(c == 1), tile_position=(0, CP * e))
                last.then_inc(gu_full, 1)

            def hidden(p):
                pe.wait_ge(hid_ready, p + 1)
                if p >= 1:
                    pe.wait_ge(ht_free, p)
                nc.tensor.transpose(outp[0:FF, 0:P], hid[:, p % 2, :], identf[:, :]).then_inc(ht_full, 1)

            def down(p):
                pe.wait_ge(ht_free, p + 1)
                if p >= 2:
                    pe.wait_ge(y_free, p - 1)
                for e in range(2):
                    last = mm(proj[CP * e:CP * e + CP, (p % 2) * 512:(p % 2) * 512 + E], hidT[:, p % 2, CP * e:CP * (e + 1)],
                              down_weights(p)[:, e, :], start=True, stop=True, tile_position=(0, CP * e))
                last.then_inc(y_full, 1)

            run = {"X0": lambda b: context_projection(0), "X1": lambda b: context_projection(1), "X2": lambda b: similarity(),
                   "A1b": transpose_norm, "A1c": project_qk, "A1d": project_v, "MT": shifts_turned, "ME": last_outputs,
                   "D1a": adjacency_turned, "D1b": heads_by_token, "D1d": heads_by_dim, "D1e": project_out,
                   "D3a": transpose_x3, "D3b": router, "Sa": shared_in, "Sc": shared_out, "P": positions, **{f"U{n}": units(n) for n in range(6)}}
            for stage, b in STEPS:
                if stage in run:
                    run[stage](b)
            if ("Sc", 0) not in STEPS:
                shared_out(0)
            shared_in(1)
            keep_clock(WARM[0])
            positions(1)
            keep_clock(WARM[1])
            slot_map(0)
            keep_clock(WARM[2])
            slot_map(1)
            keep_clock(WARM[3])
            emptied(pe, "out", ("pos", 1))
            emptied(pe, "unit", ("sd", 0))
            emptied(pe, "unit", ("sg", 1))
            for p in range(NP + 3):
                if p < NP and p % PPG < CPG:
                    tokens_in(CPG * (p // PPG) + p % PPG)
                if 0 <= p - 1 < NP:
                    gate_up(p - 1)
                if 0 <= p - 3 < NP:
                    down(p - 3)
                if 0 <= p - 2 < NP:
                    hidden(p - 2)
                if p in MAPPED:
                    slot_map(MAPPED[p])
            pe.wait_ge(y_free, NP)
            shared_out(1)

        @block.scalar
        def _(sc):
            steps = [0]
            act_fn = nc.scalar.activation

            def link(ins):
                steps[0] += 1
                ins.then_inc(act_step, 1)
                sc.wait_ge(act_step, steps[0])

            def copy_ctx(name, dst):
                filled(sc, "proj", (name, 0))
                nc.scalar.copy(dst, proj[:, :]).then_inc(free["proj"], 1)

            def similarity():
                sc.wait_ge(gamma_in, 16)
                act_fn(gam[:, 1:2], gam[:, 0:1], ACT.Sigmoid).then_inc(gamma_sig, 1)
                for u in range(2):
                    filled(sc, "unit", ("sim", u))
                    nc.scalar.copy(simS[:, 4 * u:4 * u + 4, :].rearrange("p t s -> p (t s)"), unit[:, u, :]).then_inc(sim_ready, 1)
                    act_fn(adj[:, 4 * u:4 * u + 4, :].rearrange("p t s -> p (t s)"), unit[:, u, :], ACT.Sigmoid,
                           scale=1.0 / (HC * (DC // HC) ** 0.5)).then_inc(free["unit"][u], 1)

            def norm_dims(b):
                filled(sc, "gen", ("xnT", b))
                nc.scalar.copy(xnT[:, b % 2].rearrange("p c s -> p (c s)"), gen[:, :]).then_inc(free["gen"], 1)

            def values(b):
                filled(sc, "gen", ("v", b))
                if b == 0:
                    sc.wait_ge(pads_ready, 2)
                if b >= 3:
                    filled(sc, "out", (1, b - 3))
                nc.scalar.copy(vaug[:, b % 3, :, :, 0:D], gen[:, :].rearrange("p (t h d) -> p t h d", t=TPB, h=H)).then_inc(free["gen"], 1)

            def first_part(b):
                sc.wait_ge(roped, b + 1)
                if b >= 1:
                    for j in range(3):
                        sc.wait_ge(parts_out[b - 1][j], 16)
                nc.scalar.copy(parts[:, 0], qkc).then_inc(part0, 1)

            def second_part(b):
                sc.wait_ge(rest_ready, b + 1)
                nc.scalar.copy(parts[:, 1], qkc).then_inc(part1, 1)

            def head_outputs(b, half):
                filled(sc, "out", (half, b))
                if b >= 1:
                    filled(sc, "proj", ("otok", b - 1))
                nc.scalar.copy(oT[:, 2 * half:2 * half + 2, :].rearrange("p g s -> p (g s)"), outp[:, :]).then_inc(free["out"], 1)

            def exponentials(n):
                def step(m):
                    if m == 0:
                        return
                    b = m - 1
                    key = T_UNITS[n]
                    filled(sc, "unit", (key, b))
                    if b == 0 and n == 0:
                        filled(sc, "unit", ("sim", 1))
                    if b >= 1 and n == 0:
                        filled(sc, "out", (1, b - 1))
                    act_fn(prob[:, n, :], unit_at((key, b)), ACT.Exp, scale=D ** -0.5).then_inc(unit_free((key, b)), 1)
                    if n == 5:
                        head_outputs(b, 0)
                return step

            def last_outputs(m):
                if m >= 1:
                    head_outputs(m - 1, 1)

            def output_dims(b):
                filled(sc, "gen", ("onT", b))
                nc.scalar.copy(onT.rearrange("p c s -> p (c s)"), gen[:, :]).then_inc(free["gen"], 1)

            def x3_dims(b):
                filled(sc, "gen", ("x3T", b))
                nc.scalar.copy(x3T[:, :, b * S:(b + 1) * S], gen[:, :].rearrange("p (c s) -> p c s", c=2)).then_inc(free["gen"], 1)

            def logits(b):
                filled(sc, "gen", ("lg", b))
                nc.scalar.copy(logit[:, TPB * b:TPB * b + TPB, :], gen[:, 0:TPB * NE].rearrange("p (t e) -> p t e", t=TPB)).then_inc(free["gen"], 1)

            def scores(n):
                tiles = slice(*((0, ROUTED), (ROUTED, NT))[n])
                if n == 0:
                    filled(sc, "gen", ("v", B - 1))
                emptied(sc, "gen", ("lg", (ROUTED // TPB - 1, B - 1)[n]))
                act_fn(score[:, tiles, :], logit[:, tiles, :], ACT.Sigmoid).then_inc(score_ready, 1)

            def shared_silu(n):
                filled(sc, "unit", ("sg", n))
                act_fn(ssh[0:FF, n * 512:(n + 1) * 512], unit_at(("sg", n))[0:FF, 0:512], ACT.Silu).then_inc(sh_act, 1)

            def slot_infos(g):
                if g >= 2:
                    sc.wait_ge(index_ready, g - 1)
                    sc.wait_ge(token_ready, g - 1)
                sc.wait_ge(chunk_full if g == 0 else info_full, g + 1)
                nc.scalar.copy(infoc[:, g % 2].rearrange("p j v -> p (j v)"), gen[:, PPG * 8:PPG * 8 + CPG * 2]).then_inc(chunk_free, 1)
                if g == 0:
                    sc.wait_ge(info_full, 1)
                    sc.wait_ge(vals_init, 2)
                for e in range(2):
                    rows = slice(CP * e, CP * e + CAP)
                    ins = nc.scalar.copy(info[rows, g % 2].rearrange("p q v -> p (q v)"), gen[rows, 0:PPG * 8])
                ins.then_inc(info_free, 1)

            run = {"X0": lambda b: copy_ctx("QT", cq), "X1": lambda b: copy_ctx("KT", ck), "X2": lambda b: similarity(),
                   "A1b": norm_dims, "A1d": values, "A2b": first_part, "A2d": second_part, "ME": last_outputs,
                   "D1d": output_dims, "D3a": x3_dims, "D3b": logits, "R": scores, "Sa": shared_silu, **{f"U{n}": exponentials(n) for n in range(6)}}
            for stage, b in STEPS:
                if stage in run:
                    run[stage](b)
            scores(1)
            shared_silu(1)
            slot_infos(0)
            slot_infos(1)
            for p in range(NP + 3):
                if 0 <= p - 1 < NP:
                    q = p - 1
                    sc.wait_ge(gu_full, q + 1)
                    if q >= 2:
                        sc.wait_ge(hid_ready, q - 1)
                    act_fn(act[:, q % 2, :], unit[:, 1, (q % 2) * 512:(q % 2) * 512 + FF], ACT.Silu).then_inc(act_ready, 1)
                if 0 <= p - 3 < NP:
                    q = p - 3
                    sc.wait_ge(y_full, q + 1)
                    if q >= NY:
                        sc.wait_ge(scattered[q % NY], 16 * (q // NY))
                    sc.wait_ge(index_ready, q // PPG + 1)
                    act_fn(yrow[:, q % NY, :], proj[:, (q % 2) * 512:(q % 2) * 512 + E], ACT.Copy, scale=wslot[:, q:q + 1]).then_inc(y_free, 1)
                if p in MAPPED:
                    slot_infos(MAPPED[p])

        @block.gpsimd
        def _(gp):
            steps = [0]

            def link(ins):
                steps[0] += 1
                ins.then_inc(pool_step, 1)
                gp.wait_ge(pool_step, steps[0])

            pool = nc.gpsimd
            link(pool.memset(cexp[:, 0:1], -0.5))
            link(pool.memset(identf[:, :], 0.0))
            pool.affine_select(out=identf[:, :], in_=identf[:, :], compare_op=ALU.not_equal, fill=1.0,
                               base=0, pattern=[[-1, P]], channel_multiplier=1).then_inc(ident_ready, 1)
            gp.wait_ge(ident_ready, 1)

            def inverse_root(kind, b):
                gp.wait_ge(var_ready, NORMS.index((kind, b)) + 1)
                if NORMS.index((kind, b)):
                    gp.wait_ge(rstd_ready, NORMS.index((kind, b)))
                k = int(kind[2]) - 1
                link(pool.tensor_scalar(srs[:, :], mv[:, k, :, 1], EPS, None, ALU.add))
                end = pool.tensor_tensor(rstd[:, k, :], srs[:, :], cexp[:, 0:1].broadcast_to((P, TPB)), ALU.pow)
                if kind == "ln2":
                    link(end)
                    end = pool.tensor_scalar(rstd[:, k, :], rstd[:, k, :], gam[:, 2:3], None, ALU.mult)
                end.then_inc(rstd_ready, 1)

            def constants():
                link(pool.tensor_copy(identb[:, :], identf[:, :]))
                link(pool.memset(masks, 0.0))
                link(pool.affine_select(out=masks, in_=masks, compare_op=ALU.is_ge, fill=NEG, base=0,
                                        pattern=[[-1, P]], channel_multiplier=1))
                link(pool.memset(nmp, 0.0))
                link(pool.memset(sel, 0.0))
                for j in range(3):
                    end = pool.affine_select(out=sel, in_=sel, compare_op=ALU.not_equal, fill=1.0, base=-16 * j,
                                             pattern=[[-1, H], [0, P]], channel_multiplier=1)
                    if j < 2:
                        link(end)
                end.then_inc(const_ready, 1)

            def gamma_constants():
                gp.wait_ge(gamma_sig, 1)
                link(pool.tensor_scalar(gam[:, 2:3], gam[:, 1:2], -1.0, 1.0, ALU.mult, ALU.add))
                link(pool.tensor_scalar(gam[:, 3:4], gam[:, 1:2], 0.5, None, ALU.mult))
                for u in range(2):
                    emptied(gp, "unit", ("sim", u))
                    half = adj[:, 4 * u:4 * u + 4, :].rearrange("p t s -> p (t s)")
                    pool.tensor_scalar(half, half, gam[:, 3:4], None, ALU.mult).then_inc(adj_half, 1)
                pool.memset(zero[:, :], 0.0).then_inc(zero_ready, 1)

            def moe_constants():
                link(pool.memset(tri[:, :], 1.0))
                link(pool.affine_select(out=tri[:, :], in_=tri[:, :], compare_op=ALU.is_ge, fill=0.0, base=-1,
                                        pattern=[[1, P]], channel_multiplier=-1))
                link(pool.memset(ones[:, :], 1.0))
                link(pool.iota(iotac[:, :, :], pattern=[[1, CAP], [0, NT]], base=-CP, channel_multiplier=0, allow_small_or_imprecise_dtypes=True))
                link(pool.memset(keep[:, :, :], 1.0))
                link(pool.memset(keep[:, :, 0:1], 0.0))
                pool.memset(ring_dn[FF:P].rearrange("p a e n -> p (a e n)"), 0.0).then_inc(order_ready, 1)
                gp.wait_ge(order_ready, 1)

            def times_sin(b):
                if b == 0:
                    return
                gp.wait_ge(shuffled, b)
                pool.tensor_tensor(qks, qks, sinb.unsqueeze(1).broadcast_to((P, 4, S)), ALU.mult).then_inc(sin_done, 1)

            def rope_sum(b):
                if b >= 1:
                    gp.wait_ge(sin_done, b + 1)
                    emptied(gp, "proj", ("qk", b))
                    pool.tensor_tensor(qkc, qkc, qks, ALU.add).then_inc(roped, 1)

            def first_rest(b):
                if b >= 1:
                    gp.wait_ge(part0, b + 1)
                    pool.tensor_tensor(qkc, qkc, parts[:, 0], ALU.subtract).then_inc(rest_ready, 1)

            def third_part(b):
                if b >= 1:
                    gp.wait_ge(part1, b + 1)
                    pool.tensor_tensor(parts[:, 2], qkc, parts[:, 1], ALU.subtract).then_inc(part2, 1)
                if b == 1:
                    gamma_constants()
                if b == 2:
                    moe_constants()

            def norm1(b):
                inverse_root("ln1", b)
                if b == 0:
                    constants()

            def causal(n):
                def step(m):
                    if m == 0:
                        return
                    key = T_UNITS[n]
                    emptied(gp, "unit", (key, m - 1))
                    w = S - key[1] * P
                    v = prob[:, n, :].rearrange("p (h q) -> p h q", q=w)[:, :, 0:P]
                    pool.affine_select(out=v, in_=v, compare_op=ALU.is_ge, fill=0.0, base=0,
                                       pattern=[[0, 1024 // w], [1, P]], channel_multiplier=-1).then_inc(prob_ready, 1)
                return step

            def routing_constants(_):
                filled(gp, "gen", ("v", B - 1))
                for j in range(3):
                    gp.wait_ge(parts_out[B - 1][j], 16)
                filled(gp, "unit", (T_UNITS[-1], 1))
                link(pool.memset(gsum, NEG))
                link(pool.memset(gpick, NEG))
                link(pool.memset(epick, 3 * NEG))
                link(pool.memset(cand[:, :, NE:], 3 * NEG))
                pool.memset(selb[:, 0:NT - 1, :], 0.0).then_inc(pick_ready, 1)
                gp.wait_ge(pick_ready, 1)
                link(pool.memset(vals.rearrange("p t e v -> p (t e v)"), -16.0 * T))
                for col, step, first in ((V_TOKEN8, 8, 0), (V_TOKEN, 1, 0), (V_TILE8, 0, 8 * P)):
                    end = pool.iota(vals[:, :, :, col], pattern=[[first, NT], [0, NE]], base=0,
                                    channel_multiplier=step, allow_small_or_imprecise_dtypes=True)
                    if col != V_TILE8:
                        link(end)
                end.then_inc(vals_init, 1)

            run = {"V": routing_constants, "A1a": norm1, "A2a": times_sin, "A2b": rope_sum, "A2c": first_rest, "A2d": third_part,
                   "D1e": lambda b: inverse_root("ln2", b), "D2": lambda b: inverse_root("ln3", b), **{f"U{n}": causal(n) for n in range(6)}}
            for stage, b in STEPS:
                if stage in run:
                    run[stage](b)

            gp.wait_ge(x3_ready, B)
            emptied(gp, "gen", ("onT", B - 1))
            filled(gp, "gen", ("att", B - 1))
            link(pool.memset(hidT, 0.0))
            link(pool.memset(info, 0.0))
            link(pool.memset(ring2_dn[FF:P].rearrange("p a e n -> p (a e n)"), 0.0))
            pool.memset(xgT[:, :, :, EPG * CAP:], 0.0).then_inc(vals_init, 1)

            def gather(k):
                gp.wait_ge(token_ready, k // CPG + 1)
                if k >= NX:
                    gp.wait_ge(xt_full, k - NX + 1)
                pool.indirect_dma_start(out=xg[:, k % NX, :], out_offset=None, in_=x3_dram,
                                        in_offset=bass.IndirectOffsetOnAxis(ap=toki[:, k:k + 1], axis=0)).then_inc(gathered[k % NX], 16)

            def scatter(p):
                gp.wait_ge(y_free, p + 1)
                pool.indirect_dma_start(out=z_dram, out_offset=bass.IndirectOffsetOnAxis(ap=rowi[:, p:p + 1], axis=0),
                                        in_=yrow[:, p % NY, :], in_offset=None, bounds_check=T * 8 - 1,
                                        oob_is_err=False).then_inc(scattered[p % NY], 16)

            gp.wait_ge(x3_out, 16 * B)
            gp.wait_ge(z_zeroed, 16 * NT)
            for p in range(NP + LAG):
                if p < NP and p % PPG < CPG:
                    gather(CPG * (p // PPG) + p % PPG)
                if p >= LAG:
                    scatter(p - LAG)

        @block.vector
        def _(ve):
            steps = [0]
            v = nc.vector

            def mark(ins):
                steps[0] += 1
                ins.then_inc(dve_step, 1)
                return steps[0]

            def need(n):
                ve.wait_ge(dve_step, n)

            def link(ins):
                need(mark(ins))

            def adjacency():
                rounds = (TOPA - 1) // 8
                col = (TOPA - 1) % 8
                for t in range(0, NT, 2):
                    ve.wait_ge(sim_ready, t // 4 + 1)
                    last = [0, 0]
                    for r in range(rounds + 1):
                        for i in range(2):
                            if last[i]:
                                need(last[i])
                            last[i] = mark(v.max(best[:, i, :], simS[:, t + i, :] if r == 0 else work[:, i, :]))
                            yield t
                        for i in range(2):
                            if r < rounds:
                                need(last[i])
                                last[i] = mark(v.match_replace(work[:, i, :], best[:, i, :], simS[:, t + i, :] if r == 0 else work[:, i, :], NEG))
                                yield t
                    ve.wait_ge(adj_half, t // 4 + 1)
                    for i in range(2):
                        need(last[i])
                        ins = v.scalar_tensor_tensor(adj[:, t + i, :], simS[:, t + i, :], best[:, i, col:col + 1], adj[:, t + i, :], ALU.is_ge, ALU.mult)
                        if i == 0:
                            end = mark(ins)
                    ins.then_inc(adj_row, 1)
                    need(end)
                    ve.wait_ge(adj_row, t // TPB + 1)
                    yield t + 2
                while True:
                    yield NT

            filler = adjacency()
            at_tile = [0]

            def fill(n):
                for _ in range(n):
                    at_tile[0] = max(at_tile[0], next(filler))

            def stats(kind, b, src):
                k = int(kind[2]) - 1
                if NORMS.index((kind, b)):
                    ve.wait_ge(var_ready, NORMS.index((kind, b)))
                ends = [mark(v.bn_stats(st6[:, t, :], src[:, t, :])) for t in range(TPB)]
                for t in range(TPB):
                    need(ends[t])
                    ins = v.bn_aggr(mv[:, k, t, :], st6[:, t, :])
                ins.then_inc(var_ready, 1)

            def normalise(dst, src, kind, b):
                k = int(kind[2]) - 1
                ve.wait_ge(rstd_ready, NORMS.index((kind, b)) + 1)
                for t in range(TPB):
                    ins = v.tensor_scalar(dst[:, t, :], src[:, t, :], mv[:, k, t, 0:1], rstd[:, k, t:t + 1], ALU.subtract, ALU.mult)
                return ins

            def pads():
                v.memset(ctxs[DC:P, :], 0.0)
                v.memset(wx[DC:P, :, :], 0.0)
                v.memset(wx[0:DC, :, DC:P], 0.0).then_inc(pads_ready, 1)

            def value_pads():
                link(v.memset(vaug.rearrange("p a t h d -> p (a t h d)"), 0.0))
                v.memset(vaug[:, :, :, :, D:D + 1].rearrange("p a t h o -> p (a t h) o"), 1.0).then_inc(pads_ready, 1)

            def rows_of(b):
                return res[:, TPB * b:TPB * b + TPB, :]

            def adj_of(b):
                return adj[:, TPB * b:TPB * b + TPB, :]

            def norm1_stats(b):
                ve.wait_ge(x_in[b], 16)
                if b >= 1:
                    ve.wait_ge(xn_ready, b)
                stats("ln1", b, rows_of(b))

            def norm1(b):
                if b >= 2:
                    filled(ve, "gen", ("xnT", b - 2))
                normalise(xn[:, b % 2], rows_of(b), "ln1", b).then_inc(xn_ready, 1)
                if b == 0:
                    value_pads()

            def rope_products(b):
                filled(ve, "proj", ("qk", b))
                ve.wait_ge(rope_in, 32)
                if b >= 1:
                    ve.wait_ge(part2, b)
                pv = proj[:, :].rearrange("p (m s) -> p m s", m=4)
                ins = v.stream_shuffle(qks.rearrange("p m s -> p (m s)"), proj[:, :], [i ^ HPC for i in range(32)])
                if b == 0:
                    done = mark(ins)
                else:
                    ins.then_inc(shuffled, 1)
                v.tensor_tensor(qkc, pv, cosb.unsqueeze(1).broadcast_to((P, 4, S)), ALU.mult).then_inc(free["proj"], 1)
                if b == 0:
                    need(done)
                    v.tensor_tensor(qks, qks, sinb.unsqueeze(1).broadcast_to((P, 4, S)), ALU.mult).then_inc(sin_done, 1)

            def rope_sum(b):
                if b >= 1:
                    return
                ve.wait_ge(sin_done, b + 1)
                emptied(ve, "proj", ("qk", b))
                v.tensor_tensor(qkc, qkc, qks, ALU.add).then_inc(roped, 1)

            def first_rest(b):
                if b == 0:
                    ve.wait_ge(part0, 1)
                    v.tensor_tensor(qkc, qkc, parts[:, 0], ALU.subtract).then_inc(rest_ready, 1)

            def third_part(b):
                if b == 0:
                    ve.wait_ge(part1, 1)
                    v.tensor_tensor(parts[:, 2], qkc, parts[:, 1], ALU.subtract).then_inc(part2, 1)

            def shifts_turned(b):
                if b >= 1:
                    filled(ve, "gen", ("mT", b - 1))
                    if b >= 2:
                        filled(ve, "unit", (T_UNITS[-1], b - 2))
                    v.tensor_copy(nmT, genb[:, 0:S]).then_inc(free["gen"], 1)

            def maxima(i):
                def step(b):
                    if b == B:
                        return
                    key = S_UNITS[i]
                    _, t, u = key
                    n = P * (t + 1)
                    c = 1024 // n
                    filled(ve, "unit", (key, b))
                    v.tensor_reduce(nmax[:, t, c * u:c * u + c], unit_at((key, b)).rearrange("p (h k) -> p h k", k=n), axis=AX,
                                    op=ALU.max, negate=True).then_inc(unit_free((key, b)), 1)
                return step

            def shift_parts(b):
                if b == B:
                    return
                emptied(ve, "unit", (S_UNITS[-1], b))
                emptied(ve, "unit", (S_UNITS[-2], b))
                if b >= 1:
                    filled(ve, "gen", ("mT", b - 1))
                link(v.tensor_copy(nmp[:, :, 0:H], nmax))
                link(v.tensor_tensor(nmr, nmax, nmp[:, :, 0:H], ALU.subtract))
                link(v.tensor_copy(nmp[:, :, H:2 * H], nmr))
                v.tensor_tensor(nmp[:, :, 2 * H:3 * H], nmr, nmp[:, :, H:2 * H], ALU.subtract).then_inc(shift_ready, 1)

            def add_transposed(b):
                filled(ve, "gen", ("aT", b))
                v.tensor_tensor(adj_of(b), adj_of(b), gen[:, :].rearrange("p (t e) -> p t e", t=TPB), ALU.add).then_inc(free["gen"], 1)

            def head_average(b):
                filled(ve, "proj", ("otok", b))
                ov = proj[:, :].rearrange("p (t h d) -> p t h d", t=TPB, d=32)
                link(v.reciprocal(rec, ov[:, :, :, D]))
                if b >= 1:
                    filled(ve, "gen", ("onT", b - 1))
                v.tensor_tensor(otok.rearrange("p t (h d) -> p t h d", d=D), ov[:, :, :, 0:D],
                                rec.unsqueeze(3).broadcast_to((P, TPB, H, D)), ALU.mult).then_inc(free["proj"], 1)

            def attention_residual(b):
                filled(ve, "gen", ("att", b))
                v.tensor_tensor(rows_of(b), rows_of(b), gen[:, :].rearrange("p (t e) -> p t e", t=TPB), ALU.add).then_inc(free["gen"], 1)
                emptied(ve, "gen", ("att", b))
                stats("ln2", b, rows_of(b))

            def mixing(b):
                link(normalise(mix, rows_of(b), "ln2", b))
                link(v.tensor_tensor(mix, mix, adj_of(b), ALU.add))
                link(v.tensor_tensor(rows_of(b), rows_of(b), mix, ALU.add))
                stats("ln3", b, rows_of(b))

            def moe_input(b):
                normalise(x3[:, TPB * b:TPB * b + TPB, :], rows_of(b), "ln3", b).then_inc(x3_ready, 1)

            def routing(n):
                t0, t1 = ((0, ROUTED), (ROUTED, NT))[n]
                nt = t1 - t0
                ts = slice(t0, t1)
                gs = slice(t0 * NG, t1 * NG)
                if n == 0:
                    for j in range(3):
                        ve.wait_ge(parts_out[B - 1][j], 16)
                    filled(ve, "gen", ("v", B - 1))
                    ve.wait_ge(pick_ready, 1)
                ve.wait_ge(score_ready, n + 1)
                done = mark(v.tensor_tensor(sbias[:, ts], score[:, ts], biasb[:, :].unsqueeze(1).broadcast_to((P, nt, NE)), ALU.add))
                yield
                g8 = sbias[:, ts].rearrange("p t (g j) -> p (t g) j", j=NE // NG)
                need(done)
                hi = mark(v.tensor_tensor(hi1[:, gs], g8[:, :, 0:4], g8[:, :, 4:8], ALU.max))
                yield
                lo = mark(v.tensor_tensor(lo1[:, gs], g8[:, :, 0:4], g8[:, :, 4:8], ALU.min))
                yield
                for h, l, ho, lw, ta, tb, w in ((hi1, lo1, hi2, lo2, ta2, tb2, 2), (hi2, lo2, hi3, lo3, ta3, tb3, 1)):
                    h, l, ho, lw, ta, tb = (a[:, gs] for a in (h, l, ho, lw, ta, tb))
                    need(hi)
                    hi_next = mark(v.tensor_tensor(ho, h[:, :, 0:w], h[:, :, w:2 * w], ALU.max))
                    yield
                    v.tensor_tensor(ta, h[:, :, 0:w], h[:, :, w:2 * w], ALU.min)
                    yield
                    need(lo)
                    both = mark(v.tensor_tensor(tb, l[:, :, 0:w], l[:, :, w:2 * w], ALU.max))
                    yield
                    need(both)
                    lo = mark(v.tensor_tensor(lw, ta, tb, ALU.max))
                    hi = hi_next
                    yield
                tg = lambda a: a[:, gs].rearrange("p (t g) o -> p t (g o)", t=nt)
                need(lo)
                done = mark(v.tensor_tensor(gsum[:, ts, 0:NG], tg(hi3), tg(lo3), ALU.add))
                yield
                need(done)
                for t in range(t0, t1):
                    done = mark(v.max(gtop[:, t, :], gsum[:, t, 0:NG]))
                    yield
                need(done)
                done = mark(v.tensor_copy(gpick[:, ts, 0:KG], gtop[:, ts, 0:KG]))
                yield
                need(done)
                for t in range(t0, t1):
                    done = mark(v.match_replace(gout[:, t, :], gpick[:, t, :], gsum[:, t, :], -NEG))
                    yield
                need(done)
                done = mark(v.tensor_scalar(gpen[:, ts], gout[:, ts, 0:NG], -NEG / 10, NEG, ALU.is_lt, ALU.mult))
                yield
                need(done)
                done = mark(v.tensor_tensor(cand[:, ts, 0:NE].rearrange("p t (g j) -> p t g j", g=NG),
                                            sbias[:, ts].rearrange("p t (g j) -> p t g j", g=NG),
                                            gpen[:, ts].unsqueeze(3).broadcast_to((P, nt, NG, NE // NG)), ALU.add))
                yield
                need(done)
                for t in range(t0, t1):
                    done = mark(v.max(etop[:, t, :], cand[:, t, 0:NE]))
                    yield
                need(done)
                done = mark(v.tensor_copy(epick[:, ts, 0:KE], etop[:, ts, 0:KE]))
                yield
                need(done)
                for t in range(t0, t1):
                    done = mark(v.match_replace(eout[:, t, :], epick[:, t, :], cand[:, t, :], -NEG))
                    yield
                need(done)
                chosen = selb[:, NT - 1 + t0:NT - 1 + t1, :]
                v.tensor_scalar(chosen, eout[:, ts, 0:NE], -NEG / 10, None, ALU.is_ge).then_inc(sel_ready, 1)
                yield
                fl = lambda a: a.rearrange("p t e -> p (t e)")
                ve.wait_ge(sel_ready, n + 1)
                done = mark(v.tensor_tensor(wsel[:, ts], score[:, ts], chosen, ALU.mult))
                yield
                if n == 0:
                    ve.wait_ge(vals_init, 1)
                v.tensor_tensor_scan(vals[:, ts].rearrange("p t e v -> p (t e) v")[:, :, V_RANK], fl(keep[:, ts, :]), fl(chosen), 0.0, ALU.mult, ALU.add)
                yield
                need(done)
                done = mark(v.reduce_sum(wsum[:, ts], wsel[:, ts], axis=AX))
                yield
                need(done)
                done = mark(v.reciprocal(wsum[:, ts], wsum[:, ts]))
                yield
                need(done)
                done = mark(v.scalar_tensor_tensor(wsel[:, ts], wsel[:, ts], SCALE, wsum[:, ts].unsqueeze(2).broadcast_to((P, nt, NE)), ALU.mult, ALU.mult))
                yield
                filled(ve, "out", ("pos", n))
                v.scalar_tensor_tensor(slot[:, :, ts], chosen.rearrange("p t e -> p e t"), -float(CP),
                                       outp[:, t0 * NE:t1 * NE].rearrange("p (t e) -> p e t", t=nt), ALU.mult, ALU.add).then_inc(free["out"], 1)
                yield
                if n == 0:
                    yield from weight_parts(n, done)
                else:
                    last_weights[0] = done

            last_weights = [0]

            def weight_parts(n, done):
                ts = slice(*((0, ROUTED), (ROUTED, NT))[n])
                for i in range(3):
                    need(done)
                    part = vals[:, ts, :, V_WEIGHT + i]
                    ins = v.tensor_copy(part, wsel[:, ts])
                    if i == 2:
                        ins.then_inc(vals_ready, 1)
                        yield
                        return
                    done = mark(ins)
                    yield
                    need(done)
                    done = mark(v.tensor_tensor(wsel[:, ts], wsel[:, ts], part, ALU.subtract))
                    yield

            routed = routing(0)

            def route_some(n):
                for _ in range(n):
                    next(routed, None)

            def shared_hidden(n):
                ve.wait_ge(sh_act, n + 1)
                cols = slice(n * 512, (n + 1) * 512)
                v.tensor_tensor(hsh[0:FF, cols], ssh[0:FF, cols], unit_at(("sg", n))[0:FF, 512:1024], ALU.mult).then_inc(unit_free(("sg", n)), 1)

            def shared_add(n):
                area, of = (("unit", unit_at(("sd", 0))), ("proj", proj[:, :]))[n]
                filled(ve, area, ("sd", n))
                r = res[:, 4 * n:4 * n + 4, :].rearrange("p t e -> p (t e)")
                v.tensor_tensor(r, r, of, ALU.add).then_inc(free["proj"] if n else unit_free(("sd", 0)), 1)

            def one_hot(g, half):
                if g >= 2:
                    ve.wait_ge(info_full, g - 1)
                n = EPG // 2
                e0 = EPG * g + n * half
                v.tensor_tensor(hotbuf[:, g % 2, n * half:n * (half + 1)], slot[:, e0:e0 + n, :].unsqueeze(2).broadcast_to((P, n, CAP, NT)),
                                iotac[:, :, :].unsqueeze(1).broadcast_to((P, n, CAP, NT)), ALU.is_equal).then_inc(hot_ready, 1)

            def chunk_tokens(g):
                ve.wait_ge(chunk_free, g + 1)
                o = g % 2
                v.scalar_tensor_tensor(toki[:, CPG * g:CPG * (g + 1)], infoc[:, o, :, 0], 0.125, infoc[:, o, :, 1], ALU.mult, ALU.add).then_inc(token_ready, 1)

            def indices(g):
                ve.wait_ge(info_free, g + 1)
                o = g % 2
                cols = slice(PPG * g, PPG * (g + 1))
                if g >= 2:
                    ve.wait_ge(index_ready, g)
                done = mark(v.reduce_sum(rowf[:, o], info[:, o, :, V_TOKEN8:V_TILE8 + 1], axis=AX))
                v.reduce_sum(wslot[:, cols], info[:, o, :, V_WEIGHT:V_WEIGHT + 3], axis=AX)
                need(done)
                v.tensor_scalar(rowi[:, cols], rowf[:, o], 16.0 * T - 1.0, None, ALU.add).then_inc(index_ready, 1)

            pads()
            run = {"A1a": norm1_stats, "A1b": norm1, "A2a": rope_products, "A2b": rope_sum, "A2c": first_rest, "A2d": third_part,
                   "MT": shifts_turned, "MS": shift_parts, "D1a": add_transposed, "D1c": head_average, "D1e": attention_residual,
                   "D2": mixing, "D3a": moe_input, "Sb": shared_hidden, "Sd": shared_add, **{f"U{n}": maxima(n) for n in range(6)}}
            for stage, b in STEPS:
                if stage == "F":
                    fill(b)
                if stage == "G":
                    route_some(b)
                if stage == "D1a":
                    while at_tile[0] < TPB * (b + 1):
                        fill(1)
                if stage in run:
                    run[stage](b)
            for _ in routed:
                pass
            if ("Sd", 0) not in STEPS:
                shared_add(0)
            routed = routing(1)
            for _ in routed:
                pass
            emptied(ve, "out", ("pos", 1))
            ve.wait_ge(vals_init, 2)
            one_hot(0, 0)
            one_hot(0, 1)
            for _ in weight_parts(1, last_weights[0]):
                pass
            shared_hidden(1)
            chunk_tokens(0)
            one_hot(1, 0)
            one_hot(1, 1)
            indices(0)
            chunk_tokens(1)
            indices(1)
            one_hot(2, 0)
            one_hot(2, 1)
            for p in range(NP + 3):
                if p < NP and p % PPG < CPG:
                    g, j = divmod(p, PPG)
                    k = CPG * g + j
                    ve.wait_ge(xt_full, k + 1)
                    if g >= 2:
                        ve.wait_ge(gu_full, PPG * (g - 1))
                    v.tensor_copy(xgT[:, g % 2, :, j * P:(j + 1) * P], unit[:, 0, (k % 2) * 512:(k % 2) * 512 + E].rearrange("p (c s) -> p c s", c=2)).then_inc(xt_free, 1)
                if 0 <= p - 1 < NP:
                    q = p - 1
                    ve.wait_ge(act_ready, q + 1)
                    if q >= 2:
                        ve.wait_ge(ht_full, q - 1)
                    v.tensor_tensor(hid[:, q % 2, :], act[:, q % 2, :], unit[:, 1, (q % 2) * 512 + FF:(q % 2) * 512 + 2 * FF], ALU.mult).then_inc(hid_ready, 1)
                if 0 <= p - 2 < NP:
                    q = p - 2
                    ve.wait_ge(ht_full, q + 1)
                    if q >= 2:
                        ve.wait_ge(y_full, q - 1)
                    v.tensor_copy(hidT[0:FF, q % 2, :], outp[0:FF, 0:P]).then_inc(ht_free, 1)
                for half in range(2):
                    if p - half in HOTTED:
                        one_hot(HOTTED[p - half], half)
                if p in INDEXED:
                    chunk_tokens(INDEXED[p])
                    indices(INDEXED[p])
            shared_add(1)
            for i, (t, cols) in enumerate(PIECES):
                ve.wait_ge(z_in[i % NZ], 16 * (i // NZ + 1))
                if i >= NZ:
                    ve.wait_ge(out_done[i % NZ], 16 * (i // NZ))
                link(v.reduce_sum(fin[:, i % NZ, cols], zin[:, i % NZ, :, cols].rearrange("p k e -> p e k"), axis=AX))
                v.tensor_tensor(fin[:, i % NZ, cols], fin[:, i % NZ, cols], res[:, t, cols], ALU.add).then_inc(fin_ready, 1)


def rope_tables():
    inv = 1.0 / np.float32(10000.0) ** (np.arange(0, D, 2, dtype=np.float32) / np.float32(D))
    ang = np.outer(np.arange(S, dtype=np.float32), inv.astype(np.float32)).astype(np.float32)
    ang = np.concatenate([ang, ang], axis=-1).T
    sign = np.where(np.arange(D) % 2 == 0, -1.0, 1.0).astype(np.float32)[:, None]
    cos, sin = np.cos(ang).astype(np.float32), (np.sin(ang) * sign).astype(np.float32)
    return np.repeat(cos, HPC, axis=0), np.repeat(sin, HPC, axis=0)


def kernel(x, ctx_512, L0_attn_Wqkv, L0_attn_Wout, L0_xattn_Wq, L0_xattn_Wk, L0_xattn_gamma_raw, L0_ffn_gate_w, L0_ffn_bias,
           L0_ffn_w_gate, L0_ffn_w_up, L0_ffn_w_down, L0_ffn_ws_gate, L0_ffn_ws_up, L0_ffn_ws_down):
    import numpy as _np
    import concourse.bacc as _bacc
    from concourse import mybir as _mybir
    from concourse.bass_utils import run_bass_kernel_spmd as _run

    a = _np.asarray
    cos, sin = rope_tables()
    wqk = a(L0_attn_Wqkv)[:2 * E].reshape(2, E, E)
    gu = _np.stack([a(L0_ffn_w_gate), a(L0_ffn_w_up)], axis=2).reshape(NP, 2, 2, P, 2, FF)
    ins = {
        "x": a(x).reshape(T, E),
        "cosT": cos, "sinT": sin,
        "ctxT": a(ctx_512).reshape(T, DC).T,
        "wxT": _np.stack([a(L0_xattn_Wq).T, a(L0_xattn_Wk).T]),
        "wqkvT": _np.concatenate([w.reshape(HPC, 2, D, E).transpose(1, 2, 0, 3).reshape(E, E) for w in wqk] + [a(L0_attn_Wqkv)[2 * E:]]).T,
        "woT": a(L0_attn_Wout).T,
        "gamma": a(L0_xattn_gamma_raw).reshape(1, 1),
        "gate_w": a(L0_ffn_gate_w),
        "bias": a(L0_ffn_bias).reshape(1, NE),
        "w_gu": gu.transpose(0, 3, 1, 2, 4, 5).reshape(NP, P, 8 * FF),
        "w_dn": a(L0_ffn_w_down).reshape(NP, 2, FF, E).transpose(0, 2, 1, 3).reshape(NP, FF, 2 * E),
        "ws_gu": _np.concatenate([a(L0_ffn_ws_gate), a(L0_ffn_ws_up)], axis=1),
        "ws_dn": a(L0_ffn_ws_down),
    }
    nc = _bacc.Bacc("TRN2", target_bir_lowering=False, num_devices=1)
    arrays, args = {}, []
    for name, arr in ins.items():
        arr = _np.ascontiguousarray(arr)
        arrays[f"in_{name}"] = arr
        args.append(nc.dram_tensor(f"in_{name}", arr.shape, _mybir.dt.from_np(arr.dtype), kind="ExternalInput").ap())
    args.append(nc.dram_tensor("out_0", (T, E), _mybir.dt.float32, kind="ExternalOutput").ap())
    decoder_kernel(nc, *args)
    r = _run(nc, [arrays], core_ids=[0])
    return r.results[0]["out_0"].reshape(B, S, E)
```
